# Optimizing a Trainium2 kernel written in Bass

```python
import numpy as np
import jax
import jax.numpy as jnp

def _softmax(x, axis=-1):
    return jax.nn.softmax(x, axis=axis)

def _gelu(x):
    return jax.nn.gelu(x, approximate=True)

def _silu(x):
    return jax.nn.silu(x)

def _sigmoid(x):
    return jax.nn.sigmoid(x)

def _layernorm(x, axis=-1, eps=1e-05):
    m = jnp.mean(x, axis=axis, keepdims=True)
    v = jnp.var(x, axis=axis, keepdims=True)
    return (x - m) / jnp.sqrt(v + eps)

def _scatter_add(tgt, idx, src, axis=0):
    return tgt.at[idx].add(src)

def _segment_sum(src, seg, n):
    return jax.ops.segment_sum(src, seg, n)
kernel_name = 'mk_vit_tower_d2_tok_img512_r4_5cd7cf'

def setup_inputs(seed: int=0):
    np.random.seed(seed)
    _w = jnp.asarray

    def _rec_inputs():
        import jax
        import jax.numpy as jnp
        _rk = jax.random.key(seed)
        x = -0.000392918 + 0.999932 * jax.random.normal(jax.random.fold_in(_rk, 1), (16, 1, 128, 128), jnp.float32)
        return x
    x = _rec_inputs()

    def _L0_tok_setup():
        import math
        import jax, jax.numpy as jnp
        import numpy as np
        PW = PH = 16
        EMB = 128
        HID = 128
        B, H, W = (64, 128, 128)
        L = H // PW * (W // PH)
        SIGMA_ZERO = 0.1

        def _f_noise(x):
            return jnp.sign(x) * jnp.sqrt(jnp.abs(x))

        def _noisy_linear(x, w, b, sw, sb, eps_in, eps_out):
            ei = _f_noise(eps_in)
            eo = _f_noise(eps_out)
            w_n = w + sw * (eo[:, None] * ei[None, :])
            b_n = b + sb * eo
            return x @ w_n.T + b_n

        def _unfold_patches(x):
            b = x.shape[0]
            p = x.reshape(b, H // PW, PW, W // PH, PH)
            p = p.transpose(0, 1, 3, 2, 4)
            return p.reshape(b, L, PW * PH)

        def _pos_encoding(x):
            pos = jnp.arange(L, dtype=jnp.float32)[:, None]
            div = jnp.exp(jnp.arange(0, EMB, 2, dtype=jnp.float32) * (-math.log(10000.0) / EMB))
            ang = pos * div
            pe = jnp.stack([jnp.sin(ang), jnp.cos(ang)], axis=-1).reshape(L, EMB)
            return x + pe[None, :, :]
        key = jax.random.key(seed)
        ks = jax.random.split(key, 12)
        in_f = PW * PH
        sig = SIGMA_ZERO / math.sqrt(in_f)
        bnd1 = 1.0 / math.sqrt(in_f)
        bnd3 = 1.0 / math.sqrt(HID)
        u = lambda k, shape, bnd: jax.random.uniform(k, shape, jnp.float32, -bnd, bnd)
        return {'inputs': jax.random.normal(ks[0], (B, 1, H, W), jnp.float32), 'W1_w': u(ks[1], (HID, in_f), bnd1), 'W1_b': u(ks[2], (HID,), bnd1), 'W1_sw': jnp.full((HID, in_f), sig, jnp.float32), 'W1_sb': jnp.full((HID,), sig, jnp.float32), 'W2_w': u(ks[3], (HID, in_f), bnd1), 'W2_b': u(ks[4], (HID,), bnd1), 'W2_sw': jnp.full((HID, in_f), sig, jnp.float32), 'W2_sb': jnp.full((HID,), sig, jnp.float32), 'W3_w': u(ks[5], (EMB, HID), bnd3), 'W3_b': u(ks[6], (EMB,), bnd3), 'eps_in1': jax.random.normal(ks[7], (in_f,), jnp.float32), 'eps_out1': jax.random.normal(ks[8], (HID,), jnp.float32), 'eps_in2': jax.random.normal(ks[9], (in_f,), jnp.float32), 'eps_out2': jax.random.normal(ks[10], (HID,), jnp.float32)}
    _L0_tok_all = _L0_tok_setup()
    _L0_tok_in = {k: v for k, v in _L0_tok_all.items() if k in ('W1_w', 'W1_b', 'W1_sw', 'W1_sb', 'W2_w', 'W2_b', 'W2_sw', 'W2_sb', 'W3_w', 'W3_b', 'eps_in1', 'eps_out1', 'eps_in2', 'eps_out2')}
    del _L0_tok_all

    def _L0_attn_setup():
        import jax, jax.numpy as jnp
        import numpy as np
        B, S, X = (2, 512, 128)
        HEADS, HEAD_SIZE = (8, 64)
        FREQS, MAX_PERIOD = (64, 2500)

        def sinusoid_embedding(sequence_length, frequencies, max_period):
            index = np.arange(frequencies)
            frequency = np.pi * (2 / max_period) ** (index // 2 / (frequencies // 2 - 1))
            phase = np.pi / 2 * (index % 2)
            time = np.arange(sequence_length)
            return np.sin(frequency * time[:, np.newaxis] + phase)

        def relative_causal_reshape(scores):
            s = scores.shape[-1]
            nd = scores.ndim
            padded = jnp.pad(scores[..., ::-1], [(0, 0)] * (nd - 1) + [(0, s)])
            tmp = padded.reshape(padded.shape[:-2] + (2 * s * s,))
            tmp = tmp[..., :-s]
            tmp = tmp.reshape(tmp.shape[:-1] + (s, 2 * s - 1))
            return tmp[..., s - 1:]
        key = jax.random.key(seed)
        k1, k2, k3, k4 = jax.random.split(key, 4)
        qkv_scale = np.sqrt(3) * X ** (-0.5)
        pos_scale = np.sqrt(3) * FREQS ** (-0.5)
        glorot = np.sqrt(6.0 / (HEADS * HEAD_SIZE + X))
        return {'x': jax.random.normal(k1, (B, S, X), dtype=jnp.float32), 'qkv': jax.random.uniform(k2, (X, 3, HEADS, HEAD_SIZE), jnp.float32, -qkv_scale, qkv_scale), 'q_bias': jnp.zeros((HEADS, HEAD_SIZE), jnp.float32), 'positional': jax.random.uniform(k3, (FREQS, HEADS, HEAD_SIZE), jnp.float32, -pos_scale, pos_scale), 'out_w': jax.random.uniform(k4, (HEADS * HEAD_SIZE, X), jnp.float32, -glorot, glorot), 'out_b': jnp.zeros((X,), jnp.float32)}
    _L0_attn_all = _L0_attn_setup()
    _L0_attn_in = {k: v for k, v in _L0_attn_all.items() if k in ('qkv', 'q_bias', 'positional', 'out_w', 'out_b')}
    del _L0_attn_all

    def _L0_ffn_setup():
        import jax, jax.numpy as jnp
        import numpy as np
        H = 128
        FF = 4 * H
        E = 8
        K = 2
        B, S = (4, 1024)
        key = jax.random.key(seed)
        ks = jax.random.split(key, 4)
        s = 0.02
        return {'x': jax.random.normal(ks[0], (B, S, H), dtype=jnp.float32), 'Wg': jax.random.normal(ks[1], (H, E), dtype=jnp.float32) * s, 'bg': jnp.zeros((E,), dtype=jnp.float32), 'W1': jax.random.normal(ks[2], (E, H, FF), dtype=jnp.float32) * s, 'b1': jnp.zeros((E, FF), dtype=jnp.float32), 'W2': jax.random.normal(ks[3], (E, FF, H), dtype=jnp.float32) * s, 'b2': jnp.zeros((E, H), dtype=jnp.float32)}
    _L0_ffn_all = _L0_ffn_setup()
    _L0_ffn_in = {k: v for k, v in _L0_ffn_all.items() if k in ('Wg', 'bg', 'W1', 'b1', 'W2', 'b2')}
    del _L0_ffn_all

    def _L1_attn_setup():
        import jax, jax.numpy as jnp
        import numpy as np
        key = jax.random.key(seed)
        X = jax.random.normal(key, (4, 1024, 128), dtype=jnp.float32)
        return {'X': X}
    _L1_attn_all = _L1_attn_setup()
    _L1_attn_in = {k: v for k, v in _L1_attn_all.items() if k in ()}
    del _L1_attn_all

    def _L1_ffn_setup():
        import jax, jax.numpy as jnp
        import numpy as np
        B, L, H, E, F, C = (8, 2048, 128, 8, 256, 2)
        key = jax.random.key(seed)
        ks = jax.random.split(key, 4)
        x = jax.random.normal(ks[0], (B, L, H), jnp.float32)
        Wg = jax.random.normal(ks[1], (H, E), jnp.float32) * H ** (-0.5)
        W1 = jax.random.normal(ks[2], (E, H, F), jnp.float32) * H ** (-0.5)
        b1 = jnp.zeros((E, F), jnp.float32)
        W2 = jax.random.normal(ks[3], (E, F, H), jnp.float32) * F ** (-0.5)
        b2 = jnp.zeros((E, H), jnp.float32)
        return {'x': x, 'Wg': Wg, 'W1': W1, 'b1': b1, 'W2': W2, 'b2': b2}
    _L1_ffn_all = _L1_ffn_setup()
    _L1_ffn_in = {k: v for k, v in _L1_ffn_all.items() if k in ('Wg', 'W1', 'b1', 'W2', 'b2')}
    del _L1_ffn_all
    return {'x': x, 'L0_tok_W1_w': _L0_tok_in['W1_w'], 'L0_tok_W1_b': _L0_tok_in['W1_b'], 'L0_tok_W1_sw': _L0_tok_in['W1_sw'], 'L0_tok_W1_sb': _L0_tok_in['W1_sb'], 'L0_tok_W2_w': _L0_tok_in['W2_w'], 'L0_tok_W2_b': _L0_tok_in['W2_b'], 'L0_tok_W2_sw': _L0_tok_in['W2_sw'], 'L0_tok_W2_sb': _L0_tok_in['W2_sb'], 'L0_tok_W3_w': _L0_tok_in['W3_w'], 'L0_tok_W3_b': _L0_tok_in['W3_b'], 'L0_tok_eps_in1': _L0_tok_in['eps_in1'], 'L0_tok_eps_out1': _L0_tok_in['eps_out1'], 'L0_tok_eps_in2': _L0_tok_in['eps_in2'], 'L0_tok_eps_out2': _L0_tok_in['eps_out2'], 'L0_attn_qkv': _L0_attn_in['qkv'], 'L0_attn_q_bias': _L0_attn_in['q_bias'], 'L0_attn_positional': _L0_attn_in['positional'], 'L0_attn_out_w': _L0_attn_in['out_w'], 'L0_attn_out_b': _L0_attn_in['out_b'], 'L0_ffn_Wg': _L0_ffn_in['Wg'], 'L0_ffn_bg': _L0_ffn_in['bg'], 'L0_ffn_W1': _L0_ffn_in['W1'], 'L0_ffn_b1': _L0_ffn_in['b1'], 'L0_ffn_W2': _L0_ffn_in['W2'], 'L0_ffn_b2': _L0_ffn_in['b2'], 'L1_ffn_Wg': _L1_ffn_in['Wg'], 'L1_ffn_W1': _L1_ffn_in['W1'], 'L1_ffn_b1': _L1_ffn_in['b1'], 'L1_ffn_W2': _L1_ffn_in['W2'], 'L1_ffn_b2': _L1_ffn_in['b2']}

def reference(x, L0_tok_W1_w, L0_tok_W1_b, L0_tok_W1_sw, L0_tok_W1_sb, L0_tok_W2_w, L0_tok_W2_b, L0_tok_W2_sw, L0_tok_W2_sb, L0_tok_W3_w, L0_tok_W3_b, L0_tok_eps_in1, L0_tok_eps_out1, L0_tok_eps_in2, L0_tok_eps_out2, L0_attn_qkv, L0_attn_q_bias, L0_attn_positional, L0_attn_out_w, L0_attn_out_b, L0_ffn_Wg, L0_ffn_bg, L0_ffn_W1, L0_ffn_b1, L0_ffn_W2, L0_ffn_b2, L1_ffn_Wg, L1_ffn_W1, L1_ffn_b1, L1_ffn_W2, L1_ffn_b2):
    import jax
    import jax.numpy as jnp

    def _L0_tok_ref(inputs, W1_w, W1_b, W1_sw, W1_sb, W2_w, W2_b, W2_sw, W2_sb, W3_w, W3_b, eps_in1, eps_out1, eps_in2, eps_out2):
        import math
        import jax, jax.numpy as jnp
        import numpy as np
        PW = PH = 16
        EMB = 128
        HID = 128
        B, H, W = (64, 128, 128)
        L = H // PW * (W // PH)
        SIGMA_ZERO = 0.1

        def _f_noise(x):
            return jnp.sign(x) * jnp.sqrt(jnp.abs(x))

        def _noisy_linear(x, w, b, sw, sb, eps_in, eps_out):
            ei = _f_noise(eps_in)
            eo = _f_noise(eps_out)
            w_n = w + sw * (eo[:, None] * ei[None, :])
            b_n = b + sb * eo
            return x @ w_n.T + b_n

        def _unfold_patches(x):
            b = x.shape[0]
            p = x.reshape(b, H // PW, PW, W // PH, PH)
            p = p.transpose(0, 1, 3, 2, 4)
            return p.reshape(b, L, PW * PH)

        def _pos_encoding(x):
            pos = jnp.arange(L, dtype=jnp.float32)[:, None]
            div = jnp.exp(jnp.arange(0, EMB, 2, dtype=jnp.float32) * (-math.log(10000.0) / EMB))
            ang = pos * div
            pe = jnp.stack([jnp.sin(ang), jnp.cos(ang)], axis=-1).reshape(L, EMB)
            return x + pe[None, :, :]
        x = _unfold_patches(inputs)
        g = _noisy_linear(x, W1_w, W1_b, W1_sw, W1_sb, eps_in1, eps_out1)
        x_gate = g * jnp.tanh(jax.nn.softplus(g))
        x_inner = _noisy_linear(x, W2_w, W2_b, W2_sw, W2_sb, eps_in2, eps_out2)
        x = x_gate * x_inner
        x = x @ W3_w.T + W3_b
        return _pos_encoding(x)

    def _L0_attn_ref(x, qkv, q_bias, positional, out_w, out_b):
        import jax, jax.numpy as jnp
        import numpy as np
        B, S, X = (2, 512, 128)
        HEADS, HEAD_SIZE = (8, 64)
        FREQS, MAX_PERIOD = (64, 2500)

        def sinusoid_embedding(sequence_length, frequencies, max_period):
            index = np.arange(frequencies)
            frequency = np.pi * (2 / max_period) ** (index // 2 / (frequencies // 2 - 1))
            phase = np.pi / 2 * (index % 2)
            time = np.arange(sequence_length)
            return np.sin(frequency * time[:, np.newaxis] + phase)

        def relative_causal_reshape(scores):
            s = scores.shape[-1]
            nd = scores.ndim
            padded = jnp.pad(scores[..., ::-1], [(0, 0)] * (nd - 1) + [(0, s)])
            tmp = padded.reshape(padded.shape[:-2] + (2 * s * s,))
            tmp = tmp[..., :-s]
            tmp = tmp.reshape(tmp.shape[:-1] + (s, 2 * s - 1))
            return tmp[..., s - 1:]
        b, s, _ = x.shape
        scale = HEAD_SIZE ** (-0.5)
        proj = jnp.einsum('bsx,xAnh->Abnsh', x, qkv)
        q, k, v = (proj[0], proj[1], proj[2])
        q = q + q_bias[:, None, :]
        a = jnp.einsum('bnqh,bnkh->bnqk', q, k) * scale
        sins = jnp.asarray(sinusoid_embedding(s, FREQS, MAX_PERIOD), dtype=x.dtype)
        emb = jnp.einsum('sf,fnh->nsh', sins, positional)
        pos_scores = jnp.einsum('bnqh,nvh->bnqv', q, emb) * scale
        a = a + relative_causal_reshape(pos_scores)
        mask = jnp.triu(jnp.full((s, s), -1000.0, dtype=a.dtype), k=1)
        a = a + mask
        a = jax.nn.softmax(a, axis=-1)
        o = jnp.einsum('bnqk,bnkh->bqnh', a, v)
        o = o.reshape(b, s, HEADS * HEAD_SIZE)
        return o @ out_w + out_b

    def _L0_ffn_ref(x, Wg, bg, W1, b1, W2, b2):
        import jax, jax.numpy as jnp
        import numpy as np
        H = 128
        FF = 4 * H
        E = 8
        K = 2
        B, S = (4, 1024)
        logits = x @ Wg + bg
        w, idx = jax.lax.top_k(logits, K)
        w = jax.nn.softmax(w, axis=-1)
        h = jax.nn.silu(jnp.einsum('bsh,ehf->ebsf', x, W1) + b1[:, None, None, :])
        y = jnp.einsum('ebsf,efh->ebsh', h, W2) + b2[:, None, None, :]
        comb = jnp.einsum('bske,bsk->ebs', jax.nn.one_hot(idx, E, dtype=x.dtype), w)
        return jnp.einsum('ebsh,ebs->bsh', y, comb)

    def _L1_attn_ref(X):
        import jax, jax.numpy as jnp
        import numpy as np
        raw_weights = jnp.einsum('bnd,bmd->bnm', X, X)
        weights = jax.nn.softmax(raw_weights, axis=-1)
        y = jnp.einsum('bnm,bmd->bnd', weights, X).astype(jnp.float32)
        return y

    def _L1_ffn_ref(x, Wg, W1, b1, W2, b2):
        import jax, jax.numpy as jnp
        import numpy as np
        B, L, H, E, F, C = (8, 2048, 128, 8, 256, 2)
        b, l, h = x.shape
        e = Wg.shape[1]
        k = min(max(int(l * C / e), 1), l)
        S = jax.nn.softmax(x @ Wg, axis=-1)
        St = jnp.swapaxes(S, 1, 2)
        G, I = jax.lax.top_k(St, k)
        ex = jnp.take_along_axis(x[:, None], I[..., None], axis=2)
        hmid = jax.nn.gelu(jnp.einsum('bekh,ehf->bekf', ex, W1) + b1[None, :, None, :], approximate=False)
        out = jnp.einsum('bekf,efh->bekh', hmid, W2) + b2[None, :, None, :]
        vals = G[..., None] * out
        new_x = jnp.zeros_like(x).at[jnp.arange(b)[:, None, None], I].add(vals)
        return new_x
    h = _L0_tok_ref(x, L0_tok_W1_w, L0_tok_W1_b, L0_tok_W1_sw, L0_tok_W1_sb, L0_tok_W2_w, L0_tok_W2_b, L0_tok_W2_sw, L0_tok_W2_sb, L0_tok_W3_w, L0_tok_W3_b, L0_tok_eps_in1, L0_tok_eps_out1, L0_tok_eps_in2, L0_tok_eps_out2)
    h = h + _L0_attn_ref(_layernorm(h, axis=-1), L0_attn_qkv, L0_attn_q_bias, L0_attn_positional, L0_attn_out_w, L0_attn_out_b)
    h = h + _L0_ffn_ref(_layernorm(h, axis=-1), L0_ffn_Wg, L0_ffn_bg, L0_ffn_W1, L0_ffn_b1, L0_ffn_W2, L0_ffn_b2)
    h = h + _L1_attn_ref(_layernorm(h, axis=-1))
    h = h + _L1_ffn_ref(_layernorm(h, axis=-1), L1_ffn_Wg, L1_ffn_W1, L1_ffn_b1, L1_ffn_W2, L1_ffn_b2)
    return h

_drawn_inputs = setup_inputs


def setup_inputs(seed=0):
    import zlib

    import numpy as np

    out = dict(_drawn_inputs(seed))
    spreads = {'L0_tok_W1_sw': (0.0062500000931322575, 0.6),
     'L0_tok_W1_sb': (0.0062500000931322575, 0.6),
     'L0_tok_W2_sw': (0.0062500000931322575, 0.6),
     'L0_tok_W2_sb': (0.0062500000931322575, 0.6),
     'L0_attn_q_bias': (0.0, 0.282),
     'L0_attn_out_b': (0.0, 0.1),
     'L0_ffn_bg': (0.0, 0.1),
     'L0_ffn_b1': (0.0, 0.476),
     'L0_ffn_b2': (0.0, 0.1),
     'L1_ffn_b1': (0.0, 0.656),
     'L1_ffn_b2': (0.0, 0.427)}
    factors = {'L0_tok_W1_b': 3.053, 'L0_tok_W2_b': 3.452}
    for name, (base, spread) in spreads.items():
        noise = np.random.default_rng([zlib.crc32(name.encode()), seed]).standard_normal(out[name].shape)
        drawn = base * np.exp(spread * noise) if base else spread * noise
        out[name] = jnp.asarray(drawn.astype(out[name].dtype))
    for name, factor in factors.items():
        out[name] = (out[name] * factor).astype(out[name].dtype)
    return out
```

```python
import numpy as np

import concourse.bass as bass
from concourse import mybir
from contextlib import ExitStack

F32 = mybir.dt.float32
F32R = mybir.dt.float32r
ALU = mybir.AluOpType
ACT = mybir.ActivationFunctionType
AX = mybir.AxisListType

P = 128
B, L, X = 16, 64, 128
TOK = B * L
NT = TOK // P
HALF = TOK // 2
TH = NT // 2
KT = 2
HEADS, HD = 8, 64
NP = HEADS // 2
FREQS = 64
E0, F0 = 8, 512
FT = F0 // P
E1, F1 = 8, 256
CAP = L * 2 // E1
SLOT = 2 * CAP
EPS = 1e-5
MASKED = -1000.0 * HD ** 0.5
NREL = 4
NS = NREL + 2

EO, EI, EOC, BIAS = 0, 256, 260, 262
W3, B3, OB, QB, WO, BG, WG0, WG1 = 0, 128, 256, 384, 388, 900, 908, 916
SMALL = 924
IDENT, PE_, SINS, REV, SLOTS, CONSTS = 0, 128, 256, 320, 328, 360
RAW0 = F0 + FT * X
NB0 = FT + 1
RAW1 = F1 + 2 * X + 2 + 1


def qkv_bank(n):
    return (0, 1, 2, 3, 5, 6)[n % 6] if n < 12 else (4, 5, 6, 7, 2, 3)[n % 6]


def tower(nc, x_cols, tok_w, tok_eps, qkv_w, pos_w, small, consts, moe0, moe0_b, moe1, rel_dram, comb_dram, out):
    names = ["dve_step", "in_tok_w0", "in_tok_w1", "in_eps", "in_x0", "in_x1", "in_small", "in_consts", "in_qkv", "in_pos", "in_moe1",
             "pads_made", "pads_out", "block_zeros", "half_made", "zeros_made",
             "eps_abs", "eps_sqrt", "eps_sign", "eps_root", "noise_outer", "noisy_w", "noisy_b", "pe_bias", "out_bias",
             "gate_full", "inner_full", "gate", "gate_cap", "gate_exp", "gate_log", "gate_sum", "gate_sigmoid",
             "gated_inner", "mixed", "embed_full", "h_ready",
             "ln_stats", "ln_moments", "ln_eps", "ln_rstd", "ln_out",
             "turned", "xt_hi", "xt_lo", "qkv_w_hi", "qkv_w_lo",
             "qkv_full", "q_even", "q_odd", "k_ready", "v_ready", "emb_full", "emb_ready",
             "scores_full", "pos_ready", "qk_ready", "rel_added", "row_max", "shifted", "probs", "prob_sum",
             "prob_rsum", "normed", "probs_turned", "probs_t", "heads_full", "heads_t", "mixed_full", "h1_ready",
             "gate_w_hi", "gate_w_lo", "router_full", "router", "combT_full", "combT", "comb_out",
             "w_hi", "w_lo", "p1_full", "silu", "h_hi", "h_lo", "y_full", "y_scaled", "acc",
             "acc_turned", "h2_ready",
             "self_full", "self_max", "self_shift", "self_probs", "self_sum", "self_rsum", "self_turned",
             "self_pt", "self_y", "h3_ready",
             "x4t", "choice_full", "choice", "choice_turned", "choice_t", "top", "slots_turned", "onehot", "gated",
             "gather_full", "gathered", "e1_full", "gelu", "e1_y_full", "e1_y", "c_turned", "c_ready",
             "y_turned", "y_ready", "h4_full", "h4_ready", "out_done"]
    with ExitStack() as ctx:
        S = {n: ctx.enter_context(nc.semaphore(n)) for n in names}
        for n in range(NREL):
            for kind in ("rel_out", "rel_in"):
                S[kind, n] = ctx.enter_context(nc.semaphore(f"{kind}{n}"))
        for n in range(2):
            for kind in ("in_raw", "in_bias", "in_comb"):
                S[kind, n] = ctx.enter_context(nc.semaphore(f"{kind}{n}"))

        def sb(where, name, *shape, dt=F32):
            return where.enter_context(nc.sbuf_tensor(name, [P, *shape], dt))

        banks = ctx.enter_context(nc.psum_tensor("banks", [P, 8, 512], F32))
        bank = [banks[:, n] for n in range(8)]

        cst = sb(ctx, "cst", CONSTS)
        sml = sb(ctx, "sml", SMALL)
        eps = sb(ctx, "eps", BIAS + 4)
        eps_f = sb(ctx, "eps_f", 3, EOC + 2)
        pe_b3 = sb(ctx, "pe_b3", X)
        h_a = sb(ctx, "h_a", NT, X)
        h_b = sb(ctx, "h_b", NT, X)
        xn = sb(ctx, "xn", NT, X)
        xt_hi = sb(ctx, "xt_hi", TOK, dt=F32R)
        xt_lo = sb(ctx, "xt_lo", TOK, dt=F32R)
        stats = sb(ctx, "stats", 4, NT, 6)
        mv = sb(ctx, "mv", 4, NT, 2)
        var_eps = sb(ctx, "var_eps", 4, NT)
        rstd = sb(ctx, "rstd", 4, NT)
        mhalf = sb(ctx, "mhalf", NT)
        raw = [sb(ctx, f"raw{j}", RAW0) for j in range(2)]
        bias0 = [sb(ctx, f"bias0_{j}", NB0) for j in range(2)]
        w_hi = [sb(ctx, f"w_hi{j}", 2 * F0, dt=F32R) for j in range(2)]
        w_lo = [sb(ctx, f"w_lo{j}", 2 * F0, dt=F32R) for j in range(2)]
        wg_hi = sb(ctx, "wg_hi", E0, dt=F32R)
        wg_lo = sb(ctx, "wg_lo", E0, dt=F32R)
        m1 = sb(ctx, "m1", E1, RAW1)
        ident = cst[:, IDENT:IDENT + P]

        with ExitStack() as tok:
            x_in = sb(tok, "x_in", 2, KT, HALF)
            tw = sb(tok, "tw", 4, KT, P)
            outer = sb(tok, "outer", 2, KT, P)
            wn = sb(tok, "wn", 2, KT, P)
            bn = sb(tok, "bn", 2)
            gate = sb(tok, "gate", 2, HALF)
            u = sb(tok, "u", 2, HALF)
            softplus = sb(tok, "softplus", 2, HALF)
            inner = sb(tok, "inner", 2, HALF)
            mixed = sb(tok, "mixed", 2, HALF)

        with ExitStack() as att:
            k_emb = sb(att, "k_emb", NP, B + 1, L)
            v_sb = sb(att, "v_sb", NT, HEADS * HD)
            score = sb(att, "score", NS, NP, 2, L)
            probs_t = sb(att, "probs_t", 2, NP, P)
            heads_t = sb(att, "heads_t", 2, NP, P)
            q_block = sb(att, "q_block", NP, B, 2, L)
            qw_hi = sb(att, "qw_hi", 3 * HEADS * HD, dt=F32R)
            qw_lo = sb(att, "qw_lo", 3 * HEADS * HD, dt=F32R)
            qw = sb(att, "qw", 3 * HEADS * HD)
            pw = sb(att, "pw", HEADS * HD)
            pos_sb = sb(att, "pos_sb", NREL, 2, L, NP)
            rel_sb = sb(att, "rel_sb", NREL, 2, L, NP)
            pads = sb(att, "pads", 2, L * NP)
            srow = sb(att, "srow", 3, NT, 8)

        with ExitStack() as mix:
            hid_hi = sb(mix, "hid_hi", 2, FT, HALF, dt=F32R)
            hid_lo = sb(mix, "hid_lo", 2, FT, HALF, dt=F32R)
            hid = sb(mix, "hid", FT, HALF)
            comb_bc = [sb(mix, f"comb_bc{j}", TOK) for j in range(2)]
            scaled = sb(mix, "scaled", 2, HALF)
            acc = sb(mix, "acc", 2, HALF)
            rt = sb(mix, "rt", 12, NT * E0)
            comb_t = sb(mix, "comb_t", P)

        with ExitStack() as sec:
            s_shift = sb(sec, "s_shift", NT, L)
            s_prob = sb(sec, "s_prob", NT, P)
            s_pt = sb(sec, "s_pt", NT, P)
            s_row = sb(sec, "s_row", 3, NT)
            x4t = sb(sec, "x4t", NT, P)
            choice = sb(sec, "choice", 4, NT, E1)
            crow = sb(sec, "crow", 3, NT)
            st = sb(sec, "st", 6, P)
            top8 = sb(sec, "top8", 4, 8)
            onehot = sb(sec, "onehot", NT, E1, SLOT)
            gated = sb(sec, "gated", NT, E1, SLOT)
            x_g = sb(sec, "x_g", E1, NT, SLOT)
            hmid = sb(sec, "hmid", 2, 2, NT * SLOT)
            y_g = sb(sec, "y_g", NT, E1, SLOT)
            y_nat = sb(sec, "y_nat", NT, 2, X)
            c_mat = sb(sec, "c_mat", NT, 2, P)

        block = ctx.enter_context(nc.Block())

        def read_rel(sp, t):
            n, k = t % NREL, t // NREL
            sp.wait_ge(S["rel_out", n], 16 * (k + 1))
            if k:
                sp.wait_ge(S["rel_added"], t - NREL + 1)
            for n2 in range(2):
                sp.dma_start(rel_sb[n2 * L:(n2 + 1) * L, n].rearrange("p b c n -> p b (c n)"),
                             bass.AP(tensor=rel_dram.tensor, offset=n * P * 1024 + n2 * L * 1024 + (L - 1) * NP,
                                     ap=[[1024 - NP, L], [512, 2], [1, 256]])).then_inc(S["rel_in", n], 16)

        @block.sync
        def _(sp):
            sp.dma_start(eps[:], tok_eps).then_inc(S["in_eps"], 16)
            sp.dma_start(tw[:, 0:2], tok_w[:, 0:2]).then_inc(S["in_tok_w0"], 16)
            sp.dma_start(x_in[:, 0], x_cols[:, 0]).then_inc(S["in_x0"], 16)
            sp.dma_start(tw[:, 2:4], tok_w[:, 2:4]).then_inc(S["in_tok_w1"], 16)
            sp.dma_start(x_in[:, 1], x_cols[:, 1]).then_inc(S["in_x1"], 16)
            sp.dma_start(cst[:], consts).then_inc(S["in_consts"], 16)
            sp.dma_start(pw[0:FREQS], pos_w).then_inc(S["in_pos"], 16)
            sp.dma_start(qw[:], qkv_w).then_inc(S["in_qkv"], 16)
            sp.dma_start(sml[:], small).then_inc(S["in_small"], 16)
            for e in range(2):
                sp.dma_start(raw[e][:], moe0[e]).then_inc(S["in_raw", e], 16)
            sp.wait_ge(S["pads_made"], 1)
            for n in range(NREL):
                sp.dma_start(bass.AP(tensor=rel_dram.tensor, offset=n * P * 1024 + 256, ap=[[1024, P], [512, 2], [1, 256]]),
                             pads[:]).then_inc(S["pads_out"], 16)
            sp.dma_start(m1[:], moe1).then_inc(S["in_moe1"], 16)
            sp.wait_ge(S["pads_out"], 16 * NREL)

            for t in range(NT):
                n, k = t % NREL, t // NREL
                base = n * P * 1024
                sp.wait_ge(S["pos_ready"], t + 1)
                if k:
                    sp.wait_ge(S["rel_in", n], 32 * k)
                sp.dma_start(bass.AP(tensor=rel_dram.tensor, offset=base, ap=[[1024, P], [512, 2], [1, 256]]),
                             pos_sb[:, n].rearrange("p b c n -> p b (c n)")).then_inc(S["rel_out", n], 16)
                if t >= 1:
                    read_rel(sp, t - 1)
            read_rel(sp, NT - 1)

            sp.wait_ge(S["combT"], 1)
            sp.dma_start(comb_dram, comb_t[0:NT * E0]).then_inc(S["comb_out"], 16)
            sp.wait_ge(S["comb_out"], 16)
            for e in range(E0):
                if e >= 2:
                    sp.wait_ge(S["w_lo"], e - 1)
                    sp.dma_start(raw[e % 2][:], moe0[e]).then_inc(S["in_raw", e % 2], 16)
                    sp.wait_ge(S["y_scaled"], 2 + 2 * (e - 1))
                sp.dma_start(bias0[e % 2][:], moe0_b[e]).then_inc(S["in_bias", e % 2], 16)
                sp.dma_start(comb_bc[e % 2][:], bass.AP(tensor=comb_dram.tensor, offset=e * TOK, ap=[[0, P], [1, TOK]]))\
                    .then_inc(S["in_comb", e % 2], 16)

            out_v = out.rearrange("(t b) l x -> (b l) t x", b=2)
            for c in range(2):
                sp.wait_ge(S["h4_ready"], TH * (c + 1))
                sp.dma_start(out_v[:, c * TH:(c + 1) * TH], h_a[:, c * TH:(c + 1) * TH]).then_inc(S["out_done"], 16)
            sp.wait_ge(S["out_done"], 32)

        @block.gpsimd
        def _(pool):
            pool.memset(mhalf[:], -0.5).then_inc(S["half_made"], 1)

            def rstd_of(k, c):
                cols = slice(c * TH, (c + 1) * TH)
                n = 2 * k + c
                pool.wait_ge(S["ln_moments"], TH * (n + 1))
                pool.tensor_scalar(var_eps[:, k, cols], mv[:, k, cols, 1], EPS, None, ALU.add).then_inc(S["ln_eps"], 1)
                pool.wait_ge(S["ln_eps"], n + 1)
                pool.tensor_tensor(rstd[:, k, cols], var_eps[:, k, cols], mhalf[:, cols], ALU.pow).then_inc(S["ln_rstd"], 1)

            pool.wait_ge(S["half_made"], 1)
            for n2 in range(2):
                rows = slice(n2 * L, (n2 + 1) * L)
                if n2:
                    pool.wait_ge(S["block_zeros"], 1)
                pool.memset(q_block[rows, :, :, 1 - n2, :].rearrange("p n b i -> p (n b) i"), 0.0).then_inc(S["block_zeros"], 1)
            pool.wait_ge(S["block_zeros"], 2)
            pool.wait_ge(S["in_consts"], 16)
            pool.wait_ge(S["in_small"], 16)
            pool.tensor_tensor(pe_b3[:], cst[:, PE_:PE_ + X], sml[:, B3:B3 + X], ALU.add).then_inc(S["pe_bias"], 1)
            pool.wait_ge(S["qkv_w_hi"], 1)
            pool.tensor_tensor(qw_lo[:], qw[:], qw_hi[:].bitcast(F32), ALU.subtract).then_inc(S["qkv_w_lo"], 1)
            for c in range(2):
                rstd_of(0, c)
            for t in range(NT):
                pool.tensor_tensor(h_b[:, t], h_a[:, t], sml[:, OB:OB + X], ALU.add).then_inc(S["out_bias"], 1)

            for t in range(NT):
                a = score[:, t % NS].rearrange("p n b j -> p (n b) j")
                pool.wait_ge(S["prob_rsum"], t + 1)
                pool.tensor_tensor(a, a, srow[:, 2, t].unsqueeze(2).broadcast_to([P, 8, L]), ALU.mult)\
                    .then_inc(S["normed"], 1)
            pool.wait_ge(S["w_hi"], 1)
            pool.tensor_tensor(w_lo[0][:], raw[0][:], w_hi[0][:].bitcast(F32), ALU.subtract).then_inc(S["w_lo"], 1)
            for c in range(2):
                rstd_of(1, c)
            pool.memset(acc[:], 0.0).then_inc(S["acc"], 2)

            def low_weights(e, j):
                pool.wait_ge(S["w_hi"], e + 1)
                pool.tensor_tensor(w_lo[j][:], raw[j][:], w_hi[j][:].bitcast(F32), ALU.subtract)\
                    .then_inc(S["w_lo"], 1)

            def accumulate(e, c):
                pool.wait_ge(S["y_scaled"], 2 + 2 * e + c + 1)
                pool.wait_ge(S["acc"], 2 + 2 * e + c)
                pool.tensor_tensor(acc[:, c], acc[:, c], scaled[:, c], ALU.add).then_inc(S["acc"], 1)

            with pool.Fori(0, 3) as i:
                for j in range(2):
                    low_weights(2 * i + (j + 1), 1 - j)
                    for c in range(2):
                        accumulate(2 * i + j, c)
            low_weights(7, 1)
            for e in (6, 7):
                for c in range(2):
                    accumulate(e, c)
            pool.memset(s_prob[:], 0.0).then_inc(S["zeros_made"], 1)
            for k in (2, 3):
                for c in range(2):
                    rstd_of(k, c)

        @block.scalar
        def _(act):
            act.wait_ge(S["eps_abs"], 1)
            act.activation(eps_f[:, 2], eps_f[:, 0], ACT.Sqrt).then_inc(S["eps_sqrt"], 1)
            act.wait_ge(S["in_eps"], 16)
            act.activation(eps_f[:, 1], eps[:, 0:BIAS], ACT.Sign).then_inc(S["eps_sign"], 1)

            for c in range(2):
                act.wait_ge(S["gate_cap"], c + 1)
                act.activation(u[:, c], u[:, c], ACT.Exp).then_inc(S["gate_exp"], 1)
            for c in range(2):
                act.wait_ge(S["gate_exp"], c + 1)
                act.activation(softplus[:, c], u[:, c], ACT.Ln, bias=1.0, scale=0.5).then_inc(S["gate_log"], 1)
            for c in range(2):
                act.wait_ge(S["gate_sum"], c + 1)
                act.activation(u[:, c], softplus[:, c], ACT.Sigmoid).then_inc(S["gate_sigmoid"], 1)

            def turned_hi(n, b, cols):
                act.wait_ge(S["turned"], n + 1)
                act.activation(xt_hi[:, cols], bank[b][:], ACT.Copy).then_inc(S["xt_hi"], 1)

            def copy_qkv(c):
                for np_ in range(NP):
                    n = 12 * c + np_
                    act.wait_ge(S["qkv_full"], n + 1)
                    act.activation(q_block[0:L, np_, c * 8:(c + 1) * 8, 0, :],
                                   bank[qkv_bank(n)][0:L].rearrange("p (b i) -> p b i", b=8), ACT.Identity,
                                   bias=sml[0:L, QB + np_:QB + np_ + 1]).then_inc(S["q_even"], 1)
                for np_ in range(NP):
                    n = 12 * c + NP + np_
                    act.wait_ge(S["qkv_full"], n + 1)
                    act.activation(k_emb[:, np_, c * 8:(c + 1) * 8].rearrange("p b i -> p (b i)"), bank[qkv_bank(n)][:], ACT.Copy)\
                        .then_inc(S["k_ready"], 1)

            def copy_scores(t):
                both = banks[:, 2 * (t % 2):2 * (t % 2) + 2].rearrange("p h (m s j) -> p (h m) s j", m=4, s=2)
                act.wait_ge(S["scores_full"], t + 1)
                if t >= NREL:
                    act.wait_ge(S["rel_out", t % NREL], 16 * (t // NREL))
                act.activation(pos_sb[:, t % NREL].rearrange("p b c n -> p n b c"),
                               both[:, :, 1].rearrange("p (n b) c -> p n b c", n=NP), ACT.Copy).then_inc(S["pos_ready"], 1)
                if t >= NS:
                    act.wait_ge(S["probs_turned"], t - NS + 1)
                act.activation(score[:, t % NS].rearrange("p n b j -> p (n b) j"), both[:, :, 0], ACT.Copy)\
                    .then_inc(S["qk_ready"], 1)

            turned_hi(0, 7, slice(0, HALF))
            copy_qkv(0)
            turned_hi(1, 4, slice(HALF, TOK))
            for t in range(2):
                copy_scores(t)
            copy_qkv(1)
            for t in range(2, NREL):
                copy_scores(t)

            act.wait_ge(S["in_raw", 0], 16)
            act.activation(w_hi[0][:], raw[0][:], ACT.Copy).then_inc(S["w_hi"], 1)
            act.wait_ge(S["in_small"], 16)
            act.activation(wg_hi[:], sml[:, WG0:WG0 + E0], ACT.Copy).then_inc(S["gate_w_hi"], 1)

            for t in range(NT + 1):
                if t >= 1:
                    act.wait_ge(S["probs_turned"], t)
                    if t >= 3:
                        act.wait_ge(S["heads_full"], t - 2)
                    act.activation(probs_t[:, (t - 1) % 2].rearrange("p n j -> p (n j)"), bank[4][:], ACT.Copy)\
                        .then_inc(S["probs_t"], 1)
                if t < NT:
                    act.wait_ge(S["shifted"], t + 1)
                    a = score[:, t % NS].rearrange("p n b j -> p (n b j)")
                    act.activation(a, a, ACT.Exp, scale=HD ** -0.5).then_inc(S["probs"], 1)
                    if t + NREL < NT:
                        copy_scores(t + NREL)
                if t >= 1:
                    act.wait_ge(S["heads_full"], t)
                    if t >= 3:
                        act.wait_ge(S["mixed_full"], t - 2)
                    for b2 in range(2):
                        act.activation(heads_t[:, (t - 1) % 2, :, b2 * L:(b2 + 1) * L],
                                       bank[5 + b2][:, 0:NP * L].rearrange("p (n i) -> p n i", n=NP), ACT.Copy)\
                            .then_inc(S["heads_t"], 1)

            for c in range(2):
                turned_hi(2 + c, 6 + c, slice(c * HALF, (c + 1) * HALF))
            act.wait_ge(S["router"], 1)
            act.activation(rt[:, 9, 0:NT], rt[:, 8, 0:NT], ACT.Exp).then_inc(S["router"], 1)
            act.wait_ge(S["combT_full"], 1)
            act.activation(comb_t[0:NT * E0], bank[5][0:NT * E0, 0:P], ACT.Copy).then_inc(S["combT"], 1)

            def silus(e, c, j, first=False):
                if c == 0:
                    act.wait_ge(S["in_bias", j], 8 * (e - j) + 16)
                for ft in range(FT):
                    n = 8 * e + 4 * c + ft
                    act.wait_ge(S["p1_full"], n + 1)
                    if not first:
                        act.wait_ge(S["h_lo"], n - 3)
                    act.activation(hid[:, ft], bank[ft][:], ACT.Silu, bias=bias0[j][:, ft:ft + 1]).then_inc(S["silu"], 1)

            def high_weights(e, j):
                act.wait_ge(S["in_raw", j], 8 * (e - j) + 16)
                act.wait_ge(S["y_full"], 2 * e)
                act.activation(w_hi[j][:], raw[j][:], ACT.Copy).then_inc(S["w_hi"], 1)

            silus(0, 0, 0, first=True)
            with act.Fori(0, 3) as i:
                for j in range(2):
                    high_weights(2 * i + (j + 1), 1 - j)
                    silus(2 * i + j, 1, j)
                    silus(2 * i + (j + 1), 0, 1 - j)
            high_weights(7, 1)
            silus(6, 1, 0)
            silus(7, 0, 1)
            silus(7, 1, 1)

            act.wait_ge(S["zeros_made"], 1)
            act.wait_ge(S["self_shift"], 1)
            for b2 in range(2):
                rows = slice(b2 * L, (b2 + 1) * L)
                act.activation(s_prob[rows, :, b2 * L:(b2 + 1) * L], s_shift[rows], ACT.Exp).then_inc(S["self_probs"], 1)
            act.wait_ge(S["self_turned"], 1)
            act.activation(s_pt[:, 0:TH].rearrange("p t j -> p (t j)"), bank[1][:], ACT.Copy).then_inc(S["self_pt"], 1)

            act.wait_ge(S["turned"], 7)
            act.activation(x4t[:, 0:TH].rearrange("p t j -> p (t j)"), bank[0][:], ACT.Copy).then_inc(S["x4t"], 1)
            act.wait_ge(S["choice"], 1)
            act.activation(choice[:, 1], choice[:, 0], ACT.Exp).then_inc(S["choice"], 1)
            act.wait_ge(S["choice_turned"], 1)
            act.activation(st[0:NT * E1, 0], bank[3][0:NT * E1, 0:P], ACT.Copy).then_inc(S["choice_t"], 1)
            for t in range(0, NT, 2):
                act.wait_ge(S["gather_full"], t // 2 + 1)
                act.activation(x_g[:, :, t:t + 2].rearrange("p e t s -> p t e s"),
                               bank[4 + t // 2][:].rearrange("p (t e s) -> p t e s", t=2, e=E1), ACT.Copy)\
                    .then_inc(S["gathered"], 1)
            for e in range(E1):
                for ft in range(2):
                    act.wait_ge(S["e1_full"], 2 * e + ft + 1)
                    if e >= 2:
                        act.wait_ge(S["e1_y_full"], e - 1)
                    act.activation(hmid[:, e % 2, ft], bank[2 * (e % 2) + ft][:, 0:NT * SLOT], ACT.Gelu,
                                   bias=m1[:, e, RAW1 - 3 + ft:RAW1 - 2 + ft]).then_inc(S["gelu"], 1)
            for g in range(4):
                act.wait_ge(S["y_turned"], g + 1)
                act.activation(y_nat[:, 2 * g:2 * g + 2].rearrange("p t g x -> p (t g x)"), bank[g][:], ACT.Copy)\
                    .then_inc(S["y_ready"], 1)

        @block.tensor
        def _(pe):
            mm = pe.matmul

            def three(out_, l_hi, l_lo, r_hi, r_lo, start=True, stop=True):
                mm(out_, l_hi, r_hi, start=start, stop=False)
                mm(out_, l_hi, r_lo, start=False, stop=False)
                return mm(out_, l_lo, r_hi, start=False, stop=stop)

            def turn(k, c, b, src):
                for t in range(TH):
                    pe.wait_ge(S["ln_out"], (2 * k + c) * TH + t + 1)
                    last = pe.transpose(bank[b][:, t * P:(t + 1) * P], src[:, c * TH + t], ident)
                last.then_inc(S["turned"], 1)

            for layer, full in ((0, "gate_full"), (1, "inner_full")):
                pe.wait_ge(S["noisy_w"], layer + 1)
                for c in range(2):
                    pe.wait_ge(S["in_x0"] if c == 0 else S["in_x1"], 16)
                    for kt in range(KT):
                        last = mm(bank[2 * c + layer][:], wn[:, layer, kt], x_in[:, c, kt], start=kt == 0, stop=kt == KT - 1)
                    last.then_inc(S[full], 1)
            pe.wait_ge(S["in_pos"], 16)
            pe.wait_ge(S["in_consts"], 16)
            for np_ in range(NP):
                last = mm(bank[4][:, np_ * L:(np_ + 1) * L], pw[0:FREQS, np_ * P:(np_ + 1) * P],
                          cst[0:FREQS, SINS:SINS + L], start=True, stop=True)
            last.then_inc(S["emb_full"], 1)
            pe.wait_ge(S["in_small"], 16)
            for c in range(2):
                pe.wait_ge(S["mixed"], c + 1)
                for t in range(TH):
                    last = mm(bank[5 + c][:, t * P:(t + 1) * P], mixed[:, c, t * P:(t + 1) * P], sml[:, W3:W3 + X],
                              start=True, stop=True)
                last.then_inc(S["embed_full"], 1)

            def project(c):
                cols = slice(c * HALF, (c + 1) * HALF)
                pe.wait_ge(S["qkv_w_lo"], 1)
                pe.wait_ge(S["xt_lo"], c + 1)
                for m in range(12):
                    n = 12 * c + m
                    qkv_bank_free(n)
                    if m < 8:
                        w = slice(m * P, (m + 1) * P)
                        last = three(bank[qkv_bank(n)][:], qw_hi[:, w], qw_lo[:, w], xt_hi[:, cols], xt_lo[:, cols])
                    else:
                        x_ = slice(c * HALF + (m - 8) * P, c * HALF + (m - 7) * P)
                        w = slice(8 * P, 12 * P)
                        last = three(bank[qkv_bank(n)][:], xt_hi[:, x_], xt_lo[:, x_], qw_hi[:, w], qw_lo[:, w])
                    last.then_inc(S["qkv_full"], 1)

            def qkv_bank_free(n):
                if n < 12:
                    if n == 5:
                        pe.wait_ge(S["h_ready"], 2)
                    if n >= 6:
                        wait_item(n - 6)
                else:
                    m = n - 12
                    if m in (0, 3):
                        pe.wait_ge(S["xt_lo"], 2 if m == 0 else 1)
                    elif m in (4, 5):
                        pe.wait_ge(S["pos_ready"], 2)
                        pe.wait_ge(S["qk_ready"], 2)
                    else:
                        wait_item({1: 10, 2: 11}[m] if m < 6 else n - 6)

            def wait_item(n):
                c, m = n // 12, n % 12
                if m < 4:
                    pe.wait_ge(S["q_even"], 4 * c + m + 1)
                    pe.wait_ge(S["q_odd"], 4 * c + m + 1)
                elif m < 8:
                    pe.wait_ge(S["k_ready"], 4 * c + m - 3)
                else:
                    pe.wait_ge(S["v_ready"], 4 * c + m - 7)

            def scores(t):
                c = t // TH
                pe.wait_ge(S["q_even"], 4 * (c + 1))
                pe.wait_ge(S["q_odd"], 4 * (c + 1))
                pe.wait_ge(S["k_ready"], 4 * (c + 1))
                if t == 0:
                    pe.wait_ge(S["emb_ready"], 1)
                    pe.wait_ge(S["block_zeros"], 2)
                for item in {0: (6, 7), 1: (8, 9), 3: (22, 23)}.get(t, ()):
                    wait_item(item)
                if t >= 2:
                    pe.wait_ge(S["pos_ready"], t - 1)
                    pe.wait_ge(S["qk_ready"], t - 1)
                for np_ in range(NP):
                    for b2 in range(2):
                        img = 2 * t + b2
                        o = (np_ % 2 * 2 + b2) * P
                        last = mm(bank[2 * (t % 2) + np_ // 2][:, o:o + P], q_block[:, np_, img].rearrange("p n i -> p (n i)"),
                                  k_emb[:, np_, img::B - img], start=True, stop=True)
                last.then_inc(S["scores_full"], 1)

            turn(0, 0, 7, xn)
            project(0)
            pe.wait_ge(S["emb_ready"], 1)
            turn(0, 1, 4, xn)
            scores(0)
            scores(1)
            project(1)
            scores(2)
            scores(3)

            for t in range(NT + 2):
                if 1 <= t <= NT:
                    pe.wait_ge(S["normed"], t)
                    if t == 1:
                        wait_item(18)
                    else:
                        pe.wait_ge(S["probs_t"], t - 1)
                    for np_ in range(NP):
                        last = pe.transpose(bank[4][:, np_ * P:(np_ + 1) * P],
                                            score[:, (t - 1) % NS, np_].rearrange("p b j -> p (b j)"), ident)
                    last.then_inc(S["probs_turned"], 1)
                if 2 <= t:
                    pe.wait_ge(S["heads_t"], 2 * (t - 1))
                    if t == 2:
                        wait_item(21)
                    else:
                        pe.wait_ge(S["h1_ready"], t - 2)
                    for np_ in range(NP):
                        last = mm(bank[7][:, 0:X], heads_t[:, (t - 2) % 2, np_], sml[:, WO + np_ * X:WO + (np_ + 1) * X],
                                  start=np_ == 0, stop=np_ == NP - 1)
                    last.then_inc(S["mixed_full"], 1)
                if t + NREL < NT:
                    scores(t + NREL)
                if 1 <= t <= NT:
                    pe.wait_ge(S["probs_t"], t)
                    pe.wait_ge(S["v_ready"], 4 * ((t - 1) // TH + 1))
                    if t == 1:
                        wait_item(19)
                        wait_item(20)
                    else:
                        pe.wait_ge(S["heads_t"], 2 * (t - 1))
                    for b2 in range(2):
                        keys = slice(b2 * L, (b2 + 1) * L)
                        for np_ in range(NP):
                            for n2 in range(2):
                                h = 2 * np_ + n2
                                last = mm(bank[5 + b2][n2 * L:(n2 + 1) * L, np_ * L:(np_ + 1) * L],
                                          v_sb[keys, t - 1, h * HD:(h + 1) * HD],
                                          probs_t[keys, (t - 1) % 2, np_, n2 * L:(n2 + 1) * L], start=True, stop=True)
                    last.then_inc(S["heads_full"], 1)

            for c in range(2):
                if c == 0:
                    pe.wait_ge(S["heads_t"], 2 * NT)
                else:
                    pe.wait_ge(S["h1_ready"], NT)
                turn(1, c, 6 + c, xn)
            pe.wait_ge(S["gate_w_lo"], 1)
            for t in range(NT):
                pe.wait_ge(S["xt_lo"], 3 + t // TH)
                w = slice(t * P, (t + 1) * P)
                last = three(bank[4][:, t * E0:(t + 1) * E0], xt_hi[:, w], xt_lo[:, w], wg_hi[:], wg_lo[:])
            last.then_inc(S["router_full"], 1)

            def up(e, c, j, first=False):
                cols = slice(c * HALF, (c + 1) * HALF)
                if c == 0:
                    pe.wait_ge(S["w_lo"], e + 1)
                for ft in range(FT):
                    n = 8 * e + 4 * c + ft
                    if not first:
                        pe.wait_ge(S["silu"], n - 3)
                    w = slice(ft * P, (ft + 1) * P)
                    three(bank[ft][:], w_hi[j][:, w], w_lo[j][:, w], xt_hi[:, cols], xt_lo[:, cols])\
                        .then_inc(S["p1_full"], 1)

            def down(e, c, j):
                pe.wait_ge(S["h_lo"], 8 * e + 4 * c + 4)
                pe.wait_ge(S["y_scaled"], 2 * e + c + 1)
                for ft in range(FT):
                    w = slice(F0 + ft * X, F0 + (ft + 1) * X)
                    last = three(bank[6 + c][:], w_hi[j][:, w], w_lo[j][:, w], hid_hi[:, c, ft], hid_lo[:, c, ft],
                                 start=ft == 0, stop=ft == FT - 1)
                last.then_inc(S["y_full"], 1)

            pe.nop().then_inc(S["y_full"], 2)
            up(0, 0, 0, first=True)
            pe.wait_ge(S["router"], 3)
            pe.transpose(bank[5][0:NT * E0, 0:P], rt[:, 11], ident).then_inc(S["combT_full"], 1)
            with pe.Fori(0, 3) as i:
                for j in range(2):
                    e = 2 * i + j
                    up(e, 1, j)
                    down(e, 0, j)
                    up(2 * i + (j + 1), 0, 1 - j)
                    down(e, 1, j)
            up(6, 1, 0)
            down(6, 0, 0)
            up(7, 0, 1)
            down(6, 1, 0)
            up(7, 1, 1)
            down(7, 0, 1)
            down(7, 1, 1)

            for c in range(2):
                pe.wait_ge(S["acc"], 2 + 2 * E0 - 1 + c)
                for t in range(TH):
                    last = pe.transpose(bank[4 + c][:, t * P:(t + 1) * P], acc[:, c, t * P:(t + 1) * P], ident)
                last.then_inc(S["acc_turned"], 1)

            x4f = x4t[:].rearrange("p t j -> p (t j)")
            for c in range(2):
                pe.wait_ge(S["y_scaled"], 2 + 2 * E0)
                turn(2, c, 6 + c, xn)
            for t in range(NT):
                pe.wait_ge(S["xt_lo"], 5 + t // TH)
                for b2 in range(2):
                    img = slice((2 * t + b2) * L, (2 * t + b2 + 1) * L)
                    last = mm(bank[0][b2 * L:(b2 + 1) * L, t * L:(t + 1) * L], x4f[:, img], x4f[:, img],
                              start=True, stop=True)
            last.then_inc(S["self_full"], 1)
            pe.wait_ge(S["self_probs"], 2)
            for c in range(2):
                for t in range(TH):
                    last = pe.transpose(bank[1 + c][:, t * P:(t + 1) * P], s_prob[:, c * TH + t], ident)
                last.then_inc(S["self_turned"], 1)
            for c in range(2):
                pe.wait_ge(S["self_pt"], 2)
                for t in range(TH):
                    tt = c * TH + t
                    last = mm(bank[4 + c][:, t * P:(t + 1) * P], s_pt[:, tt], xn[:, tt], start=True, stop=True)
                last.then_inc(S["self_y"], 1)

            turn(3, 0, 0, xn)
            turn(3, 1, 1, xn)
            for t in range(NT):
                pe.wait_ge(S["x4t"], 2)
                last = mm(bank[2][:, t * E1:(t + 1) * E1], x4t[:, t], sml[:, WG1:WG1 + E1], start=True, stop=True)
            last.then_inc(S["choice_full"], 1)
            pe.wait_ge(S["choice"], 3)
            pe.transpose(bank[3][0:NT * E1, 0:P], choice[:, 2].rearrange("p t e -> p (t e)"), ident)\
                .then_inc(S["choice_turned"], 1)
            pe.wait_ge(S["top"], 1)
            pe.transpose(bank[2][:, 0:NT * E1], st[0:NT * E1, 5], ident[0:NT * E1, 0:NT * E1]).then_inc(S["slots_turned"], 1)
            for t in range(NT):
                pe.wait_ge(S["onehot"], 1 + t // TH)
                last = mm(bank[4 + t // 2][:, (t % 2) * 256:(t % 2 + 1) * 256], xn[:, t],
                          onehot[:, t].rearrange("p e s -> p (e s)"), start=True, stop=True)
                if t % 2:
                    last.then_inc(S["gather_full"], 1)

            pe.wait_ge(S["in_moe1"], 16)
            pe.wait_ge(S["gathered"], 4)

            def up1(e):
                for ft in range(2):
                    if e >= 2:
                        pe.wait_ge(S["gelu"], 2 * e - 3 + ft)
                    mm(bank[2 * (e % 2) + ft][:, 0:NT * SLOT], m1[:, e, ft * P:(ft + 1) * P],
                       x_g[:, e].rearrange("p t s -> p (t s)"), start=True, stop=True).then_inc(S["e1_full"], 1)

            def down1(e):
                pe.wait_ge(S["gelu"], 2 * e + 2)
                if e >= 2:
                    pe.wait_ge(S["e1_y"], e - 1)
                for ft in range(2):
                    last = mm(bank[4 + e % 2][:, 0:NT * SLOT], m1[:, e, F1 + ft * X:F1 + (ft + 1) * X],
                              hmid[:, e % 2, ft], start=ft == 0, stop=ft == 1)
                last.then_inc(S["e1_y_full"], 1)

            up1(0)
            for e in range(E1):
                if e + 1 < E1:
                    up1(e + 1)
                down1(e)
                if e in (1, 3, 5, 7):
                    g = e // 2
                    b = 6 + g % 2
                    pe.wait_ge(S["gated"], 1 + g // 2)
                    if g >= 2:
                        pe.wait_ge(S["c_ready"], g - 1)
                    for k in range(4):
                        t, eg = 2 * g + k // 2, k % 2
                        last = pe.transpose(bank[b][:, k * P:(k + 1) * P],
                                            gated[:, t, eg * 4:(eg + 1) * 4].rearrange("p e s -> p (e s)"), ident)
                    last.then_inc(S["c_turned"], 1)
            pe.wait_ge(S["e1_y"], E1)
            for g in range(4):
                for k in range(4):
                    t, eg = 2 * g + k // 2, k % 2
                    last = pe.transpose(bank[g][:, k * P:(k + 1) * P], y_g[:, t, eg * 4:(eg + 1) * 4].rearrange("p e s -> p (e s)"), ident)
                last.then_inc(S["y_turned"], 1)
            for t in range(NT):
                pe.wait_ge(S["y_ready"], t // 2 + 1)
                pe.wait_ge(S["c_ready"], 4)
                if t >= 4:
                    pe.wait_ge(S["h4_ready"], t - 3)
                for eg in range(2):
                    last = mm(bank[4 + t % 4][:, 0:X], c_mat[:, t, eg], y_nat[:, t, eg],
                              start=eg == 0, stop=eg == 1)
                last.then_inc(S["h4_full"], 1)

        @block.vector
        def _(dve):
            steps = [0]

            def link(ins):
                steps[0] += 1
                ins.then_inc(S["dve_step"], 1)
                dve.wait_ge(S["dve_step"], steps[0])

            dve.memset(pads[:], MASKED).then_inc(S["pads_made"], 1)
            dve.wait_ge(S["in_eps"], 16)
            dve.scalar_tensor_tensor(out=eps_f[:, 0], in0=eps[:, 0:BIAS], scalar=-1.0, in1=eps[:, 0:BIAS], op0=ALU.mult, op1=ALU.max)\
               .then_inc(S["eps_abs"], 1)

            dve.wait_ge(S["eps_sign"], 1)
            dve.wait_ge(S["eps_sqrt"], 1)
            dve.tensor_tensor(eps_f[:, 0], eps_f[:, 1], eps_f[:, 2], ALU.mult).then_inc(S["eps_root"], 1)
            dve.wait_ge(S["eps_root"], 1)
            for layer in range(2):
                dve.wait_ge(S["in_tok_w0"] if layer == 0 else S["in_tok_w1"], 16)
                for kt in range(KT):
                    ei = EI + 2 * layer + kt
                    dve.scalar_tensor_tensor(out=outer[:, layer, kt], in0=tw[:, 2 * layer + 1, kt],
                                             scalar=eps_f[:, 0, ei:ei + 1], in1=eps_f[:, 0, layer * P:(layer + 1) * P],
                                             op0=ALU.mult, op1=ALU.mult).then_inc(S["noise_outer"], 1)
                b = BIAS + 2 * layer
                dve.scalar_tensor_tensor(out=bn[:, layer:layer + 1], in0=eps[:, b + 1:b + 2],
                                         scalar=eps_f[:, 0, EOC + layer:EOC + layer + 1], in1=eps[:, b:b + 1],
                                         op0=ALU.mult, op1=ALU.add).then_inc(S["noisy_b"], 1)
                dve.wait_ge(S["noise_outer"], 2 * layer + 2)
                dve.tensor_tensor(wn[:, layer], tw[:, 2 * layer], outer[:, layer], ALU.add).then_inc(S["noisy_w"], 1)

            for c in range(2):
                dve.wait_ge(S["noisy_b"], 1)
                dve.wait_ge(S["gate_full"], c + 1)
                dve.tensor_scalar(gate[:, c], bank[2 * c][:], bn[:, 0:1], None, ALU.add).then_inc(S["gate"], 1)
                dve.wait_ge(S["gate"], c + 1)
                dve.tensor_scalar(u[:, c], gate[:, c], 40.0, None, ALU.min).then_inc(S["gate_cap"], 1)
            dve.wait_ge(S["noisy_b"], 2)
            for c in range(2):
                dve.wait_ge(S["inner_full"], c + 1)
                dve.scalar_tensor_tensor(out=inner[:, c], in0=bank[2 * c + 1][:], scalar=bn[:, 1:2], in1=gate[:, c],
                                         op0=ALU.add, op1=ALU.mult).then_inc(S["gated_inner"], 1)
            dve.wait_ge(S["in_qkv"], 16)
            dve.tensor_copy(qw_hi[:], qw[:]).then_inc(S["qkv_w_hi"], 1)
            for c in range(2):
                dve.wait_ge(S["gate_log"], c + 1)
                dve.tensor_tensor(softplus[:, c], softplus[:, c], gate[:, c], ALU.add).then_inc(S["gate_sum"], 1)
            dve.wait_ge(S["noisy_w"], 2)
            dve.wait_ge(S["gate_sum"], 2)
            dve.wait_ge(S["emb_full"], 1)
            dve.tensor_copy(k_emb[:, :, B], bank[4][:, 0:NP * L].rearrange("p (n v) -> p n v", n=NP)).then_inc(S["emb_ready"], 1)
            for c in range(2):
                dve.wait_ge(S["gate_sigmoid"], c + 1)
                dve.wait_ge(S["gated_inner"], c + 1)
                dve.tensor_tensor(mixed[:, c], inner[:, c], u[:, c], ALU.mult).then_inc(S["mixed"], 1)

            def norm_stats(k, src, t):
                dve.bn_stats(stats[:, k, t], src[:, t]).then_inc(S["ln_stats"], 1)

            def norm_moments(k, c):
                for t in range(TH):
                    dve.wait_ge(S["ln_stats"], (2 * k + c) * TH + t + 1)
                    dve.bn_aggr(mv[:, k, c * TH + t], stats[:, k, c * TH + t]).then_inc(S["ln_moments"], 1)

            def norm_apply(k, c, src):
                dve.wait_ge(S["ln_rstd"], 2 * k + c + 1)
                for t in range(c * TH, (c + 1) * TH):
                    dve.tensor_scalar(xn[:, t], src[:, t], mv[:, k, t, 0:1], rstd[:, k, t:t + 1], ALU.subtract, ALU.mult)\
                        .then_inc(S["ln_out"], 1)

            def turned_lo(n, b, cols):
                dve.wait_ge(S["xt_hi"], n + 1)
                dve.tensor_tensor(xt_lo[:, cols], bank[b][:], xt_hi[:, cols].bitcast(F32), ALU.subtract)\
                    .then_inc(S["xt_lo"], 1)

            dve.wait_ge(S["pe_bias"], 1)
            for c in range(2):
                dve.wait_ge(S["embed_full"], c + 1)
                dve.tensor_tensor(h_a[:, c * TH:(c + 1) * TH], bank[5 + c][:].rearrange("p (t x) -> p t x", t=TH),
                                  pe_b3[:].unsqueeze(1).broadcast_to([P, TH, X]), ALU.add).then_inc(S["h_ready"], 1)
                dve.wait_ge(S["h_ready"], c + 1)
                for t in range(c * TH, (c + 1) * TH):
                    norm_stats(0, h_a, t)
                norm_moments(0, c)
            for c in range(2):
                norm_apply(0, c, h_a)

            def copy_qkv(c):
                for np_ in range(NP):
                    n = 12 * c + np_
                    dve.wait_ge(S["qkv_full"], n + 1)
                    dve.tensor_scalar(q_block[L:P, np_, c * 8:(c + 1) * 8, 1, :],
                                      bank[qkv_bank(n)][L:P].rearrange("p (b i) -> p b i", b=8),
                                      sml[L:P, QB + np_:QB + np_ + 1], None, ALU.add).then_inc(S["q_odd"], 1)
                for t in range(TH):
                    n = 12 * c + 2 * NP + t
                    dve.wait_ge(S["qkv_full"], n + 1)
                    dve.tensor_copy(v_sb[:, c * TH + t], bank[qkv_bank(n)][:]).then_inc(S["v_ready"], 1)

            turned_lo(0, 7, slice(0, HALF))
            copy_qkv(0)
            turned_lo(1, 4, slice(HALF, TOK))
            copy_qkv(1)
            dve.wait_ge(S["gate_w_hi"], 1)
            dve.tensor_tensor(wg_lo[:], sml[:, WG0:WG0 + E0], wg_hi[:].bitcast(F32), ALU.subtract).then_inc(S["gate_w_lo"], 1)

            dve.wait_ge(S["out_bias"], NT)
            for t in range(NT + 2):
                if t < NT:
                    n = t % NREL
                    a = score[:, t % NS].rearrange("p n b j -> p (n b) j")
                    dve.wait_ge(S["qk_ready"], t + 1)
                    dve.wait_ge(S["rel_in", n], 32 * (t // NREL + 1))
                    dve.tensor_tensor(score[:, t % NS], score[:, t % NS],
                                      rel_sb[:, n].rearrange("p b j n -> p n b j"), ALU.add).then_inc(S["rel_added"], 1)
                    dve.wait_ge(S["rel_added"], t + 1)
                    dve.reduce_max(srow[:, 0, t], a, AX.X).then_inc(S["row_max"], 1)
                    dve.wait_ge(S["row_max"], t + 1)
                    dve.tensor_tensor(a, a, srow[:, 0, t].unsqueeze(2).broadcast_to([P, 8, L]), ALU.subtract)\
                        .then_inc(S["shifted"], 1)
                if t >= 2:
                    dve.wait_ge(S["mixed_full"], t - 1)
                    dve.tensor_tensor(h_b[:, t - 2], bank[7][:, 0:X], h_b[:, t - 2], ALU.add).then_inc(S["h1_ready"], 1)
                    dve.wait_ge(S["h1_ready"], t - 1)
                    norm_stats(1, h_b, t - 2)
                if t < NT:
                    dve.wait_ge(S["probs"], t + 1)
                    dve.reduce_sum(srow[:, 1, t], a, AX.X).then_inc(S["prob_sum"], 1)
                    dve.wait_ge(S["prob_sum"], t + 1)
                    dve.reciprocal(srow[:, 2, t], srow[:, 1, t]).then_inc(S["prob_rsum"], 1)
            for c in range(2):
                norm_moments(1, c)
            for c in range(2):
                norm_apply(1, c, h_b)
            for c in range(2):
                turned_lo(2 + c, 6 + c, slice(c * HALF, (c + 1) * HALF))

            lg = [rt[:, k].rearrange("p (e t) -> p t e", t=NT) for k in range(12)]
            row = [rt[:, k, 0:NT] for k in range(12)]

            def bc(v):
                return v.unsqueeze(2).broadcast_to([P, NT, E0])

            dve.wait_ge(S["router_full"], 1)
            link(dve.tensor_tensor(lg[0], bank[4][:, 0:NT * E0].rearrange("p (t e) -> p t e", t=NT),
                                           sml[:, BG:BG + E0].unsqueeze(1).broadcast_to([P, NT, E0]), ALU.add))
            rev = cst[:, REV:REV + E0].unsqueeze(1).broadcast_to([P, NT, E0])
            for k, (src, one, top) in enumerate(((0, 2, 6), (3, 4, 7))):
                link(dve.reduce_max(row[top], lg[src], AX.X))
                link(dve.tensor_tensor(lg[1], lg[src], bc(row[top]), ALU.is_equal))
                link(dve.tensor_tensor(lg[1], lg[1], rev, ALU.mult))
                link(dve.reduce_max(row[5], lg[1], AX.X))
                link(dve.tensor_tensor(lg[one], bc(row[5]), rev, ALU.is_equal))
                if k == 0:
                    link(dve.scalar_tensor_tensor(out=rt[:, 3], in0=rt[:, 2], scalar=-3.0e38, in1=rt[:, 0],
                                                          op0=ALU.mult, op1=ALU.add))
            dve.tensor_tensor(row[8], row[7], row[6], ALU.subtract).then_inc(S["router"], 1)
            dve.wait_ge(S["router"], 2)
            link(dve.tensor_scalar(row[5], row[9], 1.0, None, ALU.add))
            link(dve.reciprocal(row[6], row[5]))
            link(dve.tensor_tensor(row[7], row[9], row[6], ALU.mult))
            link(dve.tensor_tensor(lg[0], lg[2], bc(row[6]), ALU.mult))
            link(dve.tensor_tensor(lg[1], lg[4], bc(row[7]), ALU.mult))
            dve.tensor_tensor(rt[:, 11], rt[:, 0], rt[:, 1], ALU.add).then_inc(S["router"], 1)
            dve.nop().then_inc(S["y_scaled"], 2)

            def splits(e, c):
                dve.wait_ge(S["y_full"], 2 * e + c + 1)
                for ft in range(FT + 1):
                    n = 8 * e + 4 * c + ft
                    if ft < FT:
                        dve.wait_ge(S["silu"], n + 1)
                        dve.tensor_copy(hid_hi[:, c, ft], hid[:, ft]).then_inc(S["h_hi"], 1)
                    if ft:
                        dve.wait_ge(S["h_hi"], n)
                        dve.tensor_tensor(hid_lo[:, c, ft - 1], hid[:, ft - 1], hid_hi[:, c, ft - 1].bitcast(F32),
                                          ALU.subtract).then_inc(S["h_lo"], 1)

            def scale(e, c, j):
                dve.wait_ge(S["y_full"], 2 + 2 * e + c + 1)
                if c == 0:
                    dve.wait_ge(S["in_comb", j], 8 * (e - j) + 16)
                dve.wait_ge(S["acc"], 2 * e + c + 1)
                dve.scalar_tensor_tensor(out=scaled[:, c], in0=bank[6 + c][:], scalar=bias0[j][:, FT:FT + 1],
                                         in1=comb_bc[j][:, c * HALF:(c + 1) * HALF], op0=ALU.add, op1=ALU.mult)\
                    .then_inc(S["y_scaled"], 1)

            splits(0, 0)
            with dve.Fori(0, 3) as i:
                for j in range(2):
                    e = 2 * i + j
                    splits(e, 1)
                    scale(e, 0, j)
                    splits(2 * i + (j + 1), 0)
                    scale(e, 1, j)
            splits(6, 1)
            scale(6, 0, 0)
            splits(7, 0)
            scale(6, 1, 0)
            splits(7, 1)
            scale(7, 0, 1)
            scale(7, 1, 1)

            for c in range(2):
                tiles = slice(c * TH, (c + 1) * TH)
                dve.wait_ge(S["acc_turned"], c + 1)
                dve.tensor_tensor(h_a[:, tiles], bank[4 + c][:].rearrange("p (t x) -> p t x", t=TH), h_b[:, tiles], ALU.add)\
                    .then_inc(S["h2_ready"], 1)
                dve.wait_ge(S["h2_ready"], c + 1)
                for t in range(c * TH, (c + 1) * TH):
                    norm_stats(2, h_a, t)
                norm_moments(2, c)
            for c in range(2):
                norm_apply(2, c, h_a)
            for c in range(2):
                dve.wait_ge(S["turned"], 5 + c)
                dve.tensor_copy(x4t[:, c * TH:(c + 1) * TH].rearrange("p t j -> p (t j)"), bank[6 + c][:])\
                    .then_inc(S["xt_lo"], 1)
            dve.wait_ge(S["self_full"], 1)
            sc = bank[0][:].rearrange("p (t j) -> p t j", t=NT)
            link(dve.reduce_max(s_row[:, 0], sc, AX.X))
            dve.tensor_tensor(s_shift[:], sc, s_row[:, 0].unsqueeze(2).broadcast_to([P, NT, L]), ALU.subtract)\
                .then_inc(S["self_shift"], 1)
            dve.wait_ge(S["self_probs"], 2)
            link(dve.reduce_sum(s_row[:, 1], s_prob[:], AX.X))
            dve.reciprocal(s_row[:, 2], s_row[:, 1]).then_inc(S["self_rsum"], 1)
            dve.wait_ge(S["self_turned"], 2)
            dve.tensor_copy(s_pt[:, TH:NT].rearrange("p t j -> p (t j)"), bank[2][:]).then_inc(S["self_pt"], 1)
            dve.wait_ge(S["self_rsum"], 1)
            for c in range(2):
                dve.wait_ge(S["self_y"], c + 1)
                for t in range(TH):
                    tt = c * TH + t
                    dve.scalar_tensor_tensor(out=h_b[:, tt], in0=bank[4 + c][:, t * P:(t + 1) * P], scalar=s_row[:, 2, tt:tt + 1],
                                             in1=h_a[:, tt], op0=ALU.mult, op1=ALU.add).then_inc(S["h3_ready"], 1)
                for t in range(TH):
                    dve.wait_ge(S["h3_ready"], c * TH + t + 1)
                    norm_stats(3, h_b, c * TH + t)
                norm_moments(3, c)
            for c in range(2):
                norm_apply(3, c, h_b)
            dve.wait_ge(S["turned"], 8)
            dve.tensor_copy(x4t[:, TH:NT].rearrange("p t j -> p (t j)"), bank[1][:]).then_inc(S["x4t"], 1)

            dve.wait_ge(S["choice_full"], 1)
            cl = bank[2][:, 0:NT * E1].rearrange("p (t e) -> p t e", t=NT)
            link(dve.reduce_max(crow[:, 0], cl, AX.X))
            dve.tensor_tensor(choice[:, 0], cl, bc(crow[:, 0]), ALU.subtract).then_inc(S["choice"], 1)
            dve.wait_ge(S["choice"], 2)
            link(dve.reduce_sum(crow[:, 1], choice[:, 1], AX.X))
            link(dve.reciprocal(crow[:, 2], crow[:, 1]))
            dve.tensor_tensor(choice[:, 2], choice[:, 1], bc(crow[:, 2]), ALU.mult).then_inc(S["choice"], 1)

            R = slice(0, NT * E1)
            dve.wait_ge(S["choice_t"], 1)
            for rnd in range(2):
                for b2 in range(2):
                    img = slice(b2 * L, (b2 + 1) * L)
                    link(dve.max(top8[R, 2 * rnd + b2], st[R, rnd, img]))
                    link(dve.match_replace(out=st[R, rnd + 1, img], in_to_replace=top8[R, 2 * rnd + b2],
                                                   in_values=st[R, rnd, img], imm_value=-1.0))
            link(dve.tensor_scalar(st[R, 3], st[R, 2], 0.0, None, ALU.is_lt))
            link(dve.memset(st[R, 1], 1.0))
            link(dve.tensor_tensor_scan(st[R, 4], st[R, 1], st[R, 3], 0.0, ALU.mult, ALU.add))
            dve.tensor_tensor(st[R, 5], st[R, 4], st[R, 3], ALU.mult).then_inc(S["top"], 1)
            dve.wait_ge(S["slots_turned"], 1)
            sl = bank[2][:, 0:NT * E1].rearrange("p (t e) -> p t e", t=NT)
            for c in range(2):
                tiles = slice(c * TH, (c + 1) * TH)
                full = [P, TH * E1, SLOT]
                dve.tensor_tensor(onehot[:, tiles].rearrange("p t e s -> p (t e) s"),
                                  sl[:, tiles].rearrange("p t e -> p (t e)").unsqueeze(2).broadcast_to(full),
                                  cst[:, SLOTS:SLOTS + SLOT].unsqueeze(1).broadcast_to(full), ALU.is_equal)\
                    .then_inc(S["onehot"], 1)
            for c in range(2):
                tiles = slice(c * TH, (c + 1) * TH)
                full = [P, TH * E1, SLOT]
                dve.wait_ge(S["onehot"], c + 1)
                dve.tensor_tensor(gated[:, tiles].rearrange("p t e s -> p (t e) s"),
                                  onehot[:, tiles].rearrange("p t e s -> p (t e) s"),
                                  choice[:, 2, tiles].rearrange("p t e -> p (t e)").unsqueeze(2).broadcast_to(full), ALU.mult)\
                    .then_inc(S["gated"], 1)
            for e in range(E1):
                dve.wait_ge(S["e1_y_full"], e + 1)
                dve.tensor_scalar(y_g[:, :, e], bank[4 + e % 2][:, 0:NT * SLOT].rearrange("p (t s) -> p t s", t=NT),
                                  m1[:, e, RAW1 - 1:RAW1], None, ALU.add).then_inc(S["e1_y"], 1)
                if e in (1, 3, 5, 7):
                    g = e // 2
                    dve.wait_ge(S["c_turned"], g + 1)
                    dve.tensor_copy(c_mat[:, 2 * g:2 * g + 2].rearrange("p t g x -> p (t g x)"), bank[6 + g % 2][:])\
                        .then_inc(S["c_ready"], 1)
            for t in range(NT):
                dve.wait_ge(S["h4_full"], t + 1)
                dve.tensor_tensor(h_a[:, t], bank[4 + t % 4][:, 0:X], h_b[:, t], ALU.add)\
                    .then_inc(S["h4_ready"], 1)


def shape_tables():
    c = np.zeros((P, CONSTS), np.float32)
    c[:, IDENT:IDENT + P] = np.eye(P, dtype=np.float32)
    at = np.arange(L, dtype=np.float32)[:, None]
    div = np.exp(np.arange(0, X, 2, dtype=np.float32) * np.float32(-np.log(10000.0) / X)).astype(np.float32)
    angle = (at * div).astype(np.float32)
    enc = np.stack([np.sin(angle), np.cos(angle)], axis=-1).reshape(L, X)
    c[:, PE_:PE_ + X] = np.concatenate([enc, enc])
    index = np.arange(FREQS)
    frequency = np.pi * (2 / 2500) ** (index // 2 / (FREQS // 2 - 1))
    sins = np.sin(frequency * np.arange(L)[:, None] + np.pi / 2 * (index % 2))
    c[0:FREQS, SINS:SINS + L] = sins.astype(np.float32)[::-1].T
    c[:, REV:REV + E0] = E0 - np.arange(E0)
    c[:, SLOTS:SLOTS + SLOT] = 1 + np.arange(SLOT)
    return c


def kernel(**inputs):
    import concourse.bacc as bacc
    from concourse.bass_utils import run_bass_kernel_spmd

    a = {k: np.asarray(v) for k, v in inputs.items()}

    def rows(v):
        return np.broadcast_to(v[None, :], (P, v.shape[0]))

    def parts(w):
        return w.reshape(-1, P, w.shape[-1]).transpose(1, 0, 2).reshape(P, -1)

    x = a["x"].reshape(B, L // 8, 16, 8, 16).transpose(2, 4, 0, 1, 3)
    x = x.reshape(KT, P, 2, HALF).transpose(1, 2, 0, 3)
    tok = {k[7:]: v for k, v in a.items() if k.startswith("L0_tok_")}
    tok_w = np.stack([parts(tok[k].T) for k in ("W1_w", "W1_sw", "W2_w", "W2_sw")], 1).reshape(P, 4, KT, P)
    tok_eps = np.concatenate(
        [rows(tok["eps_out1"]), rows(tok["eps_out2"]), tok["eps_in1"].reshape(KT, P).T, tok["eps_in2"].reshape(KT, P).T]
        + [tok[k][:, None] for k in ("eps_out1", "eps_out2", "W1_b", "W1_sb", "W2_b", "W2_sb")], 1)
    small = np.concatenate(
        [tok["W3_w"].T, rows(tok["W3_b"]), rows(a["L0_attn_out_b"]), a["L0_attn_q_bias"].reshape(NP, P).T,
         parts(a["L0_attn_out_w"]), rows(a["L0_ffn_bg"]), a["L0_ffn_Wg"], a["L1_ffn_Wg"]], 1)
    moe = []
    for layer in ("L0_ffn_", "L1_ffn_"):
        w1, b1, w2, b2 = (a[layer + k] for k in ("W1", "b1", "W2", "b2"))
        moe.append(np.stack([np.concatenate([w1[e], parts(w2[e]), b1[e].reshape(-1, P).T, b2[e][:, None]], 1)
                             for e in range(w1.shape[0])]))
    arrays = {
        "x_cols": x, "tok_w": tok_w, "tok_eps": tok_eps, "qkv_w": a["L0_attn_qkv"].reshape(X, -1),
        "pos_w": a["L0_attn_positional"].reshape(FREQS, -1), "small": small, "consts": shape_tables(),
        "moe0": moe[0][:, :, :RAW0], "moe0_b": moe[0][:, :, RAW0:], "moe1": moe[1].transpose(1, 0, 2),
    }
    nc = bacc.Bacc("TRN2", target_bir_lowering=False, num_devices=1)
    args = []
    for name, v in arrays.items():
        arrays[name] = np.ascontiguousarray(v)
        args.append(nc.dram_tensor(name, v.shape, F32, kind="ExternalInput").ap())
    args.append(nc.dram_tensor("rel_dram", (NREL, P, 1024), F32, kind="Internal").ap())
    args.append(nc.dram_tensor("comb_dram", (NT * E0, P), F32, kind="Internal").ap())
    out = nc.dram_tensor("out", (B, L, X), F32, kind="ExternalOutput").ap()
    tower(nc, *args, out)
    r = run_bass_kernel_spmd(nc, [arrays], core_ids=[0])
    return r.results[0]["out"]
```

```python
import numpy as np

import concourse.bass as bass
from concourse import mybir
from contextlib import ExitStack

F32 = mybir.dt.float32
F32R = mybir.dt.float32r
BF16 = mybir.dt.bfloat16
ALU = mybir.AluOpType
ACT = mybir.ActivationFunctionType
AX = mybir.AxisListType

P = 128
B, L, X = 16, 64, 128
TOK = B * L
NT = TOK // P
HALF = TOK // 2
TH = NT // 2
KT = 2
HEADS, HD = 8, 64
NP = HEADS // 2
FREQS = 64
E0, F0 = 8, 512
FT = F0 // P
E1, F1 = 8, 256
CAP = L * 2 // E1
SLOT = 2 * CAP
EPS = 1e-5
MASKED = -1000.0 * HD ** 0.5
NREL = 4
NS = NREL + 2

EO, EI, EOC, BIAS = 0, 256, 260, 262
W3, B3, OB, QB, WO, BG, WG0, WG1 = 0, 128, 256, 384, 388, 900, 908, 916
SMALL = 924
IDENT, PE_, SINS, REV, SLOTS, CONSTS = 0, 128, 256, 320, 328, 360
RAW0 = F0 + FT * X
RAW1 = F1 + 2 * X + 2 + 1


def qkv_bank(n):
    return (0, 1, 2, 3, 5, 6)[n % 6] if n < 12 else (4, 5, 6, 7, 2, 3)[n % 6]


def tower(nc, x_cols, tok_w, tok_eps, qkv_w, pos_w, small, consts, moe0, moe0_b1, moe0_b2, moe1, rel_dram, comb_dram, out):
    names = ["dve_step", "in_tok_w0", "in_tok_w1", "in_eps", "in_x0", "in_x1", "in_small", "in_consts", "in_qkv", "in_pos", "in_moe1",
             "idle_made", "pads_made", "pads_out", "block_zeros", "half_made", "zeros_made",
             "eps_abs", "eps_sqrt", "eps_sign", "eps_root", "noise_outer", "noisy_w", "noisy_b", "pe_bias", "out_bias",
             "gate_full", "inner_full", "gate", "gate_cap", "gate_exp", "gate_log", "gate_sum", "gate_sigmoid",
             "gated_inner", "mixed", "embed_full", "h_ready",
             "ln_stats", "ln_moments", "ln_eps", "ln_rstd", "ln_out",
             "turned", "xt_hi", "xt_lo", "qkv_w_hi", "qkv_w_lo",
             "qkv_full", "q_even", "q_odd", "k_ready", "v_ready", "v_ready_act", "emb_full", "emb_ready",
             "scores_full", "pos_ready", "qk_ready", "rel_added", "row_max", "shifted", "probs", "prob_sum",
             "prob_rsum", "normed", "probs_turned", "probs_t", "heads_full", "heads_t", "mixed_full", "h1_ready",
             "gate_w_hi", "gate_w_lo", "router_full", "router", "combT_full", "combT", "comb_out",
             "w_hi", "w_lo", "p1_full", "silu", "h_hi", "h_lo", "y_full", "y_scaled", "acc",
             "acc_turned", "h2_ready",
             "self_full", "self_max", "self_shift", "self_probs", "self_sum", "self_rsum", "self_turned",
             "self_pt", "self_y", "h3_ready",
             "x4t", "choice_full", "choice", "choice_turned", "choice_t", "top", "slots_turned", "onehot", "gated",
             "gather_full", "gathered", "e1_full", "gelu", "e1_y_full", "e1_y", "c_turned", "c_ready",
             "y_turned", "y_ready", "h4_full", "h4_ready", "out_done"]
    with ExitStack() as ctx:
        S = {n: ctx.enter_context(nc.semaphore(n)) for n in names}
        for n in range(NREL):
            for kind in ("rel_out", "rel_in"):
                S[kind, n] = ctx.enter_context(nc.semaphore(f"{kind}{n}"))
        for n in range(2):
            for kind in ("in_raw", "in_b1", "in_b2", "in_comb"):
                S[kind, n] = ctx.enter_context(nc.semaphore(f"{kind}{n}"))

        def sb(where, name, *shape, dt=F32):
            return where.enter_context(nc.sbuf_tensor(name, [P, *shape], dt))

        banks = ctx.enter_context(nc.psum_tensor("banks", [P, 8, 512], F32))
        bank = [banks[:, n] for n in range(8)]

        cst = sb(ctx, "cst", CONSTS)
        sml = sb(ctx, "sml", SMALL)
        eps = sb(ctx, "eps", BIAS + 4)
        eps_f = sb(ctx, "eps_f", 3, EOC + 2)
        pe_b3 = sb(ctx, "pe_b3", X)
        h_a = sb(ctx, "h_a", NT, X)
        h_b = sb(ctx, "h_b", NT, X)
        xn = sb(ctx, "xn", NT, X)
        xt_hi = sb(ctx, "xt_hi", TOK, dt=F32R)
        xt_lo = sb(ctx, "xt_lo", TOK, dt=F32R)
        stats = sb(ctx, "stats", 4, NT, 6)
        mv = sb(ctx, "mv", 4, NT, 2)
        var_eps = sb(ctx, "var_eps", 4, NT)
        rstd = sb(ctx, "rstd", 4, NT)
        mhalf = sb(ctx, "mhalf", NT)
        raw = [sb(ctx, f"raw{j}", RAW0) for j in range(2)]
        b1 = [sb(ctx, f"b1_{j}", FT) for j in range(2)]
        b2s = [sb(ctx, f"b2s{j}", 1) for j in range(2)]
        w_hi = [sb(ctx, f"w_hi{j}", 2 * F0, dt=F32R) for j in range(2)]
        w_lo = [sb(ctx, f"w_lo{j}", 2 * F0, dt=F32R) for j in range(2)]
        wg_hi = sb(ctx, "wg_hi", E0, dt=F32R)
        wg_lo = sb(ctx, "wg_lo", E0, dt=F32R)
        m1 = sb(ctx, "m1", E1, RAW1)
        idle = sb(ctx, "idle", 512, dt=BF16)
        ident = cst[:, IDENT:IDENT + P]

        with ExitStack() as tok:
            x_in = sb(tok, "x_in", 2, KT, HALF)
            tw = sb(tok, "tw", 4, KT, P)
            outer = sb(tok, "outer", 2, KT, P)
            wn = sb(tok, "wn", 2, KT, P)
            bn = sb(tok, "bn", 2)
            gate = sb(tok, "gate", 2, HALF)
            u = sb(tok, "u", 2, HALF)
            softplus = sb(tok, "softplus", 2, HALF)
            inner = sb(tok, "inner", 2, HALF)
            mixed = sb(tok, "mixed", 2, HALF)

        with ExitStack() as att:
            k_emb = sb(att, "k_emb", NP, B + 1, L)
            v_sb = sb(att, "v_sb", NT, HEADS * HD)
            score = sb(att, "score", NS, NP, 2, L)
            probs_t = sb(att, "probs_t", 2, NP, P)
            heads_t = sb(att, "heads_t", 2, NP, P)
            q_block = sb(att, "q_block", NP, B, 2, L)
            qw_hi = sb(att, "qw_hi", 3 * HEADS * HD, dt=F32R)
            qw_lo = sb(att, "qw_lo", 3 * HEADS * HD, dt=F32R)
            qw = sb(att, "qw", 3 * HEADS * HD)
            pw = sb(att, "pw", HEADS * HD)
            pos_sb = sb(att, "pos_sb", NREL, 2, L, NP)
            rel_sb = sb(att, "rel_sb", NREL, 2, L, NP)
            pads = sb(att, "pads", 2, L * NP)
            srow = sb(att, "srow", 3, NT, 8)

        with ExitStack() as mix:
            hid_hi = sb(mix, "hid_hi", 2, FT, HALF, dt=F32R)
            hid_lo = sb(mix, "hid_lo", 2, FT, HALF, dt=F32R)
            hid = sb(mix, "hid", FT, HALF)
            comb_bc = [sb(mix, f"comb_bc{j}", TOK) for j in range(2)]
            scaled = sb(mix, "scaled", 2, HALF)
            acc = sb(mix, "acc", 2, HALF)
            rt = sb(mix, "rt", 12, NT * E0)
            comb_t = sb(mix, "comb_t", P)

        with ExitStack() as sec:
            s_shift = sb(sec, "s_shift", NT, L)
            s_prob = sb(sec, "s_prob", NT, P)
            s_pt = sb(sec, "s_pt", NT, P)
            s_row = sb(sec, "s_row", 3, NT)
            x4t = sb(sec, "x4t", NT, P)
            choice = sb(sec, "choice", 4, NT, E1)
            crow = sb(sec, "crow", 3, NT)
            st = sb(sec, "st", 6, P)
            top8 = sb(sec, "top8", 4, 8)
            onehot = sb(sec, "onehot", NT, E1, SLOT)
            gated = sb(sec, "gated", NT, E1, SLOT)
            x_g = sb(sec, "x_g", E1, NT, SLOT)
            hmid = sb(sec, "hmid", 2, 2, NT * SLOT)
            y_g = sb(sec, "y_g", NT, E1, SLOT)
            y_nat = sb(sec, "y_nat", NT, 2, X)
            c_mat = sb(sec, "c_mat", NT, 2, P)

        block = ctx.enter_context(nc.Block())

        def read_rel(sp, t):
            n, k = t % NREL, t // NREL
            sp.wait_ge(S["rel_out", n], 16 * (k + 1))
            if k:
                sp.wait_ge(S["rel_added"], t - NREL + 1)
            for n2 in range(2):
                sp.dma_start(rel_sb[n2 * L:(n2 + 1) * L, n].rearrange("p b c n -> p b (c n)"),
                             bass.AP(tensor=rel_dram.tensor, offset=n * P * 1024 + n2 * L * 1024 + (L - 1) * NP,
                                     ap=[[1024 - NP, L], [512, 2], [1, 256]])).then_inc(S["rel_in", n], 16)

        @block.sync
        def _(sp):
            sp.dma_start(eps[:], tok_eps).then_inc(S["in_eps"], 16)
            sp.dma_start(tw[:, 0:2], tok_w[:, 0:2]).then_inc(S["in_tok_w0"], 16)
            sp.dma_start(x_in[:, 0], x_cols[:, 0]).then_inc(S["in_x0"], 16)
            sp.dma_start(tw[:, 2:4], tok_w[:, 2:4]).then_inc(S["in_tok_w1"], 16)
            sp.dma_start(x_in[:, 1], x_cols[:, 1]).then_inc(S["in_x1"], 16)
            sp.dma_start(cst[:], consts).then_inc(S["in_consts"], 16)
            sp.dma_start(pw[0:FREQS], pos_w).then_inc(S["in_pos"], 16)
            sp.dma_start(qw[:], qkv_w).then_inc(S["in_qkv"], 16)
            sp.dma_start(sml[:], small).then_inc(S["in_small"], 16)
            for e in range(2):
                sp.dma_start(raw[e][:], moe0[e]).then_inc(S["in_raw", e], 16)
                sp.dma_start(b1[e][:], moe0_b1[e]).then_inc(S["in_b1", e], 16)
                sp.dma_start(b2s[e][:], moe0_b2[e]).then_inc(S["in_b2", e], 16)
            sp.wait_ge(S["pads_made"], 1)
            for n in range(NREL):
                sp.dma_start(bass.AP(tensor=rel_dram.tensor, offset=n * P * 1024 + 256, ap=[[1024, P], [512, 2], [1, 256]]),
                             pads[:]).then_inc(S["pads_out"], 16)
            sp.dma_start(m1[:], moe1).then_inc(S["in_moe1"], 16)
            sp.wait_ge(S["pads_out"], 16 * NREL)

            def write_rel(t):
                n, k = t % NREL, t // NREL
                sp.wait_ge(S["pos_ready"], t + 1)
                if k:
                    sp.wait_ge(S["rel_in", n], 32 * k)
                sp.dma_start(bass.AP(tensor=rel_dram.tensor, offset=n * P * 1024, ap=[[1024, P], [512, 2], [1, 256]]),
                             pos_sb[:, n].rearrange("p b c n -> p b (c n)")).then_inc(S["rel_out", n], 16)

            for t in range(0, NREL, 2):
                write_rel(t)
                write_rel(t + 1)
                read_rel(sp, t)
                read_rel(sp, t + 1)
            for t in range(NREL, NT):
                write_rel(t)
                read_rel(sp, t)

            for e in (2, 3):
                sp.wait_ge(S["w_lo"], e - 1)
                sp.dma_start(raw[e % 2][:], moe0[e]).then_inc(S["in_raw", e % 2], 16)
            sp.wait_ge(S["combT"], 1)
            sp.dma_start(comb_dram, comb_t[0:NT * E0]).then_inc(S["comb_out"], 16)
            sp.wait_ge(S["comb_out"], 16)
            for e in range(E0):
                if e >= 2:
                    if e >= 4:
                        sp.wait_ge(S["w_lo"], e - 1)
                        sp.dma_start(raw[e % 2][:], moe0[e]).then_inc(S["in_raw", e % 2], 16)
                    sp.wait_ge(S["silu"], 8 * (e - 1))
                    sp.dma_start(b1[e % 2][:], moe0_b1[e]).then_inc(S["in_b1", e % 2], 16)
                    sp.wait_ge(S["y_scaled"], 2 + 2 * (e - 1))
                    sp.dma_start(b2s[e % 2][:], moe0_b2[e]).then_inc(S["in_b2", e % 2], 16)
                sp.dma_start(comb_bc[e % 2][:], bass.AP(tensor=comb_dram.tensor, offset=e * TOK, ap=[[0, P], [1, TOK]]))\
                    .then_inc(S["in_comb", e % 2], 16)

            out_v = out.rearrange("(t b) l x -> (b l) t x", b=2)
            for c in range(2):
                sp.wait_ge(S["h4_ready"], TH * (c + 1))
                sp.dma_start(out_v[:, c * TH:(c + 1) * TH], h_a[:, c * TH:(c + 1) * TH]).then_inc(S["out_done"], 16)
            sp.wait_ge(S["out_done"], 32)

        @block.gpsimd
        def _(pool):
            pool.memset(mhalf[:], -0.5).then_inc(S["half_made"], 1)

            def rstd_of(k, c):
                cols = slice(c * TH, (c + 1) * TH)
                n = 2 * k + c
                pool.wait_ge(S["ln_moments"], TH * (n + 1))
                pool.tensor_scalar(var_eps[:, k, cols], mv[:, k, cols, 1], EPS, None, ALU.add).then_inc(S["ln_eps"], 1)
                pool.wait_ge(S["ln_eps"], n + 1)
                pool.tensor_tensor(rstd[:, k, cols], var_eps[:, k, cols], mhalf[:, cols], ALU.pow).then_inc(S["ln_rstd"], 1)

            pool.wait_ge(S["half_made"], 1)
            for n2 in range(2):
                rows = slice(n2 * L, (n2 + 1) * L)
                if n2:
                    pool.wait_ge(S["block_zeros"], 1)
                pool.memset(q_block[rows, :, :, 1 - n2, :].rearrange("p n b i -> p (n b) i"), 0.0).then_inc(S["block_zeros"], 1)
            pool.wait_ge(S["block_zeros"], 2)
            pool.wait_ge(S["in_consts"], 16)
            pool.wait_ge(S["in_small"], 16)
            pool.tensor_tensor(pe_b3[:], cst[:, PE_:PE_ + X], sml[:, B3:B3 + X], ALU.add).then_inc(S["pe_bias"], 1)
            pool.wait_ge(S["qkv_w_hi"], 1)
            pool.tensor_tensor(qw_lo[:], qw[:], qw_hi[:].bitcast(F32), ALU.subtract).then_inc(S["qkv_w_lo"], 1)
            for c in range(2):
                rstd_of(0, c)
            for t in range(NT):
                pool.tensor_tensor(h_b[:, t], h_a[:, t], sml[:, OB:OB + X], ALU.add).then_inc(S["out_bias"], 1)

            def low_weights(e, j):
                pool.wait_ge(S["w_hi"], e + 1)
                pool.tensor_tensor(w_lo[j][:], raw[j][:], w_hi[j][:].bitcast(F32), ALU.subtract)\
                    .then_inc(S["w_lo"], 1)

            for e in range(2):
                low_weights(e, e)

            for t in range(NT):
                a = score[:, t % NS].rearrange("p n b j -> p (n b) j")
                if t == 6:
                    rstd_of(1, 0)
                pool.wait_ge(S["prob_rsum"], t + 1)
                pool.tensor_tensor(a, a, srow[:, 2, t].unsqueeze(2).broadcast_to([P, 8, L]), ALU.mult)\
                    .then_inc(S["normed"], 1)
            rstd_of(1, 1)
            pool.memset(acc[:], 0.0).then_inc(S["acc"], 2)

            def accumulate(e, c):
                pool.wait_ge(S["y_scaled"], 2 + 2 * e + c + 1)
                pool.wait_ge(S["acc"], 2 + 2 * e + c)
                pool.tensor_tensor(acc[:, c], acc[:, c], scaled[:, c], ALU.add).then_inc(S["acc"], 1)

            accumulate(0, 0)
            with pool.Fori(0, 3) as i:
                for j in (1, 0):
                    low_weights(2 * i + (3 - j), 1 - j)
                    accumulate(2 * i + (1 - j), 1)
                    accumulate(2 * i + (2 - j), 0)
            accumulate(6, 1)
            for c in range(2):
                accumulate(7, c)
            pool.memset(s_prob[:], 0.0).then_inc(S["zeros_made"], 1)
            for k in (2, 3):
                for c in range(2):
                    rstd_of(k, c)

        @block.scalar
        def _(act):
            act.wait_ge(S["eps_abs"], 1)
            act.activation(eps_f[:, 2], eps_f[:, 0], ACT.Sqrt).then_inc(S["eps_sqrt"], 1)
            act.wait_ge(S["in_eps"], 16)
            act.activation(eps_f[:, 1], eps[:, 0:BIAS], ACT.Sign).then_inc(S["eps_sign"], 1)

            for c in range(2):
                act.wait_ge(S["gate_cap"], c + 1)
                act.activation(u[:, c], u[:, c], ACT.Exp).then_inc(S["gate_exp"], 1)
            for c in range(2):
                act.wait_ge(S["gate_exp"], c + 1)
                act.activation(softplus[:, c], u[:, c], ACT.Ln, bias=1.0, scale=0.5).then_inc(S["gate_log"], 1)
            for c in range(2):
                act.wait_ge(S["gate_sum"], c + 1)
                act.activation(u[:, c], softplus[:, c], ACT.Sigmoid).then_inc(S["gate_sigmoid"], 1)

            def turned_hi(n, b, cols):
                act.wait_ge(S["turned"], n + 1)
                act.activation(xt_hi[:, cols], bank[b][:], ACT.Copy).then_inc(S["xt_hi"], 1)

            def copy_qk(c):
                for np_ in range(NP):
                    n = 12 * c + np_
                    act.wait_ge(S["qkv_full"], n + 1)
                    act.activation(q_block[0:L, np_, c * 8:(c + 1) * 8, 0, :],
                                   bank[qkv_bank(n)][0:L].rearrange("p (b i) -> p b i", b=8), ACT.Identity,
                                   bias=sml[0:L, QB + np_:QB + np_ + 1]).then_inc(S["q_even"], 1)
                for np_ in range(NP):
                    n = 12 * c + NP + np_
                    act.wait_ge(S["qkv_full"], n + 1)
                    act.activation(k_emb[:, np_, c * 8:(c + 1) * 8].rearrange("p b i -> p (b i)"), bank[qkv_bank(n)][:], ACT.Copy)\
                        .then_inc(S["k_ready"], 1)

            def copy_scores(t):
                both = banks[:, 2 * (t % 2):2 * (t % 2) + 2].rearrange("p h (m s j) -> p (h m) s j", m=4, s=2)
                act.wait_ge(S["scores_full"], t + 1)
                if t >= NREL:
                    act.wait_ge(S["rel_out", t % NREL], 16 * (t // NREL))
                act.activation(pos_sb[:, t % NREL].rearrange("p b c n -> p n b c"),
                               both[:, :, 1].rearrange("p (n b) c -> p n b c", n=NP), ACT.Copy).then_inc(S["pos_ready"], 1)
                if t >= NS:
                    act.wait_ge(S["probs_turned"], t - NS + 1)
                act.activation(score[:, t % NS].rearrange("p n b j -> p (n b) j"), both[:, :, 0], ACT.Copy)\
                    .then_inc(S["qk_ready"], 1)

            def exps(t):
                act.wait_ge(S["shifted"], t + 1)
                a = score[:, t % NS].rearrange("p n b j -> p (n b j)")
                act.activation(a, a, ACT.Exp, scale=HD ** -0.5).then_inc(S["probs"], 1)

            turned_hi(0, 7, slice(0, HALF))
            copy_qk(0)
            act.wait_ge(S["in_small"], 16)
            act.activation(wg_hi[:], sml[:, WG0:WG0 + E0], ACT.Copy).then_inc(S["gate_w_hi"], 1)
            for e in range(2):
                act.wait_ge(S["in_raw", e], 16)
                act.activation(w_hi[e][:], raw[e][:], ACT.Copy).then_inc(S["w_hi"], 1)
            turned_hi(1, 4, slice(HALF, TOK))
            for t in range(2):
                copy_scores(t)
            copy_qk(1)
            for t in range(2):
                act.wait_ge(S["qkv_full"], 12 + 2 * NP + t + 1)
                act.activation(v_sb[:, TH + t], bank[qkv_bank(12 + 2 * NP + t)][:], ACT.Copy).then_inc(S["v_ready_act"], 1)
            exps(0)
            for t in range(2, NREL):
                copy_scores(t)

            for t in range(NT + 1):
                if t >= 1:
                    act.wait_ge(S["probs_turned"], t)
                    if t >= 3:
                        act.wait_ge(S["heads_full"], t - 2)
                    act.activation(probs_t[:, (t - 1) % 2].rearrange("p n j -> p (n j)"), bank[4][:], ACT.Copy)\
                        .then_inc(S["probs_t"], 1)
                if t + 1 < NT:
                    exps(t + 1)
                if t + NREL < NT:
                    copy_scores(t + NREL)
                if t == NT:
                    turned_hi(2, 2, slice(0, HALF))
                if t >= 1:
                    act.wait_ge(S["heads_full"], t)
                    if t >= 3:
                        act.wait_ge(S["mixed_full"], t - 2)
                    for b2 in range(2):
                        act.activation(heads_t[:, (t - 1) % 2, :, b2 * L:(b2 + 1) * L],
                                       bank[5 + b2][:, 0:NP * L].rearrange("p (n i) -> p n i", n=NP), ACT.Copy)\
                            .then_inc(S["heads_t"], 1)

            turned_hi(3, 7, slice(HALF, TOK))

            def silus(e, c, j, first=False):
                if c == 0:
                    act.wait_ge(S["in_b1", j], 8 * (e - j) + 16)
                for ft in range(FT):
                    n = 8 * e + 4 * c + ft
                    act.wait_ge(S["p1_full"], n + 1)
                    if not first:
                        act.wait_ge(S["h_lo"], n - 3)
                    act.activation(hid[:, ft], bank[ft][:], ACT.Silu, bias=b1[j][:, ft:ft + 1]).then_inc(S["silu"], 1)

            def high_weights(e, j):
                act.wait_ge(S["in_raw", j], 8 * (e - j) + 16)
                act.wait_ge(S["y_full"], 2 * e)
                act.activation(w_hi[j][:], raw[j][:], ACT.Copy).then_inc(S["w_hi"], 1)

            silus(0, 0, 0, first=True)
            silus(0, 1, 0)
            act.wait_ge(S["router"], 1)
            act.activation(rt[:, 9, 0:NT], rt[:, 8, 0:NT], ACT.Tanh, scale=0.5).then_inc(S["router"], 1)
            act.wait_ge(S["combT_full"], 1)
            act.activation(comb_t[0:NT * E0], bank[5][0:NT * E0, 0:P], ACT.Copy).then_inc(S["combT"], 1)
            silus(1, 0, 1)
            with act.Fori(0, 3) as i:
                for j in (1, 0):
                    high_weights(2 * i + (3 - j), 1 - j)
                    silus(2 * i + (2 - j), 1, j)
                    silus(2 * i + (3 - j), 0, 1 - j)
            silus(7, 1, 1)

            act.wait_ge(S["zeros_made"], 1)
            act.wait_ge(S["self_shift"], 1)
            for b2 in range(2):
                rows = slice(b2 * L, (b2 + 1) * L)
                act.activation(s_prob[rows, :, b2 * L:(b2 + 1) * L], s_shift[rows], ACT.Exp).then_inc(S["self_probs"], 1)
            act.wait_ge(S["self_turned"], 1)
            act.activation(s_pt[:, 0:TH].rearrange("p t j -> p (t j)"), bank[1][:], ACT.Copy).then_inc(S["self_pt"], 1)

            act.wait_ge(S["turned"], 7)
            act.activation(x4t[:, 0:TH].rearrange("p t j -> p (t j)"), bank[0][:], ACT.Copy).then_inc(S["x4t"], 1)
            act.wait_ge(S["choice"], 1)
            act.activation(choice[:, 1], choice[:, 0], ACT.Exp).then_inc(S["choice"], 1)
            act.wait_ge(S["choice_turned"], 1)
            act.activation(st[0:NT * E1, 0], bank[3][0:NT * E1, 0:P], ACT.Copy).then_inc(S["choice_t"], 1)
            for t in range(0, NT, 2):
                act.wait_ge(S["gather_full"], t // 2 + 1)
                act.activation(x_g[:, :, t:t + 2].rearrange("p e t s -> p t e s"),
                               bank[4 + t // 2][:].rearrange("p (t e s) -> p t e s", t=2, e=E1), ACT.Copy)\
                    .then_inc(S["gathered"], 1)
            for e in range(E1):
                for ft in range(2):
                    act.wait_ge(S["e1_full"], 2 * e + ft + 1)
                    if e >= 2:
                        act.wait_ge(S["e1_y_full"], e - 1)
                    act.activation(hmid[:, e % 2, ft], bank[2 * (e % 2) + ft][:, 0:NT * SLOT], ACT.Gelu,
                                   bias=m1[:, e, RAW1 - 3 + ft:RAW1 - 2 + ft]).then_inc(S["gelu"], 1)
            for g in range(4):
                act.wait_ge(S["y_turned"], g + 1)
                act.activation(y_nat[:, 2 * g:2 * g + 2].rearrange("p t g x -> p (t g x)"), bank[g][:], ACT.Copy)\
                    .then_inc(S["y_ready"], 1)

        @block.tensor
        def _(pe):
            mm = pe.matmul

            def three(out_, l_hi, l_lo, r_hi, r_lo, start=True, stop=True):
                mm(out_, l_hi, r_hi, start=start, stop=False)
                mm(out_, l_hi, r_lo, start=False, stop=False)
                return mm(out_, l_lo, r_hi, start=False, stop=stop)

            def turn(k, c, b, src):
                for t in range(TH):
                    pe.wait_ge(S["ln_out"], (2 * k + c) * TH + t + 1)
                    last = pe.transpose(bank[b][:, t * P:(t + 1) * P], src[:, c * TH + t], ident)
                last.then_inc(S["turned"], 1)

            def keep_busy(n, b):
                for _ in range(n):
                    mm(bank[b][:], idle[:, 0:P], idle[:], start=True, stop=True)

            pe.wait_ge(S["idle_made"], 1)
            keep_busy(10, 7)
            for layer, full in ((0, "gate_full"), (1, "inner_full")):
                pe.wait_ge(S["noisy_w"], layer + 1)
                for c in range(2):
                    pe.wait_ge(S["in_x0"] if c == 0 else S["in_x1"], 16)
                    for kt in range(KT):
                        last = mm(bank[2 * c + layer][:], wn[:, layer, kt], x_in[:, c, kt], start=kt == 0, stop=kt == KT - 1)
                    last.then_inc(S[full], 1)
            pe.wait_ge(S["in_pos"], 16)
            pe.wait_ge(S["in_consts"], 16)
            for np_ in range(NP):
                last = mm(bank[4][:, np_ * L:(np_ + 1) * L], pw[0:FREQS, np_ * P:(np_ + 1) * P],
                          cst[0:FREQS, SINS:SINS + L], start=True, stop=True)
            last.then_inc(S["emb_full"], 1)
            keep_busy(10, 7)
            pe.wait_ge(S["in_small"], 16)
            for c in range(2):
                pe.wait_ge(S["mixed"], c + 1)
                for t in range(TH):
                    last = mm(bank[5 + c][:, t * P:(t + 1) * P], mixed[:, c, t * P:(t + 1) * P], sml[:, W3:W3 + X],
                              start=True, stop=True)
                last.then_inc(S["embed_full"], 1)

            def project(c):
                cols = slice(c * HALF, (c + 1) * HALF)
                pe.wait_ge(S["qkv_w_lo"], 1)
                pe.wait_ge(S["xt_lo"], c + 1)
                for m in range(12):
                    n = 12 * c + m
                    qkv_bank_free(n)
                    if m < 8:
                        w = slice(m * P, (m + 1) * P)
                        last = three(bank[qkv_bank(n)][:], qw_hi[:, w], qw_lo[:, w], xt_hi[:, cols], xt_lo[:, cols])
                    else:
                        x_ = slice(c * HALF + (m - 8) * P, c * HALF + (m - 7) * P)
                        w = slice(8 * P, 12 * P)
                        last = three(bank[qkv_bank(n)][:], xt_hi[:, x_], xt_lo[:, x_], qw_hi[:, w], qw_lo[:, w])
                    last.then_inc(S["qkv_full"], 1)

            def qkv_bank_free(n):
                if n < 12:
                    if n == 5:
                        pe.wait_ge(S["h_ready"], 2)
                    if n >= 6:
                        wait_item(n - 6)
                else:
                    m = n - 12
                    if m in (0, 3):
                        pe.wait_ge(S["xt_lo"], 2 if m == 0 else 1)
                    elif m in (4, 5):
                        pe.wait_ge(S["pos_ready"], 2)
                        pe.wait_ge(S["qk_ready"], 2)
                    else:
                        wait_item({1: 10, 2: 11}[m] if m < 6 else n - 6)

            def wait_item(n):
                c, m = n // 12, n % 12
                if m < 4:
                    pe.wait_ge(S["q_even"], 4 * c + m + 1)
                    pe.wait_ge(S["q_odd"], 4 * c + m + 1)
                elif m < 8:
                    pe.wait_ge(S["k_ready"], 4 * c + m - 3)
                elif c and m < 10:
                    pe.wait_ge(S["v_ready_act"], m - 7)
                else:
                    pe.wait_ge(S["v_ready"], 4 * c + m - 7 - 2 * c)

            def scores(t):
                c = t // TH
                pe.wait_ge(S["q_even"], 4 * (c + 1))
                pe.wait_ge(S["q_odd"], 4 * (c + 1))
                pe.wait_ge(S["k_ready"], 4 * (c + 1))
                if t == 0:
                    pe.wait_ge(S["emb_ready"], 1)
                    pe.wait_ge(S["block_zeros"], 2)
                for item in {0: (6, 7), 1: (8, 9), 3: (22, 23)}.get(t, ()):
                    wait_item(item)
                if t >= 2:
                    pe.wait_ge(S["pos_ready"], t - 1)
                    pe.wait_ge(S["qk_ready"], t - 1)
                for np_ in range(NP):
                    for b2 in range(2):
                        img = 2 * t + b2
                        o = (np_ % 2 * 2 + b2) * P
                        last = mm(bank[2 * (t % 2) + np_ // 2][:, o:o + P], q_block[:, np_, img].rearrange("p n i -> p (n i)"),
                                  k_emb[:, np_, img::B - img], start=True, stop=True)
                last.then_inc(S["scores_full"], 1)

            keep_busy(10, 7)
            turn(0, 0, 7, xn)
            keep_busy(6, 0)
            project(0)
            pe.wait_ge(S["emb_ready"], 1)
            turn(0, 1, 4, xn)
            scores(0)
            scores(1)
            project(1)
            scores(2)
            scores(3)

            for t in range(NT + 2):
                if 1 <= t <= NT:
                    pe.wait_ge(S["normed"], t)
                    if t == 1:
                        wait_item(18)
                    else:
                        pe.wait_ge(S["probs_t"], t - 1)
                    for np_ in range(NP):
                        last = pe.transpose(bank[4][:, np_ * P:(np_ + 1) * P],
                                            score[:, (t - 1) % NS, np_].rearrange("p b j -> p (b j)"), ident)
                    last.then_inc(S["probs_turned"], 1)
                if t + NREL < NT:
                    scores(t + NREL)
                if 2 <= t:
                    pe.wait_ge(S["heads_t"], 2 * (t - 1))
                    if t == 2:
                        wait_item(21)
                    else:
                        pe.wait_ge(S["h1_ready"], t - 2)
                    for np_ in range(NP):
                        last = mm(bank[7][:, 0:X], heads_t[:, (t - 2) % 2, np_], sml[:, WO + np_ * X:WO + (np_ + 1) * X],
                                  start=np_ == 0, stop=np_ == NP - 1)
                    last.then_inc(S["mixed_full"], 1)
                if t == NT:
                    pe.wait_ge(S["qk_ready"], NT)
                    turn(1, 0, 2, xn)
                if 1 <= t <= NT:
                    pe.wait_ge(S["probs_t"], t)
                    if t > TH:
                        pe.wait_ge(S["v_ready_act"], 2)
                    pe.wait_ge(S["v_ready"], 4 if t <= TH else 6)
                    if t == 1:
                        wait_item(19)
                        wait_item(20)
                    else:
                        pe.wait_ge(S["heads_t"], 2 * (t - 1))
                    for b2 in range(2):
                        keys = slice(b2 * L, (b2 + 1) * L)
                        for np_ in range(NP):
                            for n2 in range(2):
                                h = 2 * np_ + n2
                                last = mm(bank[5 + b2][n2 * L:(n2 + 1) * L, np_ * L:(np_ + 1) * L],
                                          v_sb[keys, t - 1, h * HD:(h + 1) * HD],
                                          probs_t[keys, (t - 1) % 2, np_, n2 * L:(n2 + 1) * L], start=True, stop=True)
                    last.then_inc(S["heads_full"], 1)

            def up(e, c, j, first=False):
                cols = slice(c * HALF, (c + 1) * HALF)
                if c == 0:
                    pe.wait_ge(S["w_lo"], e + 1)
                for ft in range(FT):
                    n = 8 * e + 4 * c + ft
                    if not first:
                        pe.wait_ge(S["silu"], n - 3)
                    elif ft == 2:
                        pe.wait_ge(S["xt_lo"], 3)
                    w = slice(ft * P, (ft + 1) * P)
                    three(bank[ft][:], w_hi[j][:, w], w_lo[j][:, w], xt_hi[:, cols], xt_lo[:, cols])\
                        .then_inc(S["p1_full"], 1)

            def down(e, c, j):
                pe.wait_ge(S["h_lo"], 8 * e + 4 * c + 4)
                pe.wait_ge(S["y_scaled"], 2 * e + c + 1)
                for ft in range(FT):
                    w = slice(F0 + ft * X, F0 + (ft + 1) * X)
                    last = three(bank[6 + c][:], w_hi[j][:, w], w_lo[j][:, w], hid_hi[:, c, ft], hid_lo[:, c, ft],
                                 start=ft == 0, stop=ft == FT - 1)
                last.then_inc(S["y_full"], 1)

            pe.nop().then_inc(S["y_full"], 2)
            pe.wait_ge(S["xt_lo"], 3)
            up(0, 0, 0, first=True)
            pe.wait_ge(S["gate_w_lo"], 1)
            for t in range(NT):
                if t == TH:
                    pe.wait_ge(S["h1_ready"], NT)
                    turn(1, 1, 7, xn)
                    pe.wait_ge(S["xt_lo"], 4)
                w = slice(t * P, (t + 1) * P)
                last = three(bank[4][:, t * E0:(t + 1) * E0], xt_hi[:, w], xt_lo[:, w], wg_hi[:], wg_lo[:])
            last.then_inc(S["router_full"], 1)
            up(0, 1, 0)
            down(0, 0, 0)
            pe.wait_ge(S["heads_t"], 2 * NT)
            pe.wait_ge(S["router"], 3)
            pe.transpose(bank[5][0:NT * E0, 0:P], rt[:, 11], ident).then_inc(S["combT_full"], 1)
            up(1, 0, 1)
            down(0, 1, 0)
            with pe.Fori(0, 3) as i:
                for j in (1, 0):
                    e = 2 * i + (2 - j)
                    up(e, 1, j)
                    down(e, 0, j)
                    up(2 * i + (3 - j), 0, 1 - j)
                    down(e, 1, j)
            up(7, 1, 1)
            down(7, 0, 1)
            down(7, 1, 1)

            for c in range(2):
                pe.wait_ge(S["acc"], 2 + 2 * E0 - 1 + c)
                for t in range(TH):
                    last = pe.transpose(bank[4 + c][:, t * P:(t + 1) * P], acc[:, c, t * P:(t + 1) * P], ident)
                last.then_inc(S["acc_turned"], 1)

            x4f = x4t[:].rearrange("p t j -> p (t j)")
            for c in range(2):
                pe.wait_ge(S["y_scaled"], 2 + 2 * E0)
                turn(2, c, 6 + c, xn)
            for t in range(NT):
                pe.wait_ge(S["xt_lo"], 5 + t // TH)
                for b2 in range(2):
                    img = slice((2 * t + b2) * L, (2 * t + b2 + 1) * L)
                    last = mm(bank[0][b2 * L:(b2 + 1) * L, t * L:(t + 1) * L], x4f[:, img], x4f[:, img],
                              start=True, stop=True)
            last.then_inc(S["self_full"], 1)
            pe.wait_ge(S["self_probs"], 2)
            for c in range(2):
                for t in range(TH):
                    last = pe.transpose(bank[1 + c][:, t * P:(t + 1) * P], s_prob[:, c * TH + t], ident)
                last.then_inc(S["self_turned"], 1)
            for c in range(2):
                pe.wait_ge(S["self_pt"], 2)
                for t in range(TH):
                    tt = c * TH + t
                    last = mm(bank[4 + c][:, t * P:(t + 1) * P], s_pt[:, tt], xn[:, tt], start=True, stop=True)
                last.then_inc(S["self_y"], 1)

            turn(3, 0, 0, xn)
            turn(3, 1, 1, xn)
            for t in range(NT):
                pe.wait_ge(S["x4t"], 2)
                last = mm(bank[2][:, t * E1:(t + 1) * E1], x4t[:, t], sml[:, WG1:WG1 + E1], start=True, stop=True)
            last.then_inc(S["choice_full"], 1)
            pe.wait_ge(S["choice"], 3)
            pe.transpose(bank[3][0:NT * E1, 0:P], choice[:, 2].rearrange("p t e -> p (t e)"), ident)\
                .then_inc(S["choice_turned"], 1)
            pe.wait_ge(S["top"], 1)
            pe.transpose(bank[2][:, 0:NT * E1], st[0:NT * E1, 5], ident[0:NT * E1, 0:NT * E1]).then_inc(S["slots_turned"], 1)
            for t in range(NT):
                pe.wait_ge(S["onehot"], 1 + t // TH)
                last = mm(bank[4 + t // 2][:, (t % 2) * 256:(t % 2 + 1) * 256], xn[:, t],
                          onehot[:, t].rearrange("p e s -> p (e s)"), start=True, stop=True)
                if t % 2:
                    last.then_inc(S["gather_full"], 1)

            pe.wait_ge(S["in_moe1"], 16)
            pe.wait_ge(S["gathered"], 4)

            def up1(e):
                for ft in range(2):
                    if e >= 2:
                        pe.wait_ge(S["gelu"], 2 * e - 3 + ft)
                    mm(bank[2 * (e % 2) + ft][:, 0:NT * SLOT], m1[:, e, ft * P:(ft + 1) * P],
                       x_g[:, e].rearrange("p t s -> p (t s)"), start=True, stop=True).then_inc(S["e1_full"], 1)

            def down1(e):
                pe.wait_ge(S["gelu"], 2 * e + 2)
                if e >= 2:
                    pe.wait_ge(S["e1_y"], e - 1)
                for ft in range(2):
                    last = mm(bank[4 + e % 2][:, 0:NT * SLOT], m1[:, e, F1 + ft * X:F1 + (ft + 1) * X],
                              hmid[:, e % 2, ft], start=ft == 0, stop=ft == 1)
                last.then_inc(S["e1_y_full"], 1)

            up1(0)
            for e in range(E1):
                if e + 1 < E1:
                    up1(e + 1)
                down1(e)
                if e in (1, 3, 5, 7):
                    g = e // 2
                    b = 6 + g % 2
                    pe.wait_ge(S["gated"], 1 + g // 2)
                    if g >= 2:
                        pe.wait_ge(S["c_ready"], g - 1)
                    for k in range(4):
                        t, eg = 2 * g + k // 2, k % 2
                        last = pe.transpose(bank[b][:, k * P:(k + 1) * P],
                                            gated[:, t, eg * 4:(eg + 1) * 4].rearrange("p e s -> p (e s)"), ident)
                    last.then_inc(S["c_turned"], 1)
            pe.wait_ge(S["e1_y"], E1)
            for g in range(4):
                for k in range(4):
                    t, eg = 2 * g + k // 2, k % 2
                    last = pe.transpose(bank[g][:, k * P:(k + 1) * P], y_g[:, t, eg * 4:(eg + 1) * 4].rearrange("p e s -> p (e s)"), ident)
                last.then_inc(S["y_turned"], 1)
            for t in range(NT):
                pe.wait_ge(S["y_ready"], t // 2 + 1)
                pe.wait_ge(S["c_ready"], 4)
                if t >= 4:
                    pe.wait_ge(S["h4_ready"], t - 3)
                for eg in range(2):
                    last = mm(bank[4 + t % 4][:, 0:X], c_mat[:, t, eg], y_nat[:, t, eg],
                              start=eg == 0, stop=eg == 1)
                last.then_inc(S["h4_full"], 1)

        @block.vector
        def _(dve):
            steps = [0]

            def link(ins):
                steps[0] += 1
                ins.then_inc(S["dve_step"], 1)
                dve.wait_ge(S["dve_step"], steps[0])

            dve.memset(idle[:], 0.0).then_inc(S["idle_made"], 1)
            dve.memset(pads[:], MASKED).then_inc(S["pads_made"], 1)
            dve.wait_ge(S["in_eps"], 16)
            dve.scalar_tensor_tensor(out=eps_f[:, 0], in0=eps[:, 0:BIAS], scalar=-1.0, in1=eps[:, 0:BIAS], op0=ALU.mult, op1=ALU.max)\
               .then_inc(S["eps_abs"], 1)

            dve.wait_ge(S["eps_sign"], 1)
            dve.wait_ge(S["eps_sqrt"], 1)
            dve.tensor_tensor(eps_f[:, 0], eps_f[:, 1], eps_f[:, 2], ALU.mult).then_inc(S["eps_root"], 1)
            dve.wait_ge(S["eps_root"], 1)
            for layer in range(2):
                dve.wait_ge(S["in_tok_w0"] if layer == 0 else S["in_tok_w1"], 16)
                for kt in range(KT):
                    ei = EI + 2 * layer + kt
                    dve.scalar_tensor_tensor(out=outer[:, layer, kt], in0=tw[:, 2 * layer + 1, kt],
                                             scalar=eps_f[:, 0, ei:ei + 1], in1=eps_f[:, 0, layer * P:(layer + 1) * P],
                                             op0=ALU.mult, op1=ALU.mult).then_inc(S["noise_outer"], 1)
                b = BIAS + 2 * layer
                dve.scalar_tensor_tensor(out=bn[:, layer:layer + 1], in0=eps[:, b + 1:b + 2],
                                         scalar=eps_f[:, 0, EOC + layer:EOC + layer + 1], in1=eps[:, b:b + 1],
                                         op0=ALU.mult, op1=ALU.add).then_inc(S["noisy_b"], 1)
                dve.wait_ge(S["noise_outer"], 2 * layer + 2)
                dve.tensor_tensor(wn[:, layer], tw[:, 2 * layer], outer[:, layer], ALU.add).then_inc(S["noisy_w"], 1)

            for c in range(2):
                dve.wait_ge(S["noisy_b"], 1)
                dve.wait_ge(S["gate_full"], c + 1)
                dve.tensor_scalar(gate[:, c], bank[2 * c][:], bn[:, 0:1], None, ALU.add).then_inc(S["gate"], 1)
                dve.wait_ge(S["gate"], c + 1)
                dve.tensor_scalar(u[:, c], gate[:, c], 40.0, None, ALU.min).then_inc(S["gate_cap"], 1)
            dve.wait_ge(S["noisy_b"], 2)
            for c in range(2):
                dve.wait_ge(S["inner_full"], c + 1)
                dve.scalar_tensor_tensor(out=inner[:, c], in0=bank[2 * c + 1][:], scalar=bn[:, 1:2], in1=gate[:, c],
                                         op0=ALU.add, op1=ALU.mult).then_inc(S["gated_inner"], 1)
            dve.wait_ge(S["in_qkv"], 16)
            dve.tensor_copy(qw_hi[:], qw[:]).then_inc(S["qkv_w_hi"], 1)
            for c in range(2):
                dve.wait_ge(S["gate_log"], c + 1)
                dve.tensor_tensor(softplus[:, c], softplus[:, c], gate[:, c], ALU.add).then_inc(S["gate_sum"], 1)
            dve.wait_ge(S["noisy_w"], 2)
            dve.wait_ge(S["gate_sum"], 2)
            dve.wait_ge(S["emb_full"], 1)
            dve.tensor_copy(k_emb[:, :, B], bank[4][:, 0:NP * L].rearrange("p (n v) -> p n v", n=NP)).then_inc(S["emb_ready"], 1)
            for c in range(2):
                dve.wait_ge(S["gate_sigmoid"], c + 1)
                dve.wait_ge(S["gated_inner"], c + 1)
                dve.tensor_tensor(mixed[:, c], inner[:, c], u[:, c], ALU.mult).then_inc(S["mixed"], 1)

            def norm_stats(k, src, t):
                dve.bn_stats(stats[:, k, t], src[:, t]).then_inc(S["ln_stats"], 1)

            def norm_moment(k, t):
                dve.wait_ge(S["ln_stats"], k * NT + t + 1)
                dve.bn_aggr(mv[:, k, t], stats[:, k, t]).then_inc(S["ln_moments"], 1)

            def norm_moments(k, c):
                for t in range(c * TH, (c + 1) * TH):
                    norm_moment(k, t)

            def norm_apply(k, c, src):
                dve.wait_ge(S["ln_rstd"], 2 * k + c + 1)
                for t in range(c * TH, (c + 1) * TH):
                    dve.tensor_scalar(xn[:, t], src[:, t], mv[:, k, t, 0:1], rstd[:, k, t:t + 1], ALU.subtract, ALU.mult)\
                        .then_inc(S["ln_out"], 1)

            def turned_lo(n, b, cols):
                dve.wait_ge(S["xt_hi"], n + 1)
                dve.tensor_tensor(xt_lo[:, cols], bank[b][:], xt_hi[:, cols].bitcast(F32), ALU.subtract)\
                    .then_inc(S["xt_lo"], 1)

            dve.wait_ge(S["pe_bias"], 1)
            for c in range(2):
                dve.wait_ge(S["embed_full"], c + 1)
                dve.tensor_tensor(h_a[:, c * TH:(c + 1) * TH], bank[5 + c][:].rearrange("p (t x) -> p t x", t=TH),
                                  pe_b3[:].unsqueeze(1).broadcast_to([P, TH, X]), ALU.add).then_inc(S["h_ready"], 1)
                dve.wait_ge(S["h_ready"], c + 1)
                for t in range(c * TH, (c + 1) * TH):
                    norm_stats(0, h_a, t)
                norm_moments(0, c)
            for c in range(2):
                norm_apply(0, c, h_a)

            def probs_of(t):
                return score[:, t % NS].rearrange("p n b j -> p (n b) j")

            def add_rel(t):
                dve.wait_ge(S["qk_ready"], t + 1)
                dve.wait_ge(S["rel_in", t % NREL], 32 * (t // NREL + 1))
                dve.tensor_tensor(score[:, t % NS], score[:, t % NS], rel_sb[:, t % NREL].rearrange("p b j n -> p n b j"),
                                  ALU.add).then_inc(S["rel_added"], 1)

            def row_max(t):
                dve.wait_ge(S["rel_added"], t + 1)
                dve.reduce_max(srow[:, 0, t], probs_of(t), AX.X).then_inc(S["row_max"], 1)

            def shift(t):
                dve.wait_ge(S["row_max"], t + 1)
                dve.tensor_tensor(probs_of(t), probs_of(t), srow[:, 0, t].unsqueeze(2).broadcast_to([P, 8, L]), ALU.subtract)\
                    .then_inc(S["shifted"], 1)

            def q_odd(c):
                for np_ in range(NP):
                    n = 12 * c + np_
                    dve.wait_ge(S["qkv_full"], n + 1)
                    dve.tensor_scalar(q_block[L:P, np_, c * 8:(c + 1) * 8, 1, :],
                                      bank[qkv_bank(n)][L:P].rearrange("p (b i) -> p b i", b=8),
                                      sml[L:P, QB + np_:QB + np_ + 1], None, ALU.add).then_inc(S["q_odd"], 1)

            def copy_v(c):
                for t in range(2 * c, TH):
                    n = 12 * c + 2 * NP + t
                    dve.wait_ge(S["qkv_full"], n + 1)
                    dve.tensor_copy(v_sb[:, c * TH + t], bank[qkv_bank(n)][:]).then_inc(S["v_ready"], 1)

            turned_lo(0, 7, slice(0, HALF))
            q_odd(0)
            copy_v(0)
            turned_lo(1, 4, slice(HALF, TOK))
            q_odd(1)
            add_rel(0)
            row_max(0)
            shift(0)
            copy_v(1)
            dve.wait_ge(S["gate_w_hi"], 1)
            dve.tensor_tensor(wg_lo[:], sml[:, WG0:WG0 + E0], wg_hi[:].bitcast(F32), ALU.subtract).then_inc(S["gate_w_lo"], 1)

            dve.wait_ge(S["out_bias"], NT)
            for t in range(NT + 2):
                if t + 1 < NT:
                    add_rel(t + 1)
                if t < NT:
                    dve.wait_ge(S["probs"], t + 1)
                    dve.reduce_sum(srow[:, 1, t], probs_of(t), AX.X).then_inc(S["prob_sum"], 1)
                if t + 1 < NT:
                    row_max(t + 1)
                if t < NT:
                    dve.wait_ge(S["prob_sum"], t + 1)
                    dve.reciprocal(srow[:, 2, t], srow[:, 1, t]).then_inc(S["prob_rsum"], 1)
                if t + 1 < NT:
                    shift(t + 1)
                if t >= 2:
                    dve.wait_ge(S["mixed_full"], t - 1)
                    dve.tensor_tensor(h_b[:, t - 2], bank[7][:, 0:X], h_b[:, t - 2], ALU.add).then_inc(S["h1_ready"], 1)
                    dve.wait_ge(S["h1_ready"], t - 1)
                    norm_stats(1, h_b, t - 2)
                    norm_moment(1, t - 2)
                if t == NT - 1:
                    norm_apply(1, 0, h_b)
                if t == NT:
                    turned_lo(2, 2, slice(0, HALF))
            norm_apply(1, 1, h_b)
            turned_lo(3, 7, slice(HALF, TOK))

            def splits(e, c):
                dve.wait_ge(S["y_full"], 2 * e + c + 1)
                for ft in range(FT + 1):
                    n = 8 * e + 4 * c + ft
                    if ft < FT:
                        dve.wait_ge(S["silu"], n + 1)
                        dve.tensor_copy(hid_hi[:, c, ft], hid[:, ft]).then_inc(S["h_hi"], 1)
                    if ft:
                        dve.wait_ge(S["h_hi"], n)
                        dve.tensor_tensor(hid_lo[:, c, ft - 1], hid[:, ft - 1], hid_hi[:, c, ft - 1].bitcast(F32),
                                          ALU.subtract).then_inc(S["h_lo"], 1)

            dve.nop().then_inc(S["y_scaled"], 2)
            splits(0, 0)

            lg = [rt[:, k].rearrange("p (e t) -> p t e", t=NT) for k in range(12)]
            row = [rt[:, k, 0:NT] for k in range(12)]

            def bc(v):
                return v.unsqueeze(2).broadcast_to([P, NT, E0])

            dve.wait_ge(S["router_full"], 1)
            link(dve.tensor_tensor(lg[0], bank[4][:, 0:NT * E0].rearrange("p (t e) -> p t e", t=NT),
                                           sml[:, BG:BG + E0].unsqueeze(1).broadcast_to([P, NT, E0]), ALU.add))
            rev = cst[:, REV:REV + E0].unsqueeze(1).broadcast_to([P, NT, E0])
            for k, (src, one, top) in enumerate(((0, 2, 6), (3, 4, 7))):
                link(dve.reduce_max(row[top], lg[src], AX.X))
                link(dve.tensor_tensor(lg[1], lg[src], bc(row[top]), ALU.is_equal))
                link(dve.tensor_tensor(lg[1], lg[1], rev, ALU.mult))
                link(dve.reduce_max(row[5], lg[1], AX.X))
                link(dve.tensor_tensor(lg[one], bc(row[5]), rev, ALU.is_equal))
                if k == 0:
                    link(dve.scalar_tensor_tensor(out=rt[:, 3], in0=rt[:, 2], scalar=-3.0e38, in1=rt[:, 0],
                                                          op0=ALU.mult, op1=ALU.add))
            dve.tensor_tensor(row[8], row[7], row[6], ALU.subtract).then_inc(S["router"], 1)
            dve.wait_ge(S["router"], 2)
            link(dve.tensor_scalar(row[6], row[9], -0.5, 0.5, ALU.mult, ALU.add))
            link(dve.tensor_scalar(row[7], row[9], 0.5, 0.5, ALU.mult, ALU.add))
            link(dve.tensor_tensor(lg[0], lg[2], bc(row[6]), ALU.mult))
            link(dve.tensor_tensor(lg[1], lg[4], bc(row[7]), ALU.mult))
            dve.tensor_tensor(rt[:, 11], rt[:, 0], rt[:, 1], ALU.add).then_inc(S["router"], 1)

            def scale(e, c, j):
                dve.wait_ge(S["y_full"], 2 + 2 * e + c + 1)
                if c == 0:
                    dve.wait_ge(S["in_comb", j], 8 * (e - j) + 16)
                    dve.wait_ge(S["in_b2", j], 8 * (e - j) + 16)
                dve.wait_ge(S["acc"], 2 * e + c + 1)
                dve.scalar_tensor_tensor(out=scaled[:, c], in0=bank[6 + c][:], scalar=b2s[j][:],
                                         in1=comb_bc[j][:, c * HALF:(c + 1) * HALF], op0=ALU.add, op1=ALU.mult)\
                    .then_inc(S["y_scaled"], 1)

            splits(0, 1)
            splits(1, 0)
            scale(0, 0, 0)
            with dve.Fori(0, 3) as i:
                for j in (1, 0):
                    e = 2 * i + (2 - j)
                    splits(e, 1)
                    scale(2 * i + (1 - j), 1, 1 - j)
                    splits(2 * i + (3 - j), 0)
                    scale(e, 0, j)
            splits(7, 1)
            scale(6, 1, 0)
            scale(7, 0, 1)
            scale(7, 1, 1)

            for c in range(2):
                tiles = slice(c * TH, (c + 1) * TH)
                dve.wait_ge(S["acc_turned"], c + 1)
                dve.tensor_tensor(h_a[:, tiles], bank[4 + c][:].rearrange("p (t x) -> p t x", t=TH), h_b[:, tiles], ALU.add)\
                    .then_inc(S["h2_ready"], 1)
                dve.wait_ge(S["h2_ready"], c + 1)
                for t in range(c * TH, (c + 1) * TH):
                    norm_stats(2, h_a, t)
                norm_moments(2, c)
            for c in range(2):
                norm_apply(2, c, h_a)
            for c in range(2):
                dve.wait_ge(S["turned"], 5 + c)
                dve.tensor_copy(x4t[:, c * TH:(c + 1) * TH].rearrange("p t j -> p (t j)"), bank[6 + c][:])\
                    .then_inc(S["xt_lo"], 1)
            dve.wait_ge(S["self_full"], 1)
            sc = bank[0][:].rearrange("p (t j) -> p t j", t=NT)
            link(dve.reduce_max(s_row[:, 0], sc, AX.X))
            dve.tensor_tensor(s_shift[:], sc, s_row[:, 0].unsqueeze(2).broadcast_to([P, NT, L]), ALU.subtract)\
                .then_inc(S["self_shift"], 1)
            dve.wait_ge(S["self_probs"], 2)
            link(dve.reduce_sum(s_row[:, 1], s_prob[:], AX.X))
            dve.reciprocal(s_row[:, 2], s_row[:, 1]).then_inc(S["self_rsum"], 1)
            dve.wait_ge(S["self_turned"], 2)
            dve.tensor_copy(s_pt[:, TH:NT].rearrange("p t j -> p (t j)"), bank[2][:]).then_inc(S["self_pt"], 1)
            dve.wait_ge(S["self_rsum"], 1)
            for c in range(2):
                dve.wait_ge(S["self_y"], c + 1)
                for t in range(TH):
                    tt = c * TH + t
                    dve.scalar_tensor_tensor(out=h_b[:, tt], in0=bank[4 + c][:, t * P:(t + 1) * P], scalar=s_row[:, 2, tt:tt + 1],
                                             in1=h_a[:, tt], op0=ALU.mult, op1=ALU.add).then_inc(S["h3_ready"], 1)
                for t in range(TH):
                    dve.wait_ge(S["h3_ready"], c * TH + t + 1)
                    norm_stats(3, h_b, c * TH + t)
                norm_moments(3, c)
            for c in range(2):
                norm_apply(3, c, h_b)
            dve.wait_ge(S["turned"], 8)
            dve.tensor_copy(x4t[:, TH:NT].rearrange("p t j -> p (t j)"), bank[1][:]).then_inc(S["x4t"], 1)

            dve.wait_ge(S["choice_full"], 1)
            cl = bank[2][:, 0:NT * E1].rearrange("p (t e) -> p t e", t=NT)
            link(dve.reduce_max(crow[:, 0], cl, AX.X))
            dve.tensor_tensor(choice[:, 0], cl, bc(crow[:, 0]), ALU.subtract).then_inc(S["choice"], 1)
            dve.wait_ge(S["choice"], 2)
            link(dve.reduce_sum(crow[:, 1], choice[:, 1], AX.X))
            link(dve.reciprocal(crow[:, 2], crow[:, 1]))
            dve.tensor_tensor(choice[:, 2], choice[:, 1], bc(crow[:, 2]), ALU.mult).then_inc(S["choice"], 1)

            R = slice(0, NT * E1)
            dve.wait_ge(S["choice_t"], 1)
            for rnd in range(2):
                for b2 in range(2):
                    img = slice(b2 * L, (b2 + 1) * L)
                    link(dve.max(top8[R, 2 * rnd + b2], st[R, rnd, img]))
                    link(dve.match_replace(out=st[R, rnd + 1, img], in_to_replace=top8[R, 2 * rnd + b2],
                                                   in_values=st[R, rnd, img], imm_value=-1.0))
            link(dve.tensor_scalar(st[R, 3], st[R, 2], 0.0, None, ALU.is_lt))
            link(dve.memset(st[R, 1], 1.0))
            link(dve.tensor_tensor_scan(st[R, 4], st[R, 1], st[R, 3], 0.0, ALU.mult, ALU.add))
            dve.tensor_tensor(st[R, 5], st[R, 4], st[R, 3], ALU.mult).then_inc(S["top"], 1)
            dve.wait_ge(S["slots_turned"], 1)
            sl = bank[2][:, 0:NT * E1].rearrange("p (t e) -> p t e", t=NT)
            for c in range(2):
                tiles = slice(c * TH, (c + 1) * TH)
                full = [P, TH * E1, SLOT]
                dve.tensor_tensor(onehot[:, tiles].rearrange("p t e s -> p (t e) s"),
                                  sl[:, tiles].rearrange("p t e -> p (t e)").unsqueeze(2).broadcast_to(full),
                                  cst[:, SLOTS:SLOTS + SLOT].unsqueeze(1).broadcast_to(full), ALU.is_equal)\
                    .then_inc(S["onehot"], 1)
            for c in range(2):
                tiles = slice(c * TH, (c + 1) * TH)
                full = [P, TH * E1, SLOT]
                dve.wait_ge(S["onehot"], c + 1)
                dve.tensor_tensor(gated[:, tiles].rearrange("p t e s -> p (t e) s"),
                                  onehot[:, tiles].rearrange("p t e s -> p (t e) s"),
                                  choice[:, 2, tiles].rearrange("p t e -> p (t e)").unsqueeze(2).broadcast_to(full), ALU.mult)\
                    .then_inc(S["gated"], 1)
            for e in range(E1):
                dve.wait_ge(S["e1_y_full"], e + 1)
                dve.tensor_scalar(y_g[:, :, e], bank[4 + e % 2][:, 0:NT * SLOT].rearrange("p (t s) -> p t s", t=NT),
                                  m1[:, e, RAW1 - 1:RAW1], None, ALU.add).then_inc(S["e1_y"], 1)
                if e in (1, 3, 5, 7):
                    g = e // 2
                    dve.wait_ge(S["c_turned"], g + 1)
                    dve.tensor_copy(c_mat[:, 2 * g:2 * g + 2].rearrange("p t g x -> p (t g x)"), bank[6 + g % 2][:])\
                        .then_inc(S["c_ready"], 1)
            for t in range(NT):
                dve.wait_ge(S["h4_full"], t + 1)
                dve.tensor_tensor(h_a[:, t], bank[4 + t % 4][:, 0:X], h_b[:, t], ALU.add)\
                    .then_inc(S["h4_ready"], 1)


def shape_tables():
    c = np.zeros((P, CONSTS), np.float32)
    c[:, IDENT:IDENT + P] = np.eye(P, dtype=np.float32)
    at = np.arange(L, dtype=np.float32)[:, None]
    div = np.exp(np.arange(0, X, 2, dtype=np.float32) * np.float32(-np.log(10000.0) / X)).astype(np.float32)
    angle = (at * div).astype(np.float32)
    enc = np.stack([np.sin(angle), np.cos(angle)], axis=-1).reshape(L, X)
    c[:, PE_:PE_ + X] = np.concatenate([enc, enc])
    index = np.arange(FREQS)
    frequency = np.pi * (2 / 2500) ** (index // 2 / (FREQS // 2 - 1))
    sins = np.sin(frequency * np.arange(L)[:, None] + np.pi / 2 * (index % 2))
    c[0:FREQS, SINS:SINS + L] = sins.astype(np.float32)[::-1].T
    c[:, REV:REV + E0] = E0 - np.arange(E0)
    c[:, SLOTS:SLOTS + SLOT] = 1 + np.arange(SLOT)
    return c


def kernel(**inputs):
    import concourse.bacc as bacc
    from concourse.bass_utils import run_bass_kernel_spmd

    a = {k: np.asarray(v) for k, v in inputs.items()}

    def rows(v):
        return np.broadcast_to(v[None, :], (P, v.shape[0]))

    def parts(w):
        return w.reshape(-1, P, w.shape[-1]).transpose(1, 0, 2).reshape(P, -1)

    x = a["x"].reshape(B, L // 8, 16, 8, 16).transpose(2, 4, 0, 1, 3)
    x = x.reshape(KT, P, 2, HALF).transpose(1, 2, 0, 3)
    tok = {k[7:]: v for k, v in a.items() if k.startswith("L0_tok_")}
    tok_w = np.stack([parts(tok[k].T) for k in ("W1_w", "W1_sw", "W2_w", "W2_sw")], 1).reshape(P, 4, KT, P)
    tok_eps = np.concatenate(
        [rows(tok["eps_out1"]), rows(tok["eps_out2"]), tok["eps_in1"].reshape(KT, P).T, tok["eps_in2"].reshape(KT, P).T]
        + [tok[k][:, None] for k in ("eps_out1", "eps_out2", "W1_b", "W1_sb", "W2_b", "W2_sb")], 1)
    small = np.concatenate(
        [tok["W3_w"].T, rows(tok["W3_b"]), rows(a["L0_attn_out_b"]), a["L0_attn_q_bias"].reshape(NP, P).T,
         parts(a["L0_attn_out_w"]), rows(a["L0_ffn_bg"]), a["L0_ffn_Wg"], a["L1_ffn_Wg"]], 1)
    moe = []
    for layer in ("L0_ffn_", "L1_ffn_"):
        w1, b1, w2, b2 = (a[layer + k] for k in ("W1", "b1", "W2", "b2"))
        moe.append(np.stack([np.concatenate([w1[e], parts(w2[e]), b1[e].reshape(-1, P).T, b2[e][:, None]], 1)
                             for e in range(w1.shape[0])]))
    arrays = {
        "x_cols": x, "tok_w": tok_w, "tok_eps": tok_eps, "qkv_w": a["L0_attn_qkv"].reshape(X, -1),
        "pos_w": a["L0_attn_positional"].reshape(FREQS, -1), "small": small, "consts": shape_tables(),
        "moe0": moe[0][:, :, :RAW0], "moe0_b1": moe[0][:, :, RAW0:RAW0 + FT], "moe0_b2": moe[0][:, :, RAW0 + FT:], "moe1": moe[1].transpose(1, 0, 2),
    }
    nc = bacc.Bacc("TRN2", target_bir_lowering=False, num_devices=1)
    args = []
    for name, v in arrays.items():
        arrays[name] = np.ascontiguousarray(v)
        args.append(nc.dram_tensor(name, v.shape, F32, kind="ExternalInput").ap())
    args.append(nc.dram_tensor("rel_dram", (NREL, P, 1024), F32, kind="Internal").ap())
    args.append(nc.dram_tensor("comb_dram", (NT * E0, P), F32, kind="Internal").ap())
    out = nc.dram_tensor("out", (B, L, X), F32, kind="ExternalOutput").ap()
    tower(nc, *args, out)
    r = run_bass_kernel_spmd(nc, [arrays], core_ids=[0])
    return r.results[0]["out"]
```

```python
import numpy as np

import concourse.bass as bass
from concourse import mybir
from contextlib import ExitStack

F32 = mybir.dt.float32
F32R = mybir.dt.float32r
BF16 = mybir.dt.bfloat16
ALU = mybir.AluOpType
ACT = mybir.ActivationFunctionType
AX = mybir.AxisListType

P = 128
B, L, X = 16, 64, 128
TOK = B * L
NT = TOK // P
HALF = TOK // 2
TH = NT // 2
KT = 2
HEADS, HD = 8, 64
NP = HEADS // 2
FREQS = 64
E0, F0 = 8, 512
FT = F0 // P
E1, F1 = 8, 256
CAP = L * 2 // E1
SLOT = 2 * CAP
EPS = 1e-5
E_CAP = float(np.exp(40.0))
MASKED = -1000.0 * HD ** 0.5
NREL = 4
NS = NREL + 2

EO, EI, EOC, BIAS = 0, 256, 260, 262
W3, B3, OB, QB, WO, BG, WG0, WG1 = 0, 128, 256, 384, 388, 900, 908, 916
SMALL = 924
IDENT, PE_, SINS, REV, SLOTS, CONSTS = 0, 128, 256, 320, 328, 360
RAW0 = F0 + FT * X
RAW1 = F1 + 2 * X + 2 + 1


def qkv_bank(n):
    return (0, 1, 2, 3, 5, 6)[n % 6] if n < 12 else (4, 5, 6, 7, 2, 3)[n % 6]


def tower(nc, x_cols, tok_w, tok_eps, qkv_w, pos_w, small, consts, moe0, moe0_b1, moe0_b2, moe1, rel_dram, comb_dram, out):
    names = ["dve_step", "in_tok_w0", "in_tok_w1", "in_eps", "in_x0", "in_x1", "in_small", "in_consts", "in_qkv", "in_pos", "in_moe1",
             "idle_made", "table", "pads_made", "pads_out", "block_zeros", "half_made", "zeros_made",
             "eps_abs", "eps_sqrt", "eps_sign", "eps_root", "noise_outer", "noisy_w", "noisy_b", "pe_bias", "out_bias",
             "gate_full", "inner_full", "gate", "gate_cap", "gate_exp", "gate_log", "gate_sum", "gate_sigmoid",
             "gated_inner", "mixed", "embed_full", "h_ready",
             "ln_stats", "ln_moments", "ln_eps", "ln_rstd", "ln_out",
             "turned", "xt_hi", "xt_lo", "qkv_w_hi", "qkv_w_lo",
             "qkv_full", "q_even", "q_odd", "k_ready", "v_ready", "v_ready_act", "emb_full", "emb_ready",
             "scores_full", "pos_ready", "qk_ready", "rel_added", "row_max", "shifted", "probs", "prob_sum",
             "prob_rsum", "normed", "probs_turned", "probs_t", "heads_full", "heads_t", "mixed_full", "h1_ready",
             "gate_w_hi", "gate_w_lo", "router_full", "router", "combT_full", "combT", "comb_out",
             "w_hi", "w_lo", "p1_full", "silu", "h_hi", "h_lo", "y_full", "y_scaled", "acc", "acc_start",
             "h1_turned", "acc_turned", "h2_ready",
             "x4t", "self_full", "self_shift", "self_probs", "self_rsum",
             "self_turned", "self_pt", "self_y", "h3_ready",
             "choice_full", "choice", "choice_turned", "choice_t", "top8", "taken", "top", "slots_turned", "onehot", "gated",
             "gather_full", "xg_hi", "xg_lo", "xn_hi", "xn_lo", "u1_hi", "u1_lo", "e1_full", "gelu", "e1_y_full", "e1_y",
             "c_turned", "c_ready",
             "y_turned", "y_ready0", "y_ready1", "h4_full", "h4_ready", "out_done"]
    with ExitStack() as ctx:
        S = {n: ctx.enter_context(nc.semaphore(n)) for n in names}
        for n in range(NREL):
            for kind in ("rel_out", "rel_in"):
                S[kind, n] = ctx.enter_context(nc.semaphore(f"{kind}{n}"))
        for n in range(2):
            for kind in ("in_raw", "in_b1", "in_b2", "in_comb"):
                S[kind, n] = ctx.enter_context(nc.semaphore(f"{kind}{n}"))

        def sb(where, name, *shape, dt=F32):
            return where.enter_context(nc.sbuf_tensor(name, [P, *shape], dt))

        banks = ctx.enter_context(nc.psum_tensor("banks", [P, 8, 512], F32))
        bank = [banks[:, n] for n in range(8)]

        cst = sb(ctx, "cst", CONSTS)
        sml = sb(ctx, "sml", SMALL)
        eps = sb(ctx, "eps", BIAS + 4)
        eps_f = sb(ctx, "eps_f", 3, EOC + 2)
        pe_b3 = sb(ctx, "pe_b3", X)
        h_a = sb(ctx, "h_a", NT, X)
        h_b = sb(ctx, "h_b", NT, X)
        xn = sb(ctx, "xn", NT, X)
        xt_hi = sb(ctx, "xt_hi", TOK, dt=F32R)
        xt_lo = sb(ctx, "xt_lo", TOK, dt=F32R)
        stats = sb(ctx, "stats", 4, NT, 6)
        mv = sb(ctx, "mv", 4, NT, 2)
        var_eps = sb(ctx, "var_eps", 4, NT)
        rstd = sb(ctx, "rstd", 4, NT)
        mhalf = sb(ctx, "mhalf", NT)
        raw = [sb(ctx, f"raw{j}", RAW0) for j in range(2)]
        b1 = [sb(ctx, f"b1_{j}", FT) for j in range(2)]
        b2s = [sb(ctx, f"b2s{j}", 1) for j in range(2)]
        w_hi = [sb(ctx, f"w_hi{j}", 2 * F0, dt=F32R) for j in range(2)]
        w_lo = [sb(ctx, f"w_lo{j}", 2 * F0, dt=F32R) for j in range(2)]
        wg_hi = sb(ctx, "wg_hi", E0, dt=F32R)
        wg_lo = sb(ctx, "wg_lo", E0, dt=F32R)
        m1 = sb(ctx, "m1", E1, RAW1)
        idle = sb(ctx, "idle", 512, dt=BF16)
        spare = sb(ctx, "spare", 4)
        s_prob = sb(ctx, "s_prob", NT, P)
        ident = cst[:, IDENT:IDENT + P]

        with ExitStack() as tok:
            x_in = sb(tok, "x_in", 2, KT, HALF)
            tw = sb(tok, "tw", 4, KT, P)
            outer = sb(tok, "outer", 2, KT, P)
            wn = sb(tok, "wn", 2, KT, P)
            bn = sb(tok, "bn", 2)
            gate = sb(tok, "gate", 2, HALF)
            u = sb(tok, "u", 2, HALF)
            softplus = sb(tok, "softplus", 2, HALF)
            inner = sb(tok, "inner", 2, HALF)
            mixed = sb(tok, "mixed", 2, HALF)

        with ExitStack() as att:
            k_emb = sb(att, "k_emb", NP, B + 1, L)
            v_sb = sb(att, "v_sb", NT, HEADS * HD)
            score = sb(att, "score", NS, NP, 2, L)
            probs_t = sb(att, "probs_t", 2, NP, P)
            heads_t = sb(att, "heads_t", 3, NP, P)
            q_block = sb(att, "q_block", NP, B, 2, L)
            qw_hi = sb(att, "qw_hi", 3 * HEADS * HD, dt=F32R)
            qw_lo = sb(att, "qw_lo", 3 * HEADS * HD, dt=F32R)
            qw = sb(att, "qw", 3 * HEADS * HD)
            pw = sb(att, "pw", HEADS * HD)
            pos_sb = sb(att, "pos_sb", NREL, 2, L, NP)
            rel_sb = sb(att, "rel_sb", NREL, 2, L, NP)
            pads = sb(att, "pads", 2, L * NP)
            srow = sb(att, "srow", 3, NT, 8)

        u1_hi = sb(ctx, "u1_hi", E1, F1, dt=F32R)
        u1_lo = sb(ctx, "u1_lo", E1, F1, dt=F32R)

        with ExitStack() as mix:
            hid_hi = sb(mix, "hid_hi", 2, FT, HALF, dt=F32R)
            hid_lo = sb(mix, "hid_lo", 2, FT, HALF, dt=F32R)
            hid = sb(mix, "hid", FT, HALF)
            comb_bc = [sb(mix, f"comb_bc{j}", TOK) for j in range(2)]
            scaled = sb(mix, "scaled", 2, HALF)
            acc = sb(mix, "acc", 2, HALF)
            rt = sb(mix, "rt", 12, NT * E0)
            comb_t = sb(mix, "comb_t", P)

        with ExitStack() as sec:
            s_shift = sb(sec, "s_shift", NT, L)
            s_pt = sb(sec, "s_pt", NT, P)
            s_row = sb(sec, "s_row", 3, NT)
            x4t = sb(sec, "x4t", NT, P)
            choice = sb(sec, "choice", 4, NT, E1)
            crow = sb(sec, "crow", 3, NT)
            st = sb(sec, "st", 6, P)
            top8 = sb(sec, "top8", 4, 8)
            xn_hi = sb(sec, "xn_hi", NT, X, dt=F32R)
            xn_lo = sb(sec, "xn_lo", NT, X, dt=F32R)
            onehot = sb(sec, "onehot", NT, E1, SLOT, dt=F32R)
            gated = sb(sec, "gated", NT, E1, SLOT)
            xg_hi = sb(sec, "xg_hi", E1, NT, SLOT, dt=F32R)
            xg_lo = sb(sec, "xg_lo", E1, NT, SLOT, dt=F32R)
            hmid = sb(sec, "hmid", 2, 2, NT * SLOT)
            y_g = sb(sec, "y_g", NT, E1, SLOT)
            y_nat = sb(sec, "y_nat", NT, 2, X)
            c_mat = sb(sec, "c_mat", NT, 2, P)

        block = ctx.enter_context(nc.Block())

        def read_rel(sp, t):
            n, k = t % NREL, t // NREL
            sp.wait_ge(S["rel_out", n], 16 * (k + 1))
            if k:
                sp.wait_ge(S["rel_added"], t - NREL + 1)
            for n2 in range(2):
                sp.dma_start(rel_sb[n2 * L:(n2 + 1) * L, n].rearrange("p b c n -> p b (c n)"),
                             bass.AP(tensor=rel_dram.tensor, offset=n * P * 1024 + n2 * L * 1024 + (L - 1) * NP,
                                     ap=[[1024 - NP, L], [512, 2], [1, 256]])).then_inc(S["rel_in", n], 16)

        @block.sync
        def _(sp):
            sp.dma_start(eps[:], tok_eps).then_inc(S["in_eps"], 16)
            sp.dma_start(tw[:, 0:2], tok_w[:, 0:2]).then_inc(S["in_tok_w0"], 16)
            sp.dma_start(x_in[:, 0], x_cols[:, 0]).then_inc(S["in_x0"], 16)
            sp.dma_start(tw[:, 2:4], tok_w[:, 2:4]).then_inc(S["in_tok_w1"], 16)
            sp.dma_start(x_in[:, 1], x_cols[:, 1]).then_inc(S["in_x1"], 16)
            sp.dma_start(cst[:], consts).then_inc(S["in_consts"], 16)
            sp.dma_start(pw[0:FREQS], pos_w).then_inc(S["in_pos"], 16)
            sp.dma_start(qw[:], qkv_w).then_inc(S["in_qkv"], 16)
            sp.dma_start(sml[:], small).then_inc(S["in_small"], 16)
            for e in range(2):
                sp.dma_start(raw[e][:], moe0[e]).then_inc(S["in_raw", e], 16)
                sp.dma_start(b1[e][:], moe0_b1[e]).then_inc(S["in_b1", e], 16)
                sp.dma_start(b2s[e][:], moe0_b2[e]).then_inc(S["in_b2", e], 16)
            sp.wait_ge(S["pads_made"], 1)
            for n in range(NREL):
                sp.dma_start(bass.AP(tensor=rel_dram.tensor, offset=n * P * 1024 + 256, ap=[[1024, P], [512, 2], [1, 256]]),
                             pads[:]).then_inc(S["pads_out"], 16)
            sp.dma_start(m1[:], moe1).then_inc(S["in_moe1"], 16)
            sp.wait_ge(S["pads_out"], 16 * NREL)

            def write_rel(t):
                n, k = t % NREL, t // NREL
                sp.wait_ge(S["pos_ready"], t + 1)
                if k:
                    sp.wait_ge(S["rel_in", n], 32 * k)
                sp.dma_start(bass.AP(tensor=rel_dram.tensor, offset=n * P * 1024, ap=[[1024, P], [512, 2], [1, 256]]),
                             pos_sb[:, n].rearrange("p b c n -> p b (c n)")).then_inc(S["rel_out", n], 16)

            for t in range(2):
                write_rel(t)
            for t in range(2):
                read_rel(sp, t)
            for t in range(2, NREL):
                write_rel(t)
                read_rel(sp, t)
            for t in range(NREL, NT):
                write_rel(t)
                if t > NREL:
                    read_rel(sp, t - 1)
            read_rel(sp, NT - 1)

            for e in (2, 3):
                sp.wait_ge(S["w_lo"], e - 1)
                sp.dma_start(raw[e % 2][:], moe0[e]).then_inc(S["in_raw", e % 2], 16)
            sp.wait_ge(S["combT"], 1)
            sp.dma_start(comb_dram, comb_t[0:NT * E0]).then_inc(S["comb_out"], 16)
            sp.wait_ge(S["comb_out"], 16)
            for e in range(E0):
                if e >= 2:
                    sp.wait_ge(S["silu"], 8 * (e - 1))
                    sp.dma_start(b1[e % 2][:], moe0_b1[e]).then_inc(S["in_b1", e % 2], 16)
                    if 4 <= e + 1 < E0:
                        sp.wait_ge(S["w_lo"], e)
                        sp.dma_start(raw[(e + 1) % 2][:], moe0[e + 1]).then_inc(S["in_raw", (e + 1) % 2], 16)
                    sp.wait_ge(S["y_scaled"], 2 + 2 * (e - 1))
                    sp.dma_start(b2s[e % 2][:], moe0_b2[e]).then_inc(S["in_b2", e % 2], 16)
                sp.dma_start(comb_bc[e % 2][:], bass.AP(tensor=comb_dram.tensor, offset=e * TOK, ap=[[0, P], [1, TOK]]))\
                    .then_inc(S["in_comb", e % 2], 16)

            out_v = out.rearrange("(t b) l x -> (b l) t x", b=2)
            for c in range(2):
                sp.wait_ge(S["h4_ready"], c + 1)
                sp.dma_start(out_v[:, c * TH:(c + 1) * TH], h_a[:, c * TH:(c + 1) * TH]).then_inc(S["out_done"], 16)
            sp.wait_ge(S["out_done"], 32)

        @block.gpsimd
        def _(pool):
            pool.memset(mhalf[:], -0.5).then_inc(S["half_made"], 1)

            def rstd_of(k, c):
                cols = slice(c * TH, (c + 1) * TH)
                n = 2 * k + c
                pool.wait_ge(S["ln_moments"], TH * (n + 1))
                pool.tensor_scalar(var_eps[:, k, cols], mv[:, k, cols, 1], EPS, None, ALU.add).then_inc(S["ln_eps"], 1)
                pool.wait_ge(S["ln_eps"], n + 1)
                pool.tensor_tensor(rstd[:, k, cols], var_eps[:, k, cols], mhalf[:, cols], ALU.pow).then_inc(S["ln_rstd"], 1)

            pool.wait_ge(S["half_made"], 1)
            for n2 in range(2):
                rows = slice(n2 * L, (n2 + 1) * L)
                if n2:
                    pool.wait_ge(S["block_zeros"], 1)
                pool.memset(q_block[rows, :, :, 1 - n2, :].rearrange("p n b i -> p (n b) i"), 0.0).then_inc(S["block_zeros"], 1)
            pool.wait_ge(S["block_zeros"], 2)
            pool.wait_ge(S["in_consts"], 16)
            pool.wait_ge(S["in_small"], 16)
            pool.tensor_tensor(pe_b3[:], cst[:, PE_:PE_ + X], sml[:, B3:B3 + X], ALU.add).then_inc(S["pe_bias"], 1)
            pool.wait_ge(S["qkv_w_hi"], 1)
            pool.tensor_tensor(qw_lo[:], qw[:], qw_hi[:].bitcast(F32), ALU.subtract).then_inc(S["qkv_w_lo"], 1)
            for c in range(2):
                rstd_of(0, c)
            pool.memset(s_prob[:], 0.0).then_inc(S["zeros_made"], 1)
            pool.wait_ge(S["h_ready"], 2)
            for t in range(NT):
                pool.tensor_tensor(h_b[:, t], h_a[:, t], sml[:, OB:OB + X], ALU.add).then_inc(S["out_bias"], 1)

            def low_weights(e, j):
                pool.wait_ge(S["w_hi"], e + 1)
                pool.tensor_tensor(w_lo[j][:], raw[j][:], w_hi[j][:].bitcast(F32), ALU.subtract)\
                    .then_inc(S["w_lo"], 1)

            for e in range(2):
                low_weights(e, e)

            for t in range(NT):
                a = score[:, t % NS].rearrange("p n b j -> p (n b) j")
                if t == 7:
                    rstd_of(1, 0)
                pool.wait_ge(S["prob_rsum"], t + 1)
                pool.tensor_tensor(a, a, srow[:, 2, t].unsqueeze(2).broadcast_to([P, 8, L]), ALU.mult)\
                    .then_inc(S["normed"], 1)
            rstd_of(1, 1)

            def accumulate(e, c):
                pool.wait_ge(S["y_scaled"], 2 + 2 * e + c + 1)
                pool.wait_ge(S["acc"], 2 + 2 * e + c)
                pool.tensor_tensor(acc[:, c], acc[:, c], scaled[:, c], ALU.add).then_inc(S["acc"], 1)

            pool.wait_ge(S["acc_start"], 2)
            pool.nop().then_inc(S["acc"], 2)
            with pool.Fori(0, 3) as i:
                for j in (1, 0):
                    low_weights(2 * i + (3 - j), 1 - j)
                    for c in range(2):
                        accumulate(2 * i + (1 - j), c)
            for c in range(2):
                accumulate(6, c)
            accumulate(7, 0)
            for c in range(2):
                rstd_of(2, c)
            pool.wait_ge(S["u1_hi"], 1)
            pool.tensor_tensor(u1_lo[:], m1[:, :, 0:F1], u1_hi[:].bitcast(F32), ALU.subtract).then_inc(S["u1_lo"], 1)
            for c in range(2):
                rstd_of(3, c)
            for c in range(2):
                tiles = slice(c * TH, (c + 1) * TH)
                pool.wait_ge(S["xn_hi"], c + 1)
                pool.tensor_tensor(xn_lo[:, tiles], xn[:, tiles], xn_hi[:, tiles].bitcast(F32), ALU.subtract)\
                    .then_inc(S["xn_lo"], 1)
            for g in range(4):
                pool.wait_ge(S["onehot"], g + 1)
                pool.tensor_tensor(gated[:, 2 * g:2 * g + 2].rearrange("p t e s -> p (t e) s"),
                                   onehot[:, 2 * g:2 * g + 2].rearrange("p t e s -> p (t e) s").bitcast(F32),
                                   choice[:, 2, 2 * g:2 * g + 2].rearrange("p t e -> p (t e)").unsqueeze(2)
                                   .broadcast_to([P, 2 * E1, SLOT]), ALU.mult).then_inc(S["gated"], 1)

        @block.scalar
        def _(act):
            act.wait_ge(S["eps_abs"], 1)
            act.activation(eps_f[:, 2], eps_f[:, 0], ACT.Sqrt).then_inc(S["eps_sqrt"], 1)
            act.wait_ge(S["in_eps"], 16)
            act.activation(eps_f[:, 1], eps[:, 0:BIAS], ACT.Sign).then_inc(S["eps_sign"], 1)

            act.wait_ge(S["half_made"], 1)
            act.activation(spare[:, 3:4], mhalf[:, 0:1], ACT.Exp).then_inc(S["table"], 1)
            act.wait_ge(S["noisy_b"], 1)
            for c in range(2):
                act.wait_ge(S["gate_full"], c + 1)
                act.activation(u[:, c], bank[2 * c][:], ACT.Exp, bias=bn[:, 0:1]).then_inc(S["gate_exp"], 1)
            for c in range(2):
                act.wait_ge(S["gate_cap"], c + 1)
                act.activation(softplus[:, c], u[:, c], ACT.Ln, bias=1.0, scale=0.5).then_inc(S["gate_log"], 1)
            for c in range(2):
                act.wait_ge(S["gate_sum"], c + 1)
                act.activation(u[:, c], softplus[:, c], ACT.Sigmoid).then_inc(S["gate_sigmoid"], 1)

            def turned_hi(n, b, cols):
                act.wait_ge(S["turned"], n + 1)
                act.activation(xt_hi[:, cols], bank[b][:], ACT.Copy).then_inc(S["xt_hi"], 1)

            def copy_qk(c):
                for np_ in range(NP):
                    n = 12 * c + np_
                    act.wait_ge(S["qkv_full"], n + 1)
                    act.activation(q_block[0:L, np_, c * 8:(c + 1) * 8, 0, :],
                                   bank[qkv_bank(n)][0:L].rearrange("p (b i) -> p b i", b=8), ACT.Identity,
                                   bias=sml[0:L, QB + np_:QB + np_ + 1]).then_inc(S["q_even"], 1)
                if c:
                    copy_scores(2)
                for np_ in range(NP):
                    n = 12 * c + NP + np_
                    act.wait_ge(S["qkv_full"], n + 1)
                    act.activation(k_emb[:, np_, c * 8:(c + 1) * 8].rearrange("p b i -> p (b i)"), bank[qkv_bank(n)][:], ACT.Copy)\
                        .then_inc(S["k_ready"], 1)

            def copy_scores(t):
                both = banks[:, 2 * (t % 2):2 * (t % 2) + 2].rearrange("p h (m s j) -> p (h m) s j", m=4, s=2)
                act.wait_ge(S["scores_full"], t + 1)
                if t >= NREL:
                    act.wait_ge(S["rel_out", t % NREL], 16 * (t // NREL))
                act.activation(pos_sb[:, t % NREL].rearrange("p b c n -> p n b c"),
                               both[:, :, 1].rearrange("p (n b) c -> p n b c", n=NP), ACT.Copy).then_inc(S["pos_ready"], 1)
                if t >= NS:
                    act.wait_ge(S["probs_turned"], t - NS + 1)
                act.activation(score[:, t % NS].rearrange("p n b j -> p (n b) j"), both[:, :, 0], ACT.Copy)\
                    .then_inc(S["qk_ready"], 1)

            def exps(t):
                act.wait_ge(S["shifted"], t + 1)
                a = score[:, t % NS].rearrange("p n b j -> p (n b j)")
                act.activation(a, a, ACT.Exp, scale=HD ** -0.5).then_inc(S["probs"], 1)

            for c in range(2):
                act.wait_ge(S["ln_stats"], (c + 1) * TH)
                act.activation(h_a[:, c * TH:(c + 1) * TH].rearrange("p t x -> p (t x)"), bank[5 + c][:], ACT.Copy)\
                    .then_inc(S["h_ready"], 1)
            turned_hi(0, 7, slice(0, HALF))
            copy_qk(0)
            act.wait_ge(S["in_small"], 16)
            act.activation(wg_hi[:], sml[:, WG0:WG0 + E0], ACT.Copy).then_inc(S["gate_w_hi"], 1)
            for e in range(2):
                act.wait_ge(S["in_raw", e], 16)
                act.activation(w_hi[e][:], raw[e][:], ACT.Copy).then_inc(S["w_hi"], 1)
            turned_hi(1, 4, slice(HALF, TOK))
            for t in range(2):
                copy_scores(t)
            copy_qk(1)
            exps(0)
            copy_scores(3)
            for t in range(2):
                act.wait_ge(S["qkv_full"], 12 + 2 * NP + t + 1)
                act.activation(v_sb[:, TH + t], bank[qkv_bank(12 + 2 * NP + t)][:], ACT.Copy).then_inc(S["v_ready_act"], 1)
            for t in range(NT + 1):
                if t >= 1:
                    act.wait_ge(S["probs_turned"], t)
                    if t >= 3:
                        act.wait_ge(S["heads_full"], t - 2)
                    act.activation(probs_t[:, (t - 1) % 2].rearrange("p n j -> p (n j)"), bank[4][:], ACT.Copy)\
                        .then_inc(S["probs_t"], 1)
                if t == NT - 1:
                    act.activation(spare[:, 2:3], mhalf[:, 0:1], ACT.Silu).then_inc(S["table"], 1)
                if t + 1 < NT:
                    exps(t + 1)
                if t + NREL < NT:
                    copy_scores(t + NREL)
                if t == NT:
                    turned_hi(2, 2, slice(0, HALF))
                if t >= 1:
                    act.wait_ge(S["heads_full"], t)
                    if t >= 4:
                        act.wait_ge(S["mixed_full"], t - 3)
                    for b2 in range(2):
                        act.activation(heads_t[:, (t - 1) % 3, :, b2 * L:(b2 + 1) * L],
                                       bank[5 + b2][:, 0:NP * L].rearrange("p (n i) -> p n i", n=NP), ACT.Copy)\
                            .then_inc(S["heads_t"], 1)

            def silus(e, c, j, first=False):
                if c == 0:
                    act.wait_ge(S["in_b1", j], 8 * (e - j) + 16)
                for ft in range(FT):
                    n = 8 * e + 4 * c + ft
                    act.wait_ge(S["p1_full"], n + 1)
                    if not first:
                        act.wait_ge(S["h_lo"], n - 3)
                    act.activation(hid[:, ft], bank[ft][:], ACT.Silu, bias=b1[j][:, ft:ft + 1]).then_inc(S["silu"], 1)

            def high_weights(e, j):
                act.wait_ge(S["in_raw", j], 8 * (e - j) + 16)
                act.wait_ge(S["y_full"], 2 * e)
                act.activation(w_hi[j][:], raw[j][:], ACT.Copy).then_inc(S["w_hi"], 1)

            act.wait_ge(S["mixed_full"], NT)
            silus(0, 0, 0, first=True)
            turned_hi(3, 7, slice(HALF, TOK))
            for c in range(2):
                act.wait_ge(S["h1_turned"], c + 1)
                act.activation(acc[:, c], bank[5 + c][:], ACT.Copy).then_inc(S["acc_start"], 1)
            silus(0, 1, 0)
            act.wait_ge(S["router"], 1)
            act.activation(rt[:, 9, 0:NT], rt[:, 8, 0:NT], ACT.Tanh, scale=0.5).then_inc(S["router"], 1)
            act.wait_ge(S["combT_full"], 1)
            act.activation(comb_t[0:NT * E0], bank[5][0:NT * E0, 0:P], ACT.Copy).then_inc(S["combT"], 1)
            silus(1, 0, 1)
            with act.Fori(0, 3) as i:
                for j in (1, 0):
                    high_weights(2 * i + (3 - j), 1 - j)
                    silus(2 * i + (2 - j), 1, j)
                    silus(2 * i + (3 - j), 0, 1 - j)
            silus(7, 1, 1)

            act.activation(spare[:, 0:1], mhalf[:, 0:1], ACT.Exp).then_inc(S["table"], 1)
            act.wait_ge(S["in_moe1"], 16)
            act.activation(u1_hi[:], m1[:, :, 0:F1], ACT.Copy).then_inc(S["u1_hi"], 1)

            def copy_turned(n, b, c):
                act.wait_ge(S["turned"], n + 1)
                act.activation(x4t[:, c * TH:(c + 1) * TH].rearrange("p t j -> p (t j)"), bank[b][:], ACT.Copy)\
                    .then_inc(S["x4t"], 1)

            for c in range(2):
                act.wait_ge(S["ln_stats"], 2 * NT + (c + 1) * TH)
                act.activation(h_a[:, c * TH:(c + 1) * TH].rearrange("p t x -> p (t x)"), bank[4 + c][:], ACT.Copy)\
                    .then_inc(S["h2_ready"], 1)
            for c in range(2):
                copy_turned(4 + c, 6 + c, c)
            act.wait_ge(S["zeros_made"], 1)
            for c in range(2):
                tiles = slice(c * TH, (c + 1) * TH)
                act.wait_ge(S["self_shift"], c + 1)
                for b2 in range(2):
                    rows = slice(b2 * L, (b2 + 1) * L)
                    act.activation(s_prob[rows, tiles, b2 * L:(b2 + 1) * L], s_shift[rows, tiles], ACT.Exp)\
                        .then_inc(S["self_probs"], 1)
            for c in range(2):
                act.wait_ge(S["self_turned"], c + 1)
                act.activation(s_pt[:, c * TH:(c + 1) * TH].rearrange("p t j -> p (t j)"), bank[2 + c][:], ACT.Copy)\
                    .then_inc(S["self_pt"], 1)

            for c in range(2):
                copy_turned(6 + c, c, c)

            def high_tokens(c):
                tiles = slice(c * TH, (c + 1) * TH)
                act.wait_ge(S["ln_out"], 3 * NT + (c + 1) * TH)
                act.activation(xn_hi[:, tiles], xn[:, tiles], ACT.Copy).then_inc(S["xn_hi"], 1)

            high_tokens(0)
            act.wait_ge(S["choice"], 1)
            act.activation(choice[:, 1], choice[:, 0], ACT.Exp).then_inc(S["choice"], 1)
            high_tokens(1)
            act.wait_ge(S["choice_turned"], 1)
            act.activation(st[0:NT * E1, 0], bank[3][0:NT * E1, 0:P], ACT.Copy).then_inc(S["choice_t"], 1)
            act.activation(spare[:, 1:2], mhalf[:, 0:1], ACT.Gelu).then_inc(S["table"], 1)
            for g in range(4):
                act.wait_ge(S["gather_full"], g + 1)
                act.activation(xg_hi[:, :, 2 * g:2 * g + 2].rearrange("p e t s -> p t e s"),
                               bank[4 + g][:].rearrange("p (t e s) -> p t e s", t=2, e=E1), ACT.Copy)\
                    .then_inc(S["xg_hi"], 1)

            def copy_y(eg):
                act.wait_ge(S["y_turned"], 2 * eg + 1)
                act.activation(y_nat[:, 0:TH, eg], bank[6][:].rearrange("p (t x) -> p t x", t=TH), ACT.Copy)\
                    .then_inc(S["y_ready0"], 1)

            for e in range(E1):
                act.wait_ge(S["e1_full"], e + 1)
                if e >= 2:
                    act.wait_ge(S["e1_y_full"], e - 1)
                for ft in range(2):
                    act.activation(hmid[:, e % 2, ft], bank[e % 2][:, ft * NT * SLOT:(ft + 1) * NT * SLOT], ACT.Gelu,
                                   bias=m1[:, e, RAW1 - 3 + ft:RAW1 - 2 + ft]).then_inc(S["gelu"], 1)
                if e == 5:
                    copy_y(0)
            copy_y(1)

        @block.tensor
        def _(pe):
            mm = pe.matmul

            def three(out_, l_hi, l_lo, r_hi, r_lo, start=True, stop=True):
                mm(out_, l_hi, r_hi, start=start, stop=False)
                mm(out_, l_hi, r_lo, start=False, stop=False)
                return mm(out_, l_lo, r_hi, start=False, stop=stop)

            def turn(k, c, b, src):
                for t in range(TH):
                    pe.wait_ge(S["ln_out"], (2 * k + c) * TH + t + 1)
                    last = pe.transpose(bank[b][:, t * P:(t + 1) * P], src[:, c * TH + t], ident)
                last.then_inc(S["turned"], 1)

            def keep_busy(n, b):
                for _ in range(n):
                    mm(bank[b][:], idle[:, 0:P], idle[:], start=True, stop=True)

            pe.wait_ge(S["idle_made"], 1)
            keep_busy(10, 7)
            for layer, full in ((0, "gate_full"), (1, "inner_full")):
                pe.wait_ge(S["noisy_w"], layer + 1)
                for c in range(2):
                    pe.wait_ge(S["in_x0"] if c == 0 else S["in_x1"], 16)
                    for kt in range(KT):
                        last = mm(bank[2 * c + layer][:], wn[:, layer, kt], x_in[:, c, kt], start=kt == 0, stop=kt == KT - 1)
                    last.then_inc(S[full], 1)
            pe.wait_ge(S["in_pos"], 16)
            pe.wait_ge(S["in_consts"], 16)
            for np_ in range(NP):
                last = mm(bank[4][:, np_ * L:(np_ + 1) * L], pw[0:FREQS, np_ * P:(np_ + 1) * P],
                          cst[0:FREQS, SINS:SINS + L], start=True, stop=True)
            last.then_inc(S["emb_full"], 1)
            keep_busy(3, 7)
            pe.wait_ge(S["pe_bias"], 1)
            for c in range(2):
                for t in range(TH):
                    mm(bank[5 + c][:, t * P:(t + 1) * P], ident, pe_b3[:], start=t == 0, stop=False)
            pe.wait_ge(S["in_small"], 16)
            for c in range(2):
                pe.wait_ge(S["mixed"], c + 1)
                for t in range(TH):
                    last = mm(bank[5 + c][:, t * P:(t + 1) * P], mixed[:, c, t * P:(t + 1) * P], sml[:, W3:W3 + X],
                              start=False, stop=t == TH - 1)
                last.then_inc(S["embed_full"], 1)

            def project(c):
                cols = slice(c * HALF, (c + 1) * HALF)
                pe.wait_ge(S["qkv_w_lo"], 1)
                pe.wait_ge(S["xt_lo"], c + 1)
                for m in range(12):
                    n = 12 * c + m
                    qkv_bank_free(n)
                    if m < 8:
                        w = slice(m * P, (m + 1) * P)
                        last = three(bank[qkv_bank(n)][:], qw_hi[:, w], qw_lo[:, w], xt_hi[:, cols], xt_lo[:, cols])
                    else:
                        x_ = slice(c * HALF + (m - 8) * P, c * HALF + (m - 7) * P)
                        w = slice(8 * P, 12 * P)
                        last = three(bank[qkv_bank(n)][:], xt_hi[:, x_], xt_lo[:, x_], qw_hi[:, w], qw_lo[:, w])
                    last.then_inc(S["qkv_full"], 1)
                    if c and m in (3, 7):
                        scores(2 + m // 7)

            def qkv_bank_free(n):
                if n < 12:
                    if n in (4, 5):
                        pe.wait_ge(S["h_ready"], n - 3)
                    if n >= 6:
                        wait_item(n - 6)
                else:
                    m = n - 12
                    if m in (0, 3):
                        pe.wait_ge(S["xt_lo"], 2 if m == 0 else 1)
                    elif m in (4, 5):
                        pe.wait_ge(S["pos_ready"], 2)
                        pe.wait_ge(S["qk_ready"], 2)
                    elif m in (10, 11):
                        pe.wait_ge(S["pos_ready"], 4)
                        pe.wait_ge(S["qk_ready"], 4)
                    else:
                        wait_item({1: 10, 2: 11}[m] if m < 6 else n - 6)

            def wait_item(n):
                c, m = n // 12, n % 12
                if m < 4:
                    pe.wait_ge(S["q_even"], 4 * c + m + 1)
                    pe.wait_ge(S["q_odd"], 4 * c + m + 1)
                elif m < 8:
                    pe.wait_ge(S["k_ready"], 4 * c + m - 3)
                elif c and m < 10:
                    pe.wait_ge(S["v_ready_act"], m - 7)
                else:
                    pe.wait_ge(S["v_ready"], 4 * c + m - 7 - 2 * c)

            def scores(t):
                c = t // TH
                pe.wait_ge(S["q_even"], 4 * (c + 1))
                pe.wait_ge(S["q_odd"], 4 * (c + 1))
                pe.wait_ge(S["k_ready"], 4 * (c + 1))
                if t == 0:
                    pe.wait_ge(S["emb_ready"], 1)
                    pe.wait_ge(S["block_zeros"], 2)
                for item in {0: (6, 7), 1: (8, 9), 3: (16, 17), 5: (22, 23)}.get(t, ()):
                    wait_item(item)
                if t >= 2:
                    pe.wait_ge(S["pos_ready"], t - 1)
                    pe.wait_ge(S["qk_ready"], t - 1)
                for np_ in range(NP):
                    for b2 in range(2):
                        img = 2 * t + b2
                        o = (np_ % 2 * 2 + b2) * P
                        last = mm(bank[2 * (t % 2) + np_ // 2][:, o:o + P], q_block[:, np_, img].rearrange("p n i -> p (n i)"),
                                  k_emb[:, np_, img::B - img], start=True, stop=True)
                last.then_inc(S["scores_full"], 1)

            keep_busy(10, 7)
            turn(0, 0, 7, xn)
            keep_busy(6, 0)
            project(0)
            pe.wait_ge(S["emb_ready"], 1)
            turn(0, 1, 4, xn)
            scores(0)
            scores(1)
            project(1)

            def up(e, c, j, first=False, parts=range(FT)):
                cols = slice(c * HALF, (c + 1) * HALF)
                if c == 0:
                    pe.wait_ge(S["w_lo"], e + 1)
                for ft in parts:
                    n = 8 * e + 4 * c + ft
                    if not first:
                        pe.wait_ge(S["silu"], n - 3)
                    elif ft == 2:
                        pe.wait_ge(S["xt_lo"], 3)
                    w = slice(ft * P, (ft + 1) * P)
                    three(bank[ft][:], w_hi[j][:, w], w_lo[j][:, w], xt_hi[:, cols], xt_lo[:, cols])\
                        .then_inc(S["p1_full"], 1)

            for t in range(NT + 3):
                if t == NT + 2:
                    pe.wait_ge(S["xt_lo"], 3)
                    up(0, 0, 0, first=True, parts=(0,))
                if 1 <= t <= NT:
                    pe.wait_ge(S["normed"], t)
                    if t == 1:
                        wait_item(18)
                    else:
                        pe.wait_ge(S["probs_t"], t - 1)
                    for np_ in range(NP):
                        last = pe.transpose(bank[4][:, np_ * P:(np_ + 1) * P],
                                            score[:, (t - 1) % NS, np_].rearrange("p b j -> p (b j)"), ident)
                    last.then_inc(S["probs_turned"], 1)
                if t + NREL < NT:
                    scores(t + NREL)
                if 3 <= t:
                    pe.wait_ge(S["heads_t"], 2 * (t - 2))
                    if t == 3:
                        wait_item(21)
                    else:
                        pe.wait_ge(S["h1_ready"], t - 3)
                    for np_ in range(NP):
                        last = mm(bank[7][:, 0:X], heads_t[:, (t - 3) % 3, np_], sml[:, WO + np_ * X:WO + (np_ + 1) * X],
                                  start=np_ == 0, stop=np_ == NP - 1)
                    last.then_inc(S["mixed_full"], 1)
                if t == NT:
                    pe.wait_ge(S["qk_ready"], NT)
                    turn(1, 0, 2, xn)
                if 1 <= t <= NT:
                    pe.wait_ge(S["probs_t"], t)
                    if t > TH:
                        pe.wait_ge(S["v_ready_act"], 2)
                    pe.wait_ge(S["v_ready"], 4 if t <= TH else 6)
                    if t == 1:
                        wait_item(19)
                        wait_item(20)
                    else:
                        pe.wait_ge(S["heads_t"], 2 * (t - 1))
                    for b2 in range(2):
                        keys = slice(b2 * L, (b2 + 1) * L)
                        for np_ in range(NP):
                            for n2 in range(2):
                                h = 2 * np_ + n2
                                last = mm(bank[5 + b2][n2 * L:(n2 + 1) * L, np_ * L:(np_ + 1) * L],
                                          v_sb[keys, t - 1, h * HD:(h + 1) * HD],
                                          probs_t[keys, (t - 1) % 2, np_, n2 * L:(n2 + 1) * L], start=True, stop=True)
                    last.then_inc(S["heads_full"], 1)

            def down(e, c, j, first=False):
                if first:
                    pe.wait_ge(S["acc_start"], 2)
                pe.wait_ge(S["y_scaled"], 2 * e + c + 1)
                for ft in range(FT):
                    pe.wait_ge(S["h_lo"], 8 * e + 4 * c + ft + 1)
                    w = slice(F0 + ft * X, F0 + (ft + 1) * X)
                    last = three(bank[6 + c][:], w_hi[j][:, w], w_lo[j][:, w], hid_hi[:, c, ft], hid_lo[:, c, ft],
                                 start=ft == 0, stop=ft == FT - 1)
                last.then_inc(S["y_full"], 1)

            pe.nop().then_inc(S["y_full"], 2)
            up(0, 0, 0, first=True, parts=(1, 2, 3))

            def turn_h1(c):
                pe.wait_ge(S["h1_ready"], (c + 1) * TH)
                pe.wait_ge(S["heads_t"], 2 * NT)
                for t in range(TH):
                    last = pe.transpose(bank[5 + c][:, t * P:(t + 1) * P], h_b[:, c * TH + t], ident)
                last.then_inc(S["h1_turned"], 1)

            pe.wait_ge(S["gate_w_lo"], 1)
            for t in range(NT):
                if t == TH:
                    turn_h1(0)
                    pe.wait_ge(S["h1_ready"], NT)
                    turn(1, 1, 7, xn)
                    turn_h1(1)
                    pe.wait_ge(S["silu"], 1)
                    keep_busy(5, 0)
                    pe.wait_ge(S["xt_lo"], 4)
                w = slice(t * P, (t + 1) * P)
                last = three(bank[4][:, t * E0:(t + 1) * E0], xt_hi[:, w], xt_lo[:, w], wg_hi[:], wg_lo[:])
            last.then_inc(S["router_full"], 1)
            up(0, 1, 0)
            down(0, 0, 0, first=True)
            pe.wait_ge(S["acc_start"], 1)
            pe.wait_ge(S["router"], 3)
            pe.transpose(bank[5][0:NT * E0, 0:P], rt[:, 11], ident).then_inc(S["combT_full"], 1)
            up(1, 0, 1)
            down(0, 1, 0)
            with pe.Fori(0, 3) as i:
                for j in (1, 0):
                    e = 2 * i + (2 - j)
                    up(e, 1, j)
                    down(e, 0, j)
                    up(2 * i + (3 - j), 0, 1 - j)
                    down(e, 1, j)
            up(7, 1, 1)
            down(7, 0, 1)
            down(7, 1, 1)

            def tile_of(src, t):
                return src[:, t // TH, t % TH * P:(t % TH + 1) * P]

            pe.wait_ge(S["acc"], 2 + 2 * (E0 - 1))
            for t in range(TH, NT):
                mm(bank[5][:, t % TH * P:(t % TH + 1) * P], tile_of(acc, t), ident, start=t == TH, stop=False)
            pe.wait_ge(S["acc"], 2 + 2 * (E0 - 1) + 1)
            for t in range(TH):
                last = pe.transpose(bank[4][:, t * P:(t + 1) * P], tile_of(acc, t), ident)
            last.then_inc(S["acc_turned"], 1)
            pe.wait_ge(S["y_scaled"], 2 + 2 * E0)
            for t in range(TH, NT):
                last = mm(bank[5][:, t % TH * P:(t % TH + 1) * P], tile_of(scaled, t), ident, start=False, stop=t == NT - 1)
            last.then_inc(S["acc_turned"], 1)

            x4f = x4t[:].rearrange("p t j -> p (t j)")

            def self_scores(c):
                pe.wait_ge(S["x4t"], c + 1)
                for t in range(c * TH, (c + 1) * TH):
                    for b2 in range(2):
                        img = slice((2 * t + b2) * L, (2 * t + b2 + 1) * L)
                        o = t % TH * L
                        last = mm(bank[c][b2 * L:(b2 + 1) * L, o:o + L], x4f[:, img], x4f[:, img], start=True, stop=True)
                last.then_inc(S["self_full"], 1)

            keep_busy(7, 0)
            turn(2, 0, 6, xn)
            keep_busy(2, 0)
            turn(2, 1, 7, xn)
            keep_busy(2, 0)
            self_scores(0)
            self_scores(1)
            keep_busy(3, 6)
            for c in range(2):
                pe.wait_ge(S["self_probs"], 2 * c + 2)
                for t in range(TH):
                    last = pe.transpose(bank[2 + c][:, t * P:(t + 1) * P], s_prob[:, c * TH + t], ident)
                last.then_inc(S["self_turned"], 1)
            for c in range(2):
                pe.wait_ge(S["self_pt"], c + 1)
                for t in range(TH):
                    tt = c * TH + t
                    last = mm(bank[4 + c][:, t * P:(t + 1) * P], s_pt[:, tt], xn[:, tt], start=True, stop=True)
                last.then_inc(S["self_y"], 1)

            def choose(c):
                pe.wait_ge(S["x4t"], 2 + c + 1)
                for t in range(c * TH, (c + 1) * TH):
                    last = mm(bank[2][:, t * E1:(t + 1) * E1], x4t[:, t], sml[:, WG1:WG1 + E1], start=True, stop=True)
                return last

            keep_busy(20, 6)
            turn(3, 0, 0, xn)
            keep_busy(2, 6)
            turn(3, 1, 1, xn)
            keep_busy(1, 6)
            choose(0)
            choose(1).then_inc(S["choice_full"], 1)
            keep_busy(6, 6)
            pe.wait_ge(S["choice"], 3)
            pe.transpose(bank[3][0:NT * E1, 0:P], choice[:, 2].rearrange("p t e -> p (t e)"), ident)\
                .then_inc(S["choice_turned"], 1)
            keep_busy(11, 6)
            pe.wait_ge(S["top"], 1)
            pe.transpose(bank[2][:, 0:NT * E1], st[0:NT * E1, 5], ident[0:NT * E1, 0:NT * E1]).then_inc(S["slots_turned"], 1)
            keep_busy(4, 7)
            for t in range(NT):
                pe.wait_ge(S["onehot"], 1 + t // 2)
                pe.wait_ge(S["xn_lo"], 1 + t // TH)
                for part in (xn_hi, xn_lo):
                    last = mm(bank[4 + t // 2][:, (t % 2) * 256:(t % 2 + 1) * 256], part[:, t],
                              onehot[:, t].rearrange("p e s -> p (e s)"), start=part is xn_hi, stop=part is xn_lo)
                if t % 2:
                    last.then_inc(S["gather_full"], 1)

            def turn_gates(g):
                pe.wait_ge(S["gated"], g + 1)
                pe.wait_ge(S["onehot"], 4)
                if g >= 2:
                    pe.wait_ge(S["c_ready"], g - 1)
                for k in range(4):
                    t, eg = 2 * g + k // 2, k % 2
                    last = pe.transpose(bank[2 + g % 2][:, k * P:(k + 1) * P],
                                        gated[:, t, eg * 4:(eg + 1) * 4].rearrange("p e s -> p (e s)"), ident)
                last.then_inc(S["c_turned"], 1)

            def up1(e):
                if e >= 2:
                    pe.wait_ge(S["gelu"], 2 * e - 2)
                for ft in range(2):
                    w = slice(ft * P, (ft + 1) * P)
                    last = three(bank[e % 2][:, ft * NT * SLOT:(ft + 1) * NT * SLOT], u1_hi[:, e, w], u1_lo[:, e, w],
                                 xg_hi[:, e].rearrange("p t s -> p (t s)"), xg_lo[:, e].rearrange("p t s -> p (t s)"))
                last.then_inc(S["e1_full"], 1)

            def down1(e):
                pe.wait_ge(S["gelu"], 2 * e + 2)
                if e >= 2:
                    pe.wait_ge(S["e1_y"], e - 1)
                for ft in range(2):
                    last = mm(bank[4 + e % 2][:, 0:NT * SLOT], m1[:, e, F1 + ft * X:F1 + (ft + 1) * X],
                              hmid[:, e % 2, ft], start=ft == 0, stop=ft == 1)
                last.then_inc(S["e1_y_full"], 1)

            def turn_y(eg):
                pe.wait_ge(S["e1_y"], 4 * (eg + 1))
                for c in range(2):
                    if eg:
                        pe.wait_ge(S["y_ready0"] if c == 0 else S["y_ready1"], 1)
                    for t in range(TH):
                        last = pe.transpose(bank[6 + c][:, t * P:(t + 1) * P],
                                            y_g[:, c * TH + t, eg * 4:(eg + 1) * 4].rearrange("p e s -> p (e s)"), ident)
                    last.then_inc(S["y_turned"], 1)

            def combine(eg, c):
                pe.wait_ge(S["y_ready0"] if c == 0 else S["y_ready1"], eg + 1)
                pe.wait_ge(S["c_ready"], 4)
                for t in range(TH):
                    tt = c * TH + t
                    last = mm(bank[2 + c][:, t * P:(t + 1) * P], c_mat[:, tt, eg], y_nat[:, tt, eg],
                              start=eg == 0 and t == 0, stop=eg == 1 and t == TH - 1)
                return last

            turn_gates(0)
            turn_gates(1)
            pe.wait_ge(S["u1_lo"], 1)
            pe.wait_ge(S["xg_lo"], 4)
            up1(0)
            for e in range(E1):
                if e + 1 < E1:
                    up1(e + 1)
                if e < 2:
                    turn_gates(2 + e)
                down1(e)
                if e == 4:
                    turn_y(0)
                if e in (5, 6):
                    combine(0, e - 5)
            keep_busy(2, 0)
            turn_y(1)
            for c in range(2):
                combine(1, c).then_inc(S["h4_full"], 1)

        @block.vector
        def _(dve):
            steps = [0]

            def link(ins):
                steps[0] += 1
                ins.then_inc(S["dve_step"], 1)
                dve.wait_ge(S["dve_step"], steps[0])

            dve.memset(idle[:], 0.0).then_inc(S["idle_made"], 1)
            dve.memset(pads[:], MASKED).then_inc(S["pads_made"], 1)
            dve.wait_ge(S["in_eps"], 16)
            dve.scalar_tensor_tensor(out=eps_f[:, 0], in0=eps[:, 0:BIAS], scalar=-1.0, in1=eps[:, 0:BIAS], op0=ALU.mult, op1=ALU.max)\
               .then_inc(S["eps_abs"], 1)

            dve.wait_ge(S["eps_sign"], 1)
            dve.wait_ge(S["eps_sqrt"], 1)
            dve.tensor_tensor(eps_f[:, 0], eps_f[:, 1], eps_f[:, 2], ALU.mult).then_inc(S["eps_root"], 1)
            dve.wait_ge(S["eps_root"], 1)
            for layer in range(2):
                dve.wait_ge(S["in_tok_w0"] if layer == 0 else S["in_tok_w1"], 16)
                for kt in range(KT):
                    ei = EI + 2 * layer + kt
                    dve.scalar_tensor_tensor(out=outer[:, layer, kt], in0=tw[:, 2 * layer + 1, kt],
                                             scalar=eps_f[:, 0, ei:ei + 1], in1=eps_f[:, 0, layer * P:(layer + 1) * P],
                                             op0=ALU.mult, op1=ALU.mult).then_inc(S["noise_outer"], 1)
                b = BIAS + 2 * layer
                dve.scalar_tensor_tensor(out=bn[:, layer:layer + 1], in0=eps[:, b + 1:b + 2],
                                         scalar=eps_f[:, 0, EOC + layer:EOC + layer + 1], in1=eps[:, b:b + 1],
                                         op0=ALU.mult, op1=ALU.add).then_inc(S["noisy_b"], 1)
                dve.wait_ge(S["noise_outer"], 2 * layer + 2)
                dve.tensor_tensor(wn[:, layer], tw[:, 2 * layer], outer[:, layer], ALU.add).then_inc(S["noisy_w"], 1)

            for c in range(2):
                dve.wait_ge(S["gate_exp"], c + 1)
                dve.tensor_scalar(u[:, c], u[:, c], E_CAP, None, ALU.min).then_inc(S["gate_cap"], 1)
                dve.wait_ge(S["noisy_b"], 1)
                dve.wait_ge(S["gate_full"], c + 1)
                dve.tensor_scalar(gate[:, c], bank[2 * c][:], bn[:, 0:1], None, ALU.add).then_inc(S["gate"], 1)

            def gated_inner(c):
                dve.wait_ge(S["gate"], c + 1)
                dve.wait_ge(S["inner_full"], c + 1)
                dve.scalar_tensor_tensor(out=inner[:, c], in0=bank[2 * c + 1][:], scalar=bn[:, 1:2], in1=gate[:, c],
                                         op0=ALU.add, op1=ALU.mult).then_inc(S["gated_inner"], 1)

            dve.wait_ge(S["noisy_b"], 2)
            gated_inner(0)
            for c in range(2):
                dve.wait_ge(S["gate_log"], c + 1)
                dve.wait_ge(S["gate"], c + 1)
                dve.tensor_tensor(softplus[:, c], softplus[:, c], gate[:, c], ALU.add).then_inc(S["gate_sum"], 1)
            gated_inner(1)
            dve.wait_ge(S["in_qkv"], 16)
            dve.tensor_copy(qw_hi[:], qw[:]).then_inc(S["qkv_w_hi"], 1)
            for c in range(2):
                dve.wait_ge(S["gate_sigmoid"], c + 1)
                dve.wait_ge(S["gated_inner"], c + 1)
                dve.tensor_tensor(mixed[:, c], inner[:, c], u[:, c], ALU.mult).then_inc(S["mixed"], 1)
            dve.wait_ge(S["gate_sum"], 2)
            dve.wait_ge(S["emb_full"], 1)
            dve.tensor_copy(k_emb[:, :, B], bank[4][:, 0:NP * L].rearrange("p (n v) -> p n v", n=NP)).then_inc(S["emb_ready"], 1)

            def norm_stats(k, src, t):
                dve.bn_stats(stats[:, k, t], src[:, t]).then_inc(S["ln_stats"], 1)

            def norm_moment(k, t):
                dve.wait_ge(S["ln_stats"], k * NT + t + 1)
                dve.bn_aggr(mv[:, k, t], stats[:, k, t]).then_inc(S["ln_moments"], 1)

            def norm_moments(k, c):
                for t in range(c * TH, (c + 1) * TH):
                    norm_moment(k, t)

            def norm_apply(k, c, src):
                dve.wait_ge(S["ln_rstd"], 2 * k + c + 1)
                for t in range(c * TH, (c + 1) * TH):
                    dve.tensor_scalar(xn[:, t], src[:, t], mv[:, k, t, 0:1], rstd[:, k, t:t + 1], ALU.subtract, ALU.mult)\
                        .then_inc(S["ln_out"], 1)

            def turned_lo(n, b, cols):
                dve.wait_ge(S["xt_hi"], n + 1)
                dve.tensor_tensor(xt_lo[:, cols], bank[b][:], xt_hi[:, cols].bitcast(F32), ALU.subtract)\
                    .then_inc(S["xt_lo"], 1)

            for c in range(2):
                dve.wait_ge(S["embed_full"], c + 1)
                for t in range(TH):
                    dve.bn_stats(stats[:, 0, c * TH + t], bank[5 + c][:, t * X:(t + 1) * X]).then_inc(S["ln_stats"], 1)
                norm_moments(0, c)
            for c in range(2):
                dve.wait_ge(S["h_ready"], c + 1)
                norm_apply(0, c, h_a)

            def probs_of(t):
                return score[:, t % NS].rearrange("p n b j -> p (n b) j")

            def add_rel(t):
                dve.wait_ge(S["qk_ready"], t + 1)
                dve.wait_ge(S["rel_in", t % NREL], 32 * (t // NREL + 1))
                dve.tensor_tensor(score[:, t % NS], score[:, t % NS], rel_sb[:, t % NREL].rearrange("p b j n -> p n b j"),
                                  ALU.add).then_inc(S["rel_added"], 1)

            def row_max(t):
                dve.wait_ge(S["rel_added"], t + 1)
                dve.reduce_max(srow[:, 0, t], probs_of(t), AX.X).then_inc(S["row_max"], 1)

            def shift(t):
                dve.wait_ge(S["row_max"], t + 1)
                dve.tensor_tensor(probs_of(t), probs_of(t), srow[:, 0, t].unsqueeze(2).broadcast_to([P, 8, L]), ALU.subtract)\
                    .then_inc(S["shifted"], 1)

            def row_sum(t):
                dve.wait_ge(S["probs"], t + 1)
                dve.reduce_sum(srow[:, 1, t], probs_of(t), AX.X).then_inc(S["prob_sum"], 1)

            def row_recip(t):
                dve.wait_ge(S["prob_sum"], t + 1)
                dve.reciprocal(srow[:, 2, t], srow[:, 1, t]).then_inc(S["prob_rsum"], 1)

            def q_odd(c):
                for np_ in range(NP):
                    n = 12 * c + np_
                    dve.wait_ge(S["qkv_full"], n + 1)
                    dve.tensor_scalar(q_block[L:P, np_, c * 8:(c + 1) * 8, 1, :],
                                      bank[qkv_bank(n)][L:P].rearrange("p (b i) -> p b i", b=8),
                                      sml[L:P, QB + np_:QB + np_ + 1], None, ALU.add).then_inc(S["q_odd"], 1)

            def copy_v(c):
                for t in range(2 * c, TH):
                    n = 12 * c + 2 * NP + t
                    dve.wait_ge(S["qkv_full"], n + 1)
                    dve.tensor_copy(v_sb[:, c * TH + t], bank[qkv_bank(n)][:]).then_inc(S["v_ready"], 1)

            turned_lo(0, 7, slice(0, HALF))
            q_odd(0)
            copy_v(0)
            turned_lo(1, 4, slice(HALF, TOK))
            q_odd(1)
            for t in range(2):
                add_rel(t)
                row_max(t)
                shift(t)
            row_sum(0)
            row_recip(0)
            copy_v(1)
            dve.wait_ge(S["gate_w_hi"], 1)
            dve.tensor_tensor(wg_lo[:], sml[:, WG0:WG0 + E0], wg_hi[:].bitcast(F32), ALU.subtract).then_inc(S["gate_w_lo"], 1)

            dve.wait_ge(S["out_bias"], NT)
            for t in range(NT + 3):
                if 2 <= t + 1 < NT:
                    add_rel(t + 1)
                if 1 <= t < NT:
                    row_sum(t)
                if 2 <= t + 1 < NT:
                    row_max(t + 1)
                if 1 <= t < NT:
                    row_recip(t)
                if 2 <= t + 1 < NT:
                    shift(t + 1)
                if t >= 3:
                    dve.wait_ge(S["mixed_full"], t - 2)
                    dve.tensor_tensor(h_b[:, t - 3], bank[7][:, 0:X], h_b[:, t - 3], ALU.add).then_inc(S["h1_ready"], 1)
                    dve.wait_ge(S["h1_ready"], t - 2)
                    norm_stats(1, h_b, t - 3)
                    norm_moment(1, t - 3)
                if t == NT - 1:
                    norm_apply(1, 0, h_b)
                if t == NT:
                    turned_lo(2, 2, slice(0, HALF))
            norm_apply(1, 1, h_b)

            def splits(e, c, steps=range(FT + 1)):
                dve.wait_ge(S["y_full"], 2 * e + c + 1)
                for ft in steps:
                    n = 8 * e + 4 * c + ft
                    if ft < FT:
                        dve.wait_ge(S["silu"], n + 1)
                        dve.tensor_copy(hid_hi[:, c, ft], hid[:, ft]).then_inc(S["h_hi"], 1)
                    if ft:
                        dve.wait_ge(S["h_hi"], n)
                        dve.tensor_tensor(hid_lo[:, c, ft - 1], hid[:, ft - 1], hid_hi[:, c, ft - 1].bitcast(F32),
                                          ALU.subtract).then_inc(S["h_lo"], 1)

            dve.nop().then_inc(S["y_scaled"], 2)
            splits(0, 0, range(0, 2))
            turned_lo(3, 7, slice(HALF, TOK))
            splits(0, 0, range(2, FT + 1))

            lg = [rt[:, k].rearrange("p (e t) -> p t e", t=NT) for k in range(12)]
            row = [rt[:, k, 0:NT] for k in range(12)]

            def bc(v):
                return v.unsqueeze(2).broadcast_to([P, NT, E0])

            dve.wait_ge(S["router_full"], 1)
            link(dve.tensor_tensor(lg[0], bank[4][:, 0:NT * E0].rearrange("p (t e) -> p t e", t=NT),
                                           sml[:, BG:BG + E0].unsqueeze(1).broadcast_to([P, NT, E0]), ALU.add))
            rev = cst[:, REV:REV + E0].unsqueeze(1).broadcast_to([P, NT, E0])
            for k, (src, one, top) in enumerate(((0, 2, 6), (3, 4, 7))):
                link(dve.reduce_max(row[top], lg[src], AX.X))
                link(dve.tensor_tensor(lg[1], lg[src], bc(row[top]), ALU.is_equal))
                link(dve.tensor_tensor(lg[1], lg[1], rev, ALU.mult))
                link(dve.reduce_max(row[5], lg[1], AX.X))
                link(dve.tensor_tensor(lg[one], bc(row[5]), rev, ALU.is_equal))
                if k == 0:
                    link(dve.scalar_tensor_tensor(out=rt[:, 3], in0=rt[:, 2], scalar=-3.0e38, in1=rt[:, 0],
                                                          op0=ALU.mult, op1=ALU.add))
            dve.tensor_tensor(row[8], row[7], row[6], ALU.subtract).then_inc(S["router"], 1)
            dve.wait_ge(S["router"], 2)
            link(dve.tensor_scalar(row[6], row[9], -0.5, 0.5, ALU.mult, ALU.add))
            link(dve.tensor_scalar(row[7], row[9], 0.5, 0.5, ALU.mult, ALU.add))
            link(dve.tensor_tensor(lg[0], lg[2], bc(row[6]), ALU.mult))
            link(dve.tensor_tensor(lg[1], lg[4], bc(row[7]), ALU.mult))
            dve.tensor_tensor(rt[:, 11], rt[:, 0], rt[:, 1], ALU.add).then_inc(S["router"], 1)

            def scale(e, c, j):
                dve.wait_ge(S["y_full"], 2 + 2 * e + c + 1)
                if c == 0:
                    dve.wait_ge(S["in_comb", j], 8 * (e - j) + 16)
                    dve.wait_ge(S["in_b2", j], 8 * (e - j) + 16)
                dve.wait_ge(S["acc"], 2 * e + c + 1)
                dve.scalar_tensor_tensor(out=scaled[:, c], in0=bank[6 + c][:], scalar=b2s[j][:],
                                         in1=comb_bc[j][:, c * HALF:(c + 1) * HALF], op0=ALU.add, op1=ALU.mult)\
                    .then_inc(S["y_scaled"], 1)

            splits(0, 1)
            splits(1, 0)
            scale(0, 0, 0)
            with dve.Fori(0, 3) as i:
                for j in (1, 0):
                    e = 2 * i + (2 - j)
                    splits(e, 1)
                    scale(2 * i + (1 - j), 1, 1 - j)
                    splits(2 * i + (3 - j), 0)
                    scale(e, 0, j)
            scale(6, 1, 0)
            splits(7, 1)
            scale(7, 0, 1)
            scale(7, 1, 1)

            for c in range(2):
                dve.wait_ge(S["acc_turned"], c + 1)
                for t in range(TH):
                    dve.bn_stats(stats[:, 2, c * TH + t], bank[4 + c][:, t * X:(t + 1) * X]).then_inc(S["ln_stats"], 1)
                norm_moments(2, c)
            link(dve.memset(st[0:NT * E1, 1], 1.0))
            for c in range(2):
                dve.wait_ge(S["h2_ready"], c + 1)
                norm_apply(2, c, h_a)

            def self_front(c):
                tiles = slice(c * TH, (c + 1) * TH)
                sc = bank[c][:, 0:TH * L].rearrange("p (t j) -> p t j", t=TH)
                dve.wait_ge(S["self_full"], c + 1)
                link(dve.reduce_max(s_row[:, 0, tiles], sc, AX.X))
                dve.tensor_tensor(s_shift[:, tiles], sc, s_row[:, 0, tiles].unsqueeze(2).broadcast_to([P, TH, L]), ALU.subtract)\
                    .then_inc(S["self_shift"], 1)

            def self_sum(c):
                tiles = slice(c * TH, (c + 1) * TH)
                dve.wait_ge(S["self_probs"], 2 * c + 2)
                link(dve.reduce_sum(s_row[:, 1, tiles], s_prob[:, tiles], AX.X))
                dve.reciprocal(s_row[:, 2, tiles], s_row[:, 1, tiles]).then_inc(S["self_rsum"], 1)

            self_front(0)
            self_front(1)
            self_sum(0)
            self_sum(1)
            for c in range(2):
                dve.wait_ge(S["self_rsum"], c + 1)
                dve.wait_ge(S["self_y"], c + 1)
                for t in range(c * TH, (c + 1) * TH):
                    dve.scalar_tensor_tensor(out=h_b[:, t], in0=bank[4 + c][:, t % TH * P:(t % TH + 1) * P],
                                             scalar=s_row[:, 2, t:t + 1], in1=h_a[:, t], op0=ALU.mult, op1=ALU.add)\
                        .then_inc(S["h3_ready"], 1)
                for t in range(c * TH, (c + 1) * TH):
                    dve.wait_ge(S["h3_ready"], t + 1)
                    norm_stats(3, h_b, t)
                norm_moments(3, c)
            for c in range(2):
                norm_apply(3, c, h_b)

            dve.wait_ge(S["choice_full"], 1)
            cl = bank[2][:, 0:NT * E1].rearrange("p (t e) -> p t e", t=NT)
            link(dve.reduce_max(crow[:, 0], cl, AX.X))
            dve.tensor_tensor(choice[:, 0], cl, bc(crow[:, 0]), ALU.subtract).then_inc(S["choice"], 1)
            dve.wait_ge(S["choice"], 2)
            link(dve.reduce_sum(crow[:, 1], choice[:, 1], AX.X))
            link(dve.reciprocal(crow[:, 2], crow[:, 1]))
            dve.tensor_tensor(choice[:, 2], choice[:, 1], bc(crow[:, 2]), ALU.mult).then_inc(S["choice"], 1)

            R = slice(0, NT * E1)
            dve.wait_ge(S["choice_t"], 1)
            for rnd in range(2):
                src, dst = (0, 2)[rnd], (2, 0)[rnd]
                for b2 in range(2):
                    img = slice(b2 * L, (b2 + 1) * L)
                    if rnd:
                        dve.wait_ge(S["taken"], b2 + 1)
                    dve.max(top8[R, 2 * rnd + b2], st[R, src, img]).then_inc(S["top8"], 1)
                for b2 in range(2):
                    img = slice(b2 * L, (b2 + 1) * L)
                    dve.wait_ge(S["top8"], 2 * rnd + b2 + 1)
                    dve.match_replace(out=st[R, dst, img], in_to_replace=top8[R, 2 * rnd + b2],
                                      in_values=st[R, src, img], imm_value=-1.0).then_inc(S["taken"], 1)
            dve.wait_ge(S["taken"], 4)
            link(dve.tensor_scalar(st[R, 3], st[R, 0], 0.0, None, ALU.is_lt))
            link(dve.tensor_tensor_scan(st[R, 4], st[R, 1], st[R, 3], 0.0, ALU.mult, ALU.add))
            dve.tensor_tensor(st[R, 5], st[R, 4], st[R, 3], ALU.mult).then_inc(S["top"], 1)
            dve.wait_ge(S["slots_turned"], 1)
            sl = bank[2][:, 0:NT * E1].rearrange("p (t e) -> p t e", t=NT)
            for g in range(4):
                tiles = slice(2 * g, 2 * g + 2)
                full = [P, 2 * E1, SLOT]
                dve.tensor_tensor(onehot[:, tiles].rearrange("p t e s -> p (t e) s"),
                                  sl[:, tiles].rearrange("p t e -> p (t e)").unsqueeze(2).broadcast_to(full),
                                  cst[:, SLOTS:SLOTS + SLOT].unsqueeze(1).broadcast_to(full), ALU.is_equal)\
                    .then_inc(S["onehot"], 1)

            def low_gathered(g):
                dve.wait_ge(S["xg_hi"], g + 1)
                dve.tensor_tensor(xg_lo[:, :, 2 * g:2 * g + 2].rearrange("p e t s -> p t e s"),
                                  bank[4 + g][:].rearrange("p (t e s) -> p t e s", t=2, e=E1),
                                  xg_hi[:, :, 2 * g:2 * g + 2].rearrange("p e t s -> p t e s").bitcast(F32), ALU.subtract)\
                    .then_inc(S["xg_lo"], 1)

            def copy_gates(g):
                dve.wait_ge(S["c_turned"], g + 1)
                dve.tensor_copy(c_mat[:, 2 * g:2 * g + 2].rearrange("p t g x -> p (t g x)"), bank[2 + g % 2][:])\
                    .then_inc(S["c_ready"], 1)

            def copy_y(eg):
                dve.wait_ge(S["y_turned"], 2 * eg + 2)
                dve.tensor_copy(y_nat[:, TH:NT, eg], bank[7][:].rearrange("p (t x) -> p t x", t=TH)).then_inc(S["y_ready1"], 1)

            for g in range(4):
                low_gathered(g)
            for g in range(4):
                copy_gates(g)
            for e in range(E1):
                dve.wait_ge(S["e1_y_full"], e + 1)
                dve.tensor_scalar(y_g[:, :, e], bank[4 + e % 2][:, 0:NT * SLOT].rearrange("p (t s) -> p t s", t=NT),
                                  m1[:, e, RAW1 - 1:RAW1], None, ALU.add).then_inc(S["e1_y"], 1)
                if e == 4:
                    copy_y(0)
            copy_y(1)
            for c in range(2):
                tiles = slice(c * TH, (c + 1) * TH)
                dve.wait_ge(S["h4_full"], c + 1)
                dve.tensor_tensor(h_a[:, tiles], bank[2 + c][:].rearrange("p (t x) -> p t x", t=TH), h_b[:, tiles], ALU.add)\
                    .then_inc(S["h4_ready"], 1)


def shape_tables():
    c = np.zeros((P, CONSTS), np.float32)
    c[:, IDENT:IDENT + P] = np.eye(P, dtype=np.float32)
    at = np.arange(L, dtype=np.float32)[:, None]
    div = np.exp(np.arange(0, X, 2, dtype=np.float32) * np.float32(-np.log(10000.0) / X)).astype(np.float32)
    angle = (at * div).astype(np.float32)
    enc = np.stack([np.sin(angle), np.cos(angle)], axis=-1).reshape(L, X)
    c[:, PE_:PE_ + X] = np.concatenate([enc, enc])
    index = np.arange(FREQS)
    frequency = np.pi * (2 / 2500) ** (index // 2 / (FREQS // 2 - 1))
    sins = np.sin(frequency * np.arange(L)[:, None] + np.pi / 2 * (index % 2))
    c[0:FREQS, SINS:SINS + L] = sins.astype(np.float32)[::-1].T
    c[:, REV:REV + E0] = E0 - np.arange(E0)
    c[:, SLOTS:SLOTS + SLOT] = 1 + np.arange(SLOT)
    return c


def kernel(**inputs):
    import concourse.bacc as bacc
    from concourse.bass_utils import run_bass_kernel_spmd

    a = {k: np.asarray(v) for k, v in inputs.items()}

    def rows(v):
        return np.broadcast_to(v[None, :], (P, v.shape[0]))

    def parts(w):
        return w.reshape(-1, P, w.shape[-1]).transpose(1, 0, 2).reshape(P, -1)

    x = a["x"].reshape(B, L // 8, 16, 8, 16).transpose(2, 4, 0, 1, 3)
    x = x.reshape(KT, P, 2, HALF).transpose(1, 2, 0, 3)
    tok = {k[7:]: v for k, v in a.items() if k.startswith("L0_tok_")}
    tok_w = np.stack([parts(tok[k].T) for k in ("W1_w", "W1_sw", "W2_w", "W2_sw")], 1).reshape(P, 4, KT, P)
    tok_eps = np.concatenate(
        [rows(tok["eps_out1"]), rows(tok["eps_out2"]), tok["eps_in1"].reshape(KT, P).T, tok["eps_in2"].reshape(KT, P).T]
        + [tok[k][:, None] for k in ("eps_out1", "eps_out2", "W1_b", "W1_sb", "W2_b", "W2_sb")], 1)
    small = np.concatenate(
        [tok["W3_w"].T, rows(tok["W3_b"]), rows(a["L0_attn_out_b"]), a["L0_attn_q_bias"].reshape(NP, P).T,
         parts(a["L0_attn_out_w"]), rows(a["L0_ffn_bg"]), a["L0_ffn_Wg"], a["L1_ffn_Wg"]], 1)
    moe = []
    for layer in ("L0_ffn_", "L1_ffn_"):
        w1, b1, w2, b2 = (a[layer + k] for k in ("W1", "b1", "W2", "b2"))
        moe.append(np.stack([np.concatenate([w1[e], parts(w2[e]), b1[e].reshape(-1, P).T, b2[e][:, None]], 1)
                             for e in range(w1.shape[0])]))
    arrays = {
        "x_cols": x, "tok_w": tok_w, "tok_eps": tok_eps, "qkv_w": a["L0_attn_qkv"].reshape(X, -1),
        "pos_w": a["L0_attn_positional"].reshape(FREQS, -1), "small": small, "consts": shape_tables(),
        "moe0": moe[0][:, :, :RAW0], "moe0_b1": moe[0][:, :, RAW0:RAW0 + FT], "moe0_b2": moe[0][:, :, RAW0 + FT:],
        "moe1": moe[1].transpose(1, 0, 2),
    }
    nc = bacc.Bacc("TRN2", target_bir_lowering=False, num_devices=1)
    args = []
    for name, v in arrays.items():
        arrays[name] = np.ascontiguousarray(v)
        args.append(nc.dram_tensor(name, v.shape, F32, kind="ExternalInput").ap())
    args.append(nc.dram_tensor("rel_dram", (NREL, P, 1024), F32, kind="Internal").ap())
    args.append(nc.dram_tensor("comb_dram", (NT * E0, P), F32, kind="Internal").ap())
    out = nc.dram_tensor("out", (B, L, X), F32, kind="ExternalOutput").ap()
    tower(nc, *args, out)
    r = run_bass_kernel_spmd(nc, [arrays], core_ids=[0])
    return r.results[0]["out"]
```
